# Optimizing a Trainium2 kernel written in Bass

```python
import numpy as np
import jax
import jax.numpy as jnp

def _softmax(x, axis=-1):
    return jax.nn.softmax(x, axis=axis)

def _gelu(x):
    return jax.nn.gelu(x, approximate=True)

def _silu(x):
    return jax.nn.silu(x)

def _sigmoid(x):
    return jax.nn.sigmoid(x)

def _layernorm(x, axis=-1, eps=1e-05):
    m = jnp.mean(x, axis=axis, keepdims=True)
    v = jnp.var(x, axis=axis, keepdims=True)
    return (x - m) / jnp.sqrt(v + eps)

def _scatter_add(tgt, idx, src, axis=0):
    return tgt.at[idx].add(src)

def _segment_sum(src, seg, n):
    return jax.ops.segment_sum(src, seg, n)
kernel_name = 'mk_decoder_preln_d1_seqx_r8_da6a3f'

def setup_inputs(seed: int=0):
    np.random.seed(seed)
    _w = jnp.asarray

    def _rec_inputs():
        import jax
        import jax.numpy as jnp
        _rk = jax.random.key(seed)
        x = -0.0002928 + 1 * jax.random.normal(jax.random.fold_in(_rk, 1), (32, 128, 128), jnp.float32)
        _lenS = 128 - jax.random.randint(jax.random.fold_in(_rk, 7), (32,), 0, max(1, 128 // 4) + 1, jnp.int32)
        _lenS2 = 128 - jax.random.randint(jax.random.fold_in(_rk, 8), (32,), 0, max(1, 128 // 4) + 1, jnp.int32)
        _ctx_1024P = jax.random.normal(jax.random.fold_in(_rk, 11), (32, 16, 128), jnp.float32)
        _ctx_1024c = jax.random.dirichlet(jax.random.fold_in(_rk, 511), 0.3 * jnp.ones((16,), jnp.float32), (32, 128))
        _ctx_1024t = jnp.einsum('bsk,bkd->bsd', _ctx_1024c, _ctx_1024P)
        _ctx_1024t = _ctx_1024t * jax.lax.rsqrt(jnp.mean(jnp.square(_ctx_1024t)) + 1e-12) * 0.953939
        ctx_1024 = -1.39393e-06 + 0.999914 * (_ctx_1024t + 0.3 * jax.random.normal(jax.random.fold_in(_rk, 611), (32, 128, 128), jnp.float32))
        return (x, ctx_1024)
    x, ctx_1024 = _rec_inputs()

    def _L0_attn_setup():
        import jax, jax.numpy as jnp
        import numpy as np
        import math
        D_MODEL = 128
        NUM_HEADS = 16
        key = jax.random.key(seed)
        k1, k2, k3 = jax.random.split(key, 3)
        B, S = (2, 256)
        x = jax.random.normal(k1, (B, S, D_MODEL), dtype=jnp.float32)
        W_kqv = jax.random.normal(k2, (D_MODEL, 3 * D_MODEL), dtype=jnp.float32) * (1.0 / math.sqrt(D_MODEL))
        m = jax.random.normal(k3, (NUM_HEADS, 1, 1), dtype=jnp.float32)
        return {'x': x, 'W_kqv': W_kqv, 'm': m}
    _L0_attn_all = _L0_attn_setup()
    _L0_attn_in = {k: v for k, v in _L0_attn_all.items() if k in ('W_kqv', 'm')}
    del _L0_attn_all

    def _L0_xattn_setup():
        import jax, jax.numpy as jnp
        import numpy as np
        D_MODEL = 128
        NUM_HEADS = 16

        def _split_heads(x, n_heads):
            B, L, D = x.shape
            return x.reshape(B, L, n_heads, D // n_heads).transpose(0, 2, 1, 3)
        key = jax.random.key(seed)
        ks = jax.random.split(key, 11)
        B, L, D = (1, 512, D_MODEL)
        s = 1.0 / np.sqrt(D)
        inp = {'Q': jax.random.normal(ks[0], (B, L, D), jnp.float32), 'K': jax.random.normal(ks[1], (B, L, D), jnp.float32), 'V': jax.random.normal(ks[2], (B, L, D), jnp.float32), 'w_q': jax.random.normal(ks[3], (D, D), jnp.float32) * s, 'b_q': jax.random.normal(ks[4], (D,), jnp.float32) * s, 'w_k': jax.random.normal(ks[5], (D, D), jnp.float32) * s, 'b_k': jax.random.normal(ks[6], (D,), jnp.float32) * s, 'w_v': jax.random.normal(ks[7], (D, D), jnp.float32) * s, 'b_v': jax.random.normal(ks[8], (D,), jnp.float32) * s, 'w_o': jax.random.normal(ks[9], (D, D), jnp.float32) * s, 'b_o': jax.random.normal(ks[10], (D,), jnp.float32) * s}
        return inp
    _L0_xattn_all = _L0_xattn_setup()
    _L0_xattn_in = {k: v for k, v in _L0_xattn_all.items() if k in ('w_q', 'b_q', 'w_k', 'b_k', 'w_v', 'b_v', 'w_o', 'b_o')}
    del _L0_xattn_all

    def _L0_ffn_setup():
        import jax, jax.numpy as jnp
        import numpy as np
        DIM = 128
        DEPTH = 6
        HEADS = 16
        DIM_HEAD = 64
        WINDOW = 32
        INNER = HEADS * DIM_HEAD
        DIM_INNER = int(DIM * 4 * 2 / 3)
        QK_SCALE = 8.0

        def shift_tokens(t):
            a, s = jnp.split(t, 2, -1)
            s = jnp.pad(s, ((0, 0), (1, 0), (0, 0)))[:, :-1]
            return jnp.concatenate([a, s], -1)

        def l2norm(t):
            return t / jnp.maximum(jnp.linalg.norm(t, axis=-1, keepdims=True), 1e-12)

        def rotate_half(x):
            x1, x2 = jnp.split(x, 2, -1)
            return jnp.concatenate([-x2, x1], -1)

        def rotary_tables(n):
            half = jnp.arange(0, DIM_HEAD, 2, dtype=jnp.float32)
            inv_freq = 1.0 / 10000.0 ** (half / DIM_HEAD)
            t = jnp.arange(n, dtype=jnp.float32)
            freqs = t[:, None] * inv_freq[None, :]
            freqs = jnp.concatenate([freqs, freqs], -1)
            base_scale = (half + 0.4 * DIM_HEAD) / (1.4 * DIM_HEAD)
            power = (t - n // 2) / (WINDOW // 2)
            scale = base_scale[None, :] ** power[:, None]
            scale = jnp.concatenate([scale, scale], -1)
            return (freqs, scale)

        def local_attention(q, k, v):
            b, h, n, d = q.shape
            w = WINDOW
            nw = n // w
            bq = q.reshape(b, h, nw, w, d)
            bk = k.reshape(b, h, nw, w, d)
            bv = v.reshape(b, h, nw, w, d)

            def look(t):
                p = jnp.pad(t, ((0, 0), (0, 0), (1, 0), (0, 0), (0, 0)))
                return jnp.concatenate([p[:, :, :nw], p[:, :, 1:]], axis=3)
            bk2, bv2 = (look(bk), look(bv))
            seq = jnp.arange(n).reshape(nw, w)
            seq_p = jnp.pad(seq, ((1, 0), (0, 0)), constant_values=-1)
            jt = jnp.concatenate([seq_p[:nw], seq_p[1:]], axis=1)
            it = seq[:, :, None]
            jb = jt[:, None, :]
            mask = (it < jb) | (it > jb + w) | (jb == -1)
            sim = jnp.einsum('bhwie,bhwje->bhwij', bq, bk2) * QK_SCALE
            sim = jnp.where(mask, -jnp.finfo(sim.dtype).max, sim)
            attn = jax.nn.softmax(sim, -1)
            out = jnp.einsum('bhwij,bhwje->bhwie', attn, bv2)
            return out.reshape(b, h, n, d)

        def attn_layer(x, Wqkv, qs, ksc, Wo):
            b, n, _ = x.shape
            qkv = x @ Wqkv
            q, k, v = jnp.split(qkv, 3, -1)
            sh = lambda t: t.reshape(b, n, HEADS, DIM_HEAD).transpose(0, 2, 1, 3)
            q, k, v = (sh(q), sh(k), sh(v))
            q = l2norm(q) * qs
            k = l2norm(k) * ksc
            freqs, scale = rotary_tables(n)
            cos, sin = (jnp.cos(freqs), jnp.sin(freqs))
            q = q * cos * scale + rotate_half(q) * sin * scale
            inv = 1.0 / scale
            k = k * cos * inv + rotate_half(k) * sin * inv
            out = local_attention(q, k, v)
            out = out.transpose(0, 2, 1, 3).reshape(b, n, INNER)
            return out @ Wo

        def ffn_layer(x, g, bln, W1, b1, W2, b2):
            mu = x.mean(-1, keepdims=True)
            var = ((x - mu) ** 2).mean(-1, keepdims=True)
            xn = (x - mu) / jnp.sqrt(var + 1e-05) * g + bln
            hg = xn @ W1 + b1
            a, gate = jnp.split(hg, 2, -1)
            return a * jax.nn.gelu(gate, approximate=False) @ W2 + b2
        key = jax.random.key(seed)
        ks = jax.random.split(key, 8)
        B, N = (2, 256)
        init = lambda k, shape: jax.random.normal(k, shape, jnp.float32) * 0.02
        return {'x': jax.random.normal(ks[0], (B, N, DIM), jnp.float32), 'Wqkv': init(ks[1], (DEPTH, DIM, 3 * INNER)), 'q_scale': jnp.ones((DEPTH, DIM_HEAD), jnp.float32), 'k_scale': jnp.ones((DEPTH, DIM_HEAD), jnp.float32), 'Wo': init(ks[2], (DEPTH, INNER, DIM)), 'ln_g': jnp.ones((DEPTH, DIM), jnp.float32), 'ln_b': jnp.zeros((DEPTH, DIM), jnp.float32), 'W1': init(ks[3], (DEPTH, DIM, 2 * DIM_INNER)), 'b1': jnp.zeros((DEPTH, 2 * DIM_INNER), jnp.float32), 'W2': init(ks[4], (DEPTH, DIM_INNER, DIM)), 'b2': jnp.zeros((DEPTH, DIM), jnp.float32)}
    _L0_ffn_all = _L0_ffn_setup()
    _L0_ffn_in = {k: v for k, v in _L0_ffn_all.items() if k in ('Wqkv', 'q_scale', 'k_scale', 'Wo', 'ln_g', 'ln_b', 'W1', 'b1', 'W2', 'b2')}
    del _L0_ffn_all
    return {'x': x, 'ctx_1024': ctx_1024, 'L0_attn_W_kqv': _L0_attn_in['W_kqv'], 'L0_attn_m': _L0_attn_in['m'], 'L0_xattn_w_q': _L0_xattn_in['w_q'], 'L0_xattn_b_q': _L0_xattn_in['b_q'], 'L0_xattn_w_k': _L0_xattn_in['w_k'], 'L0_xattn_b_k': _L0_xattn_in['b_k'], 'L0_xattn_w_v': _L0_xattn_in['w_v'], 'L0_xattn_b_v': _L0_xattn_in['b_v'], 'L0_xattn_w_o': _L0_xattn_in['w_o'], 'L0_xattn_b_o': _L0_xattn_in['b_o'], 'L0_ffn_Wqkv': _L0_ffn_in['Wqkv'], 'L0_ffn_q_scale': _L0_ffn_in['q_scale'], 'L0_ffn_k_scale': _L0_ffn_in['k_scale'], 'L0_ffn_Wo': _L0_ffn_in['Wo'], 'L0_ffn_ln_g': _L0_ffn_in['ln_g'], 'L0_ffn_ln_b': _L0_ffn_in['ln_b'], 'L0_ffn_W1': _L0_ffn_in['W1'], 'L0_ffn_b1': _L0_ffn_in['b1'], 'L0_ffn_W2': _L0_ffn_in['W2'], 'L0_ffn_b2': _L0_ffn_in['b2']}

def reference(x, ctx_1024, L0_attn_W_kqv, L0_attn_m, L0_xattn_w_q, L0_xattn_b_q, L0_xattn_w_k, L0_xattn_b_k, L0_xattn_w_v, L0_xattn_b_v, L0_xattn_w_o, L0_xattn_b_o, L0_ffn_Wqkv, L0_ffn_q_scale, L0_ffn_k_scale, L0_ffn_Wo, L0_ffn_ln_g, L0_ffn_ln_b, L0_ffn_W1, L0_ffn_b1, L0_ffn_W2, L0_ffn_b2):
    import jax
    import jax.numpy as jnp

    def _L0_attn_ref(x, W_kqv, m):
        import jax, jax.numpy as jnp
        import numpy as np
        import math
        D_MODEL = 128
        NUM_HEADS = 16
        B, S, D = x.shape
        H = NUM_HEADS
        hd = D // H
        scale = math.sqrt(D)
        kqv = x @ W_kqv
        k, q, v = jnp.split(kqv, 3, axis=-1)
        q = q.reshape(B, S, H, hd)
        k = k.reshape(B, S, H, hd)
        v = v.reshape(B, S, H, hd)
        rel = (jnp.arange(S)[None, :] - jnp.arange(S)[:, None]).astype(x.dtype)
        bias = m[None, :, :, :] * rel[None, None, :, :]
        score = jnp.einsum('bqhd,bkhd->bhqk', q, k) / scale + bias
        causal = jnp.tril(jnp.ones((S, S), dtype=bool))
        score = jnp.where(causal[None, None, :, :], score, -jnp.inf)
        attn = jax.nn.softmax(score, axis=-1)
        out = jnp.einsum('bhqk,bkhd->bqhd', attn, v).reshape(B, S, D)
        return out

    def _L0_xattn_ref(Q, K, V, w_q, b_q, w_k, b_k, w_v, b_v, w_o, b_o):
        import jax, jax.numpy as jnp
        import numpy as np
        D_MODEL = 128
        NUM_HEADS = 16

        def _split_heads(x, n_heads):
            B, L, D = x.shape
            return x.reshape(B, L, n_heads, D // n_heads).transpose(0, 2, 1, 3)
        H = NUM_HEADS
        q = _split_heads(Q @ w_q.T + b_q, H)
        k = _split_heads(K @ w_k.T + b_k, H)
        v = _split_heads(V @ w_v.T + b_v, H)
        d_h = q.shape[-1]
        scores = jnp.einsum('bhqd,bhkd->bhqk', q, k) / jnp.sqrt(jnp.float32(d_h))
        attn = jax.nn.softmax(scores, axis=-1)
        out = jnp.einsum('bhqk,bhkd->bhqd', attn, v)
        B, _, L, _ = out.shape
        out = out.transpose(0, 2, 1, 3).reshape(B, L, H * d_h)
        return out @ w_o.T + b_o

    def _L0_ffn_ref(x, Wqkv, q_scale, k_scale, Wo, ln_g, ln_b, W1, b1, W2, b2):
        import jax, jax.numpy as jnp
        import numpy as np
        DIM = 128
        DEPTH = 6
        HEADS = 16
        DIM_HEAD = 64
        WINDOW = 32
        INNER = HEADS * DIM_HEAD
        DIM_INNER = int(DIM * 4 * 2 / 3)
        QK_SCALE = 8.0

        def shift_tokens(t):
            a, s = jnp.split(t, 2, -1)
            s = jnp.pad(s, ((0, 0), (1, 0), (0, 0)))[:, :-1]
            return jnp.concatenate([a, s], -1)

        def l2norm(t):
            return t / jnp.maximum(jnp.linalg.norm(t, axis=-1, keepdims=True), 1e-12)

        def rotate_half(x):
            x1, x2 = jnp.split(x, 2, -1)
            return jnp.concatenate([-x2, x1], -1)

        def rotary_tables(n):
            half = jnp.arange(0, DIM_HEAD, 2, dtype=jnp.float32)
            inv_freq = 1.0 / 10000.0 ** (half / DIM_HEAD)
            t = jnp.arange(n, dtype=jnp.float32)
            freqs = t[:, None] * inv_freq[None, :]
            freqs = jnp.concatenate([freqs, freqs], -1)
            base_scale = (half + 0.4 * DIM_HEAD) / (1.4 * DIM_HEAD)
            power = (t - n // 2) / (WINDOW // 2)
            scale = base_scale[None, :] ** power[:, None]
            scale = jnp.concatenate([scale, scale], -1)
            return (freqs, scale)

        def local_attention(q, k, v):
            b, h, n, d = q.shape
            w = WINDOW
            nw = n // w
            bq = q.reshape(b, h, nw, w, d)
            bk = k.reshape(b, h, nw, w, d)
            bv = v.reshape(b, h, nw, w, d)

            def look(t):
                p = jnp.pad(t, ((0, 0), (0, 0), (1, 0), (0, 0), (0, 0)))
                return jnp.concatenate([p[:, :, :nw], p[:, :, 1:]], axis=3)
            bk2, bv2 = (look(bk), look(bv))
            seq = jnp.arange(n).reshape(nw, w)
            seq_p = jnp.pad(seq, ((1, 0), (0, 0)), constant_values=-1)
            jt = jnp.concatenate([seq_p[:nw], seq_p[1:]], axis=1)
            it = seq[:, :, None]
            jb = jt[:, None, :]
            mask = (it < jb) | (it > jb + w) | (jb == -1)
            sim = jnp.einsum('bhwie,bhwje->bhwij', bq, bk2) * QK_SCALE
            sim = jnp.where(mask, -jnp.finfo(sim.dtype).max, sim)
            attn = jax.nn.softmax(sim, -1)
            out = jnp.einsum('bhwij,bhwje->bhwie', attn, bv2)
            return out.reshape(b, h, n, d)

        def attn_layer(x, Wqkv, qs, ksc, Wo):
            b, n, _ = x.shape
            qkv = x @ Wqkv
            q, k, v = jnp.split(qkv, 3, -1)
            sh = lambda t: t.reshape(b, n, HEADS, DIM_HEAD).transpose(0, 2, 1, 3)
            q, k, v = (sh(q), sh(k), sh(v))
            q = l2norm(q) * qs
            k = l2norm(k) * ksc
            freqs, scale = rotary_tables(n)
            cos, sin = (jnp.cos(freqs), jnp.sin(freqs))
            q = q * cos * scale + rotate_half(q) * sin * scale
            inv = 1.0 / scale
            k = k * cos * inv + rotate_half(k) * sin * inv
            out = local_attention(q, k, v)
            out = out.transpose(0, 2, 1, 3).reshape(b, n, INNER)
            return out @ Wo

        def ffn_layer(x, g, bln, W1, b1, W2, b2):
            mu = x.mean(-1, keepdims=True)
            var = ((x - mu) ** 2).mean(-1, keepdims=True)
            xn = (x - mu) / jnp.sqrt(var + 1e-05) * g + bln
            hg = xn @ W1 + b1
            a, gate = jnp.split(hg, 2, -1)
            return a * jax.nn.gelu(gate, approximate=False) @ W2 + b2
        for i in range(DEPTH):
            x = attn_layer(shift_tokens(x), Wqkv[i], q_scale[i], k_scale[i], Wo[i]) + x
            x = ffn_layer(shift_tokens(x), ln_g[i], ln_b[i], W1[i], b1[i], W2[i], b2[i]) + x
        return x
    x = x + _L0_attn_ref(_layernorm(x, axis=-1), L0_attn_W_kqv, L0_attn_m)
    x = x + _L0_xattn_ref(_layernorm(x, axis=-1), ctx_1024, ctx_1024, L0_xattn_w_q, L0_xattn_b_q, L0_xattn_w_k, L0_xattn_b_k, L0_xattn_w_v, L0_xattn_b_v, L0_xattn_w_o, L0_xattn_b_o)
    x = x + _L0_ffn_ref(_layernorm(x, axis=-1), L0_ffn_Wqkv, L0_ffn_q_scale, L0_ffn_k_scale, L0_ffn_Wo, L0_ffn_ln_g, L0_ffn_ln_b, L0_ffn_W1, L0_ffn_b1, L0_ffn_W2, L0_ffn_b2)
    return x

_drawn_inputs = setup_inputs


def setup_inputs(seed=0):
    import zlib

    import numpy as np

    out = dict(_drawn_inputs(seed))
    spreads = {'L0_ffn_q_scale': (1.0, 0.6),
     'L0_ffn_k_scale': (1.0, 0.6),
     'L0_ffn_ln_g': (1.0, 0.6),
     'L0_ffn_ln_b': (0.0, 0.8),
     'L0_ffn_b1': (0.0, 0.8),
     'L0_ffn_b2': (0.0, 0.1)}
    factors = {'L0_xattn_b_q': 3.469, 'L0_xattn_b_k': 8.0, 'L0_ffn_W1': 4.202, 'L0_ffn_W2': 4.11}
    for name, (base, spread) in spreads.items():
        noise = np.random.default_rng([zlib.crc32(name.encode()), seed]).standard_normal(out[name].shape)
        drawn = base * np.exp(spread * noise) if base else spread * noise
        out[name] = jnp.asarray(drawn.astype(out[name].dtype))
    for name, factor in factors.items():
        out[name] = (out[name] * factor).astype(out[name].dtype)
    return out
```

```python
from contextlib import ExitStack

import numpy as np

import concourse.bass as bass
from concourse import mybir

F32 = mybir.dt.float32
BF16 = mybir.dt.bfloat16
ALU = mybir.AluOpType
ACT = mybir.ActivationFunctionType
AX_X = mybir.AxisListType.X

P = 128
NB = 32
NH = 16
HG = 4
NG = NH // HG
GROUPS = NB * NG
DEPTH = 6
DH = 64
HALF = DH // 2
INNER = NH * DH
DS = P // NH
PAD = 32
WINDOW = 32
HID = 341
HB = [(0, 128), (128, 128), (256, 85)]
QUAD = 4
NQ = NB // QUAD
EPS = 1e-5
MASKED = -1e30
A, B, C = 0, 1, 2

STEPS = 2 * NG


class LAG:
    heads = 2
    scores = 3
    exp = 4
    turn = 5
    value = 6
    out = 7


DRAIN = 7

COLS = {}
_at = 0
for _name, _n in (("ident", P), ("shift", P), ("iota", P), ("qrow", P), ("block", HG), ("cos", 2 * DH),
                  ("sin", 2 * DH), ("causal", P), ("band", P), ("sel", HG * P)):
    COLS[_name] = (_at, _n)
    _at += _n
NCONST = _at


def constants():
    t = np.zeros((P, NCONST), np.float32)

    def put(name, v):
        a, n = COLS[name]
        t[:v.shape[0], a:a + n] = v.reshape(v.shape[0], n)

    i = np.arange(P)
    put("ident", np.eye(P, dtype=np.float32))
    put("shift", np.eye(P, k=1, dtype=np.float32))
    put("iota", np.tile(i.astype(np.float32), (P, 1)))
    qrow = np.zeros((P, P), np.float32)
    qrow[DS::PAD] = 1.0
    qrow[DS + 1::PAD] = i
    put("qrow", qrow)
    put("block", (i[:, None] // PAD == np.arange(HG)[None]).astype(np.float32))
    half = np.arange(0, DH, 2, dtype=np.float32)
    inv_freq = (np.float32(1.0) / np.float32(10000.0) ** (half / np.float32(DH))).astype(np.float32)
    pos = i.astype(np.float32)
    freqs = pos[:, None] * inv_freq[None]
    base = (half + np.float32(0.4 * DH)) / np.float32(1.4 * DH)
    power = (pos - P // 2) / np.float32(WINDOW // 2)
    scale = (base[None] ** power[:, None]).astype(np.float32)
    cos, sin = np.cos(freqs), np.sin(freqs)
    both = lambda q, k: np.stack([8.0 * q, k], 1)
    inv = np.float32(1.0) / scale
    put("cos", both(np.concatenate([cos * scale] * 2, -1), np.concatenate([cos * inv] * 2, -1)))
    put("sin", both(np.concatenate([-sin * scale, sin * scale], -1), np.concatenate([-sin * inv, sin * inv], -1)))
    ahead = i[:, None] - i[None]
    put("causal", np.where(ahead >= 0, 0.0, MASKED))
    put("band", np.where((ahead >= 0) & (ahead <= WINDOW), 0.0, MASKED))
    sel = np.zeros((2 * HG, HG, P), np.float32)
    for h in range(HG):
        sel[h, h] = sel[HG + h, h] = 1.0
    put("sel", sel)
    return t


def has(index):
    return not isinstance(index, int) or index >= 0


def in_range(it, j, lag, n):
    return not isinstance(it, int) or 0 <= it * n[1] + j - lag < n[0]


def build(nc, x_in, ctx_in, a_w, a_m, b_wq, b_bq, b_wk, b_bk, b_wv, b_bv, b_wo, b_bo, wqkv, q_scale, k_scale,
          wo, ln_g, ln_b, w1, b1, w2, b2, const_d, out):
    with ExitStack() as stack:
        def sb(name, shape, dt=F32):
            return stack.enter_context(nc.sbuf_tensor(name, shape, dt))

        def ring(name, n, shape, dt=F32):
            return [sb(f"{name}{i}", shape, dt) for i in range(n)]

        x = sb("x", [P, NB * P])
        y = sb("y", [P, NB * P])
        ctx_all = sb("ctx_all", [P, NB * P])
        cst = sb("cst", [P, NCONST])
        ident = cst[:, 0:P]
        ident_b = sb("ident_b", [P, P], BF16)
        masks_b = sb("masks_b", [P, 2, P], BF16)
        sel_b = sb("sel_b", [2 * HG, HG * P], BF16)
        neg_half = sb("neg_half", [P, 2 * HG])
        stage = sb("stage", [P, 4 * P])
        aw = sb("aw", [P, 3 * P])
        bw = sb("bw", [P, 3 * P])
        wpad = sb("wpad", [P, 2, 2, NG, HG, PAD])
        bwo = sb("bwo", [PAD, NG, P])
        m_at = sb("m_at", [P, 2 * NG])
        krow = sb("krow", [P, NG, P])
        b_qk = sb("b_qk", [P, 2, NG])
        b_v = sb("b_v", [P, P])
        b_o = sb("b_o", [P, P])
        wqkv_sb = sb("wqkv_sb", [P, 3 * INNER])
        wo_sb = sb("wo_sb", [P, INNER])
        w1_sb = sb("w1_sb", [P, 2 * HID])
        w2_sb = sb("w2_sb", [P, 3 * P])
        qk_scale = sb("qk_scale", [P, DEPTH, 2, DH])
        rot_cos = sb("rot_cos", [P, DEPTH * 2 * DH])
        rot_sin = sb("rot_sin", [P, DEPTH * 2 * DH])
        per_layer = sb("per_layer", [P, DEPTH, 8])
        mlp_now = sb("mlp_now", [P, 8])
        b2_sb = sb("b2_sb", [P, DEPTH * P])
        tok = ring("tok", 2, [P, P])
        xt = ring("xt", 2, [P, P])
        ct = ring("ct", 2, [P, P])
        ctok = ring("ctok", 2, [P, P])
        squares = sb("squares", [P, 2 * HG, DH])
        norm2 = ring("norm2", 2, [P, 2 * HG])
        norm2g = ring("norm2g", 2, [P, 2 * HG])
        rnorm = ring("rnorm", 2, [P, 2 * HG])
        by_cos = ring("by_cos", 2, [P, 2, HG, DH])
        by_sin = ring("by_sin", 2, [P, 2, HG, DH])
        rotated = ring("rotated", 2, [P, 2, HG, DH])
        unit = ring("unit", 2, [P, 2, HG, DH])
        qt = ring("qt", 2, [P, 2 * P])
        kt = ring("kt", 2, [P, P])
        kz = ring("kz", 2, [P, HG, P])
        val = ring("val", 2 * NG, [P, HG, DH + 1])
        top = ring("top", 2, [P, HG])
        top_b = ring("top_b", 2, [P, 2 * HG], BF16)
        top_t = ring("top_t", 2, [2 * HG, P], BF16)
        prob = ring("prob", 2, [P, HG, P])
        prob_t = ring("prob_t", 2, [P, HG, P])
        rsum = ring("rsum", 2, [P, HG])
        head_out = ring("head_out", 2, [P, HG, DH])
        head_t = ring("head_t", 2, [P, 2 * P])
        stats = ring("stats", 2, [P, QUAD, 6])
        mv = ring("mv", 2, [P, QUAD, 2])
        scratch = sb("scratch", [P, 1])
        var = ring("var", 2, [P, QUAD])
        rstd = ring("rstd", 2, [P, QUAD])
        shifted = ring("shifted", 2, [P, QUAD, P])
        normed = ring("normed", 2, [P, QUAD, P])
        normed_t = ring("normed_t", 2, [P, QUAD * P])
        gate = ring("gate", 6, [P, QUAD * P])
        hidden = ring("hidden", 6, [P, QUAD * P])

        bank = [stack.enter_context(nc.psum_tensor(f"bank{i}", [P, 512], F32)) for i in range(8)]
        proj_ps = bank[0:2]
        misc_ps = bank[2]
        misc_bf = misc_ps[:, :].bitcast(BF16)
        heads_ps = bank[3]
        score_ps = bank[4:6]
        turn_ps = bank[6]
        value_ps = bank[7]
        hid_ps = [bank[0], bank[1], bank[4], bank[5]]

        def sem(name):
            return stack.enter_context(nc.semaphore(name))

        s_const_in = sem("const_in")
        s_x_in = sem("x_in")
        s_ctx_in = sem("ctx_in")
        s_small_in = sem("small_in")
        s_table_in = sem("table_in")
        s_wqkv_in = sem("wqkv_in")
        s_wo_in = sem("wo_in")
        s_w1_in = sem("w1_in")
        s_w2_in = sem("w2_in")
        s_out_done = sem("out_done")
        s_zeros_set = sem("zeros_set")
        s_cast_done = sem("cast_done")
        s_wpad_set = sem("wpad_set")
        s_krow_set = sem("krow_set")
        s_krow_neg = sem("krow_neg")
        s_tables_set = sem("tables_set")
        s_vone_set = sem("vone_set")
        s_half_set = sem("half_set")
        s_kz_zero = sem("kz_zero")
        s_xt_zero = sem("xt_zero")
        s_ln_stat = sem("ln_stat")
        s_ln_mv = sem("ln_mv")
        s_ln_var = sem("ln_var")
        s_ln_rstd = sem("ln_rstd")
        s_tok_ready = sem("tok_ready")
        s_xturn = sem("xturn")
        s_xt_ready = sem("xt_ready")
        s_cturn = sem("cturn")
        s_ct_ready = sem("ct_ready")
        s_ctok_ready = sem("ctok_ready")
        s_proj = sem("proj")
        s_sq_done = sem("sq_done")
        s_nrm2 = sem("nrm2")
        s_nrm2g = sem("nrm2g")
        s_rn_done = sem("rn_done")
        s_cos_done = sem("cos_done")
        s_sin_done = sem("sin_done")
        s_rot_done = sem("rot_done")
        s_unit_done = sem("unit_done")
        s_heads = sem("heads")
        s_q_ready = sem("q_ready")
        s_k_half = sem("k_half")
        s_k_ready = sem("k_ready")
        s_kz_ready = sem("kz_ready")
        s_v_proj = sem("v_proj")
        s_v_ready = sem("v_ready")
        s_scores = sem("scores")
        s_top_done = sem("top_done")
        s_top_hi = sem("top_hi")
        s_top_lo = sem("top_lo")
        s_top_turn = sem("top_turn")
        s_top_ready = sem("top_ready")
        s_shifted_scores = sem("shifted_scores")
        s_exp_done = sem("exp_done")
        s_pturn = sem("pturn")
        s_pt_ready = sem("pt_ready")
        s_pv = sem("pv")
        s_rsum_done = sem("rsum_done")
        s_out_ready = sem("out_ready")
        s_oturn = sem("oturn")
        s_ot_ready = sem("ot_ready")
        s_wo_done = sem("wo_done")
        s_added = sem("added")
        s_bias_added = sem("bias_added")
        s_f_shift = sem("f_shift")
        s_f_left = sem("f_left")
        s_f_right = sem("f_right")
        s_f_stat = sem("f_stat")
        s_f_mv = sem("f_mv")
        s_f_var = sem("f_var")
        s_f_rstd = sem("f_rstd")
        s_f_norm = sem("f_norm")
        s_f_b2 = sem("f_b2")
        s_f_turn = sem("f_turn")
        s_f_xt = sem("f_xt")
        s_f_gate_ps = sem("f_gate_ps")
        s_f_a_ps = sem("f_a_ps")
        s_f_gate = sem("f_gate")
        s_f_hid = sem("f_hid")
        s_f_w2 = sem("f_w2")
        s_y_done = sem("y_done")
        s_layer_set = sem("layer_set")
        s_y_stat = sem("y_stat")
        s_y_mv = sem("y_mv")
        s_y_var = sem("y_var")
        s_y_rstd = sem("y_rstd")
        s_sum_done = sem("sum_done")

        def const(name, rows=P):
            a, n = COLS[name]
            return cst[0:rows, a:a + n]

        def seq(t, b, n=1):
            return t[:, bass.ds(b * P, n * P)]

        def start_of(phase, layer):
            return phase * GROUPS + layer * GROUPS

        def attention(eng, step, phase, layer=0):
            bodies = GROUPS // STEPS
            for j in range(STEPS):
                step(phase, layer, 0, j)
            with eng.Fori(1, bodies - 1) as it:
                for j in range(STEPS):
                    step(phase, layer, it, j)
            for j in range(STEPS):
                step(phase, layer, bodies - 1, j)
            for j in range(DRAIN):
                step(phase, layer, bodies, j)

        def mlp(eng, step, layer):
            for it in (0, 1):
                for j in range(2):
                    step(layer, it, j)
            with eng.Fori(2, NQ // 2) as it:
                for j in range(2):
                    step(layer, it, j)
            for j in range(3):
                step(layer, NQ // 2 + j // 2, j % 2)

        def here(it, j, lag):
            return in_range(it, j, lag, (GROUPS, STEPS))

        def here_q(it, j, lag):
            return in_range(it, j, lag, (NQ, 2))

        def issued(it, j, lag, after):
            if not isinstance(it, int):
                return it * STEPS + j - lag + after
            return max(0, min(GROUPS, it * STEPS + j - lag + after))

        def turned(it, j, after):
            done = 1 + j // NG + (1 if j % NG > 2 or (j % NG == 2 and after) else 0)
            if not isinstance(it, int):
                return it * 2 + done
            return min(NB, it * 2 + done)

        block = stack.enter_context(nc.Block())

        @block.sync
        def _(sp):
            sp.dma_start(cst[:, :], const_d).then_inc(s_const_in, 16)
            sp.dma_start(x[:, :].rearrange("t (b c) -> t b c", c=P), x_in.rearrange("b t c -> t b c")).then_inc(s_x_in, 16)
            sp.dma_start(aw[:, :], a_w).then_inc(s_small_in, 16)
            sp.dma_start(bw[:, 0:P], b_wq).then_inc(s_small_in, 16)
            sp.dma_start(bw[:, P:2 * P], b_wk).then_inc(s_small_in, 16)
            sp.dma_start(bw[:, 2 * P:3 * P], b_wv).then_inc(s_small_in, 16)
            sp.dma_start(bwo[:, :, :], b_wo.rearrange("(g r) c -> r g c", r=PAD)).then_inc(s_small_in, 16)
            sp.dma_start(b_v[:, :], b_bv.partition_broadcast(P)).then_inc(s_small_in, 16)
            sp.dma_start(b_o[:, :], b_bo.partition_broadcast(P)).then_inc(s_small_in, 16)
            sp.wait_ge(s_zeros_set, 3)
            with nc.allow_non_contiguous_dma("small loads"):
                for r in range(2):
                    sp.dma_start(m_at[DS + r::PAD, r * NG:(r + 1) * NG],
                                 a_m.rearrange("(g h) a b -> h (g a b)", h=HG)).then_inc(s_small_in, 16)
                for i, v in enumerate((b_bq, b_bk)):
                    for h in range(HG):
                        sp.dma_start(b_qk[PAD * h:PAD * h + DS, i, :],
                                     v.rearrange("(g h d) -> h d g", h=HG, d=DS)[h]).then_inc(s_small_in, 16)
                sp.dma_start(ctx_all[:, :].rearrange("t (b c) -> t b c", c=P), ctx_in.rearrange("b t c -> t b c")).then_inc(s_ctx_in, 16)
                for i, v in enumerate((q_scale, k_scale)):
                    sp.dma_start(qk_scale[:, :, i, :], v.partition_broadcast(P)).then_inc(s_table_in, 16)
                sp.dma_start(per_layer[:, :, 0], ln_g.rearrange("l c -> c l")).then_inc(s_table_in, 16)
                sp.dma_start(per_layer[:, :, 1], ln_b.rearrange("l c -> c l")).then_inc(s_table_in, 16)
                sp.dma_start(b2_sb[:, :].rearrange("p (l c) -> p l c", c=P), b2.partition_broadcast(P)).then_inc(s_table_in, 16)
                for i in range(2):
                    for k, (a, n) in enumerate(HB):
                        sp.dma_start(per_layer[0:n, :, 2 + 3 * i + k],
                                     b1[:, i * HID + a:i * HID + a + n].rearrange("l p -> p l")).then_inc(s_table_in, 16)
            for l in range(DEPTH):
                if l:
                    sp.wait_ge(s_v_proj, start_of(C, l))
                sp.dma_start(wqkv_sb[:, :], wqkv[l]).then_inc(s_wqkv_in, 16)
                if l:
                    sp.wait_ge(s_wo_done, start_of(C, l) - GROUPS)
                sp.dma_start(wo_sb[:, :].rearrange("p (k c) -> p k c", c=P), wo[l].rearrange("(k p) c -> p k c", p=P)).then_inc(s_wo_in, 16)
                if l:
                    sp.wait_ge(s_f_a_ps, 3 * NQ * l)
                    sp.wait_ge(s_f_w2, NQ * l)
                sp.dma_start(w1_sb[:, :], w1[l]).then_inc(s_w1_in, 16)
                for k, (a, n) in enumerate(HB):
                    sp.dma_start(w2_sb[0:n, k * P:(k + 1) * P], w2[l, a:a + n]).then_inc(s_w2_in, 16)
            for q in range(NQ):
                sp.wait_ge(s_sum_done, q + 1)
                sp.dma_start(out[q * QUAD:(q + 1) * QUAD].rearrange("b t c -> t b c"),
                             y[:, q * QUAD * P:(q + 1) * QUAD * P].rearrange("t (b c) -> t b c", c=P)).then_inc(s_out_done, 16)
            sp.wait_ge(s_out_done, 16 * NQ)

        @block.tensor
        def _(pe):
            pe.wait_ge(s_const_in, 16)
            pe.wait_ge(s_cast_done, 1)

            def misc_free(phase, layer, it, j, after_top, after_v, after_out):
                base = start_of(phase, layer)
                pe.wait_ge(s_top_ready, base + issued(it, j, LAG.exp, after_top))
                pe.wait_ge(s_v_ready, base + issued(it, j, 0, after_v))
                if phase != A:
                    pe.wait_ge(s_added, base + issued(it, j, LAG.out, after_out))

            def turn_input(phase, layer, b, slot):
                nb = (phase + layer) * NB + b
                pe.wait_ge(s_tok_ready, nb + 1)
                nc.tensor.transpose(misc_ps[:, 0:P], tok[slot][:, :], ident).then_inc(s_xturn, 1)
                if phase == B:
                    pe.wait_ge(s_ctok_ready, b + 1)
                    nc.tensor.transpose(misc_ps[:, P:2 * P], ctok[slot][:, :], ident).then_inc(s_cturn, 1)

            def step(phase, layer, it, j):
                base = start_of(phase, layer)
                now = base + it * STEPS + j
                nseq = (phase + layer) * NB
                if here(it, j, LAG.exp):
                    g = now - LAG.exp
                    misc_free(phase, layer, it, j, 0, 0, 0)
                    pe.wait_ge(s_xt_ready, nseq + turned(it, j, 0))
                    if phase == B:
                        pe.wait_ge(s_ct_ready, turned(it, j, 0))
                    pe.wait_ge(s_top_lo, g + 1)
                    nc.tensor.transpose(misc_bf[0:2 * HG, 0:P], top_b[j % 2][:, :], ident_b[:, :]).then_inc(s_top_turn, 1)
                if phase == C and here(it, j, 0):
                    g = now - 2 * GROUPS
                    pe.wait_ge(s_xt_ready, nseq + it * 2 + j // NG + 1)
                    if isinstance(it, int) and it == 0 and j == 0:
                        pe.wait_ge(s_wqkv_in, 16 * (layer + 1))
                    if has(it * STEPS + j - 2):
                        pe.wait_ge(s_cos_done, g - 1)
                        pe.wait_ge(s_sin_done, g - 1)
                    gc = (j % NG) * HG * DH
                    for i in range(2):
                        last = nc.tensor.matmul(proj_ps[j % 2][:, i * HG * DH:(i + 1) * HG * DH], xt[j // NG % 2][:, :],
                                                wqkv_sb[:, i * INNER + gc:i * INNER + gc + HG * DH], start=True, stop=True)
                    last.then_inc(s_proj, 1)
                if here(it, j, LAG.heads):
                    g = now - LAG.heads
                    jl = (j - LAG.heads) % STEPS
                    if phase == C:
                        pe.wait_ge(s_unit_done, g - 2 * GROUPS + 1)
                        if has(it * STEPS + j - LAG.heads - 1):
                            pe.wait_ge(s_k_ready, g)
                        flat = unit[jl % 2][:, :, :, :].rearrange("t a h d -> t (a h d)")
                        for k in range(4):
                            last = nc.tensor.transpose(heads_ps[:, k * P:(k + 1) * P], flat[:, k * P:(k + 1) * P], ident)
                    else:
                        pe.wait_ge(s_xt_ready, nseq + (it * STEPS + j - LAG.heads) // NG + 1 if isinstance(it, int)
                                   else nseq + it * 2 + (j - LAG.heads) // NG + 1)
                        if phase == B:
                            pe.wait_ge(s_ct_ready, (it * STEPS + j - LAG.heads) // NG + 1 if isinstance(it, int)
                                       else it * 2 + (j - LAG.heads) // NG + 1)
                        pe.wait_ge(s_wpad_set, 5)
                        if has(it * STEPS + j - LAG.heads - 1):
                            pe.wait_ge(s_k_ready, g)
                        src = xt if phase == A else ct
                        for i, t in enumerate((xt, src)):
                            w = wpad[:, phase, i, jl % NG, :, :].rearrange("c h d -> c (h d)")
                            last = nc.tensor.matmul(heads_ps[:, i * P:(i + 1) * P], w, t[jl // NG % 2][:, :], start=True, stop=True)
                    last.then_inc(s_heads, 1)
                if here(it, j, LAG.value):
                    g = now - LAG.value
                    jl = (j - LAG.value) % STEPS
                    pe.wait_ge(s_pt_ready, g + 1)
                    pe.wait_ge(s_v_ready, g + 1)
                    pe.wait_ge(s_vone_set, 2 * NG * (2 if phase == C else 1))
                    if has(it * STEPS + j - LAG.value - 1):
                        if phase == A:
                            pe.wait_ge(s_out_ready, g)
                        else:
                            pe.wait_ge(s_ot_ready, g - GROUPS)
                    width = DH if phase == C else DS
                    for h in range(HG):
                        last = nc.tensor.matmul(value_ps[:, h * (DH + 1):h * (DH + 1) + width + 1], prob_t[jl % 2][:, h, :],
                                                val[jl][:, h, 0:width + 1], start=True, stop=True)
                    last.then_inc(s_pv, 1)
                if here(it, j, 0):
                    misc_free(phase, layer, it, j, 1, 0, 0)
                    pe.wait_ge(s_xt_ready, nseq + turned(it, j, 0))
                    if phase == B:
                        pe.wait_ge(s_ct_ready, turned(it, j, 0))
                    if phase != C:
                        pe.wait_ge(s_small_in, 16 * 17)
                    t = (ct if phase == B else xt)[j // NG % 2]
                    if phase == C:
                        w = wqkv_sb[:, 2 * INNER + (j % NG) * HG * DH:2 * INNER + (j % NG + 1) * HG * DH]
                    else:
                        w = (aw if phase == A else bw)[:, 2 * P + (j % NG) * PAD:2 * P + (j % NG + 1) * PAD]
                    n = HG * (DH if phase == C else DS)
                    nc.tensor.matmul(misc_ps[:, 0:n], t[:, :], w, start=True, stop=True).then_inc(s_v_proj, 1)
                if here(it, j, LAG.exp):
                    g = now - LAG.exp
                    jl = (j - LAG.exp) % STEPS
                    pe.wait_ge(s_top_ready, g + 1)
                    nc.tensor.matmul(score_ps[jl % 2][:, :], top_t[jl % 2][:, :], sel_b[:, :], start=False, stop=True,
                                     skip_group_check=True).then_inc(s_shifted_scores, 1)
                if here(it, j, LAG.scores):
                    g = now - LAG.scores
                    jl = (j - LAG.scores) % STEPS
                    pe.wait_ge(s_q_ready, g + 1)
                    pe.wait_ge(s_kz_ready if phase != C else s_k_ready, g + 1)
                    if phase == C:
                        pe.wait_ge(s_k_half, g - 2 * GROUPS + 1)
                    if has(it * STEPS + j - LAG.scores - 2):
                        pe.wait_ge(s_exp_done, g - 1)
                    if phase != B:
                        nc.tensor.matmul(score_ps[jl % 2][:, :].rearrange("q (h k) -> q h k", h=HG), ident_b[:, :],
                                         masks_b[:, phase // 2, :].unsqueeze(1).to_broadcast([P, HG, P]), start=True, stop=False,
                                         skip_group_check=True)
                    keys = kz[jl % 2][:, :, :].rearrange("d h k -> d (h k)")
                    per = 2 if phase == C else 4
                    for k in range(HG // per):
                        last = nc.tensor.matmul(score_ps[jl % 2][:, k * per * P:(k + 1) * per * P], qt[jl % 2][:, k * P:(k + 1) * P],
                                                keys[:, k * per * P:(k + 1) * per * P], start=(phase == B), stop=False,
                                                skip_group_check=True)
                    last.then_inc(s_scores, 1)
                if phase != A and here(it, j, LAG.value):
                    g = now - LAG.value
                    jl = (j - LAG.value) % STEPS
                    pe.wait_ge(s_out_ready, g + 1)
                    if phase == C:
                        flat = head_out[jl % 2][:, :, :].rearrange("t h d -> t (h d)")
                        for k in range(2):
                            last = nc.tensor.transpose(value_ps[:, k * P:(k + 1) * P], flat[:, k * P:(k + 1) * P], ident)
                    else:
                        last = nc.tensor.transpose(value_ps[0:PAD, 0:P], head_out[jl % 2][:, 0, 0:PAD], ident)
                    last.then_inc(s_oturn, 1)
                if here(it, j, LAG.turn):
                    g = now - LAG.turn
                    jl = (j - LAG.turn) % STEPS
                    pe.wait_ge(s_exp_done, g + 1)
                    if has(it * STEPS + j - LAG.turn - 1):
                        pe.wait_ge(s_pt_ready, g)
                    for h in range(HG):
                        last = nc.tensor.transpose(turn_ps[:, h * P:(h + 1) * P], prob[jl % 2][:, h, :], ident)
                    last.then_inc(s_pturn, 1)
                if phase != A and here(it, j, LAG.out):
                    g = now - LAG.out
                    jl = (j - LAG.out) % STEPS
                    misc_free(phase, layer, it, j, 1, 1, 0)
                    pe.wait_ge(s_ot_ready, g - GROUPS + 1)
                    if phase == C:
                        if isinstance(it, int) and it == 0 and j == LAG.out:
                            pe.wait_ge(s_wo_in, 16 * (layer + 1))
                        for k in range(2):
                            c = ((jl % NG) * 2 + k) * P
                            last = nc.tensor.matmul(misc_ps[:, 0:P], head_t[jl % 2][:, k * P:(k + 1) * P], wo_sb[:, c:c + P],
                                                    start=(k == 0), stop=(k == 1))
                    else:
                        last = nc.tensor.matmul(misc_ps[:, 0:P], head_t[jl % 2][0:PAD, 0:P], bwo[:, jl % NG, :], start=True, stop=True)
                    last.then_inc(s_wo_done, 1)
                if j % NG == 2 and here(it, j, -NG + 2):
                    misc_free(phase, layer, it, j, 1, 1, 1)
                    turn_input(phase, layer, it * 2 + j // NG + 1, (j // NG + 1) % 2)

            def mlp_step(layer, it, j):
                q = layer * NQ + it * 2 + j
                if here_q(it, j, 0):
                    pe.wait_ge(s_added, start_of(C, layer + 1))
                    if has(it * 2 + j - 1):
                        pe.wait_ge(s_f_right, q)
                    nc.tensor.matmul(turn_ps[:, 0:QUAD * DH].rearrange("t (b c) -> t b c", b=QUAD), const("shift"),
                                     seq(y, (it * 2 + j) * QUAD, QUAD).rearrange("t (b c) -> t b c", b=QUAD)[:, :, DH:P],
                                     start=True, stop=True).then_inc(s_f_shift, 1)
                if here_q(it, j, 2):
                    k0 = (j % 2) * 6
                    m = q - 2
                    pe.wait_ge(s_f_xt, m + 1)
                    if isinstance(it, int) and it == 1 and j == 0:
                        pe.wait_ge(s_w1_in, 16 * (layer + 1))
                        pe.wait_ge(s_exp_done, start_of(C, layer + 1))
                    for k in range(3):
                        a, n = HB[k]
                        for i, ready in ((1, s_f_gate_ps), (0, s_f_a_ps)):
                            use = 2 * k + 1 - i
                            free = s_f_gate if i else s_f_hid
                            if has(3 * (it * 2 + j - 2) + k - 2):
                                pe.wait_ge(free, 3 * m + k - 1)
                            nc.tensor.matmul(hid_ps[(k0 + use) % 4][0:n, :], w1_sb[:, i * HID + a:i * HID + a + n],
                                             normed_t[j % 2][:, :], start=True, stop=True).then_inc(ready, 1)
                if here_q(it, j, 1):
                    m = q - 1
                    pe.wait_ge(s_f_norm, 4 * m + 4)
                    if has(it * 2 + j - 2):
                        pe.wait_ge(s_f_xt, m)
                    for b in range(QUAD):
                        last = nc.tensor.transpose(heads_ps[:, b * P:(b + 1) * P], normed[(j + 1) % 2][:, b, :], ident)
                    last.then_inc(s_f_turn, 1)
                if here_q(it, j, 3):
                    m = q - 3
                    pe.wait_ge(s_f_hid, 3 * m + 3)
                    if isinstance(it, int) and it == 1 and j == 1:
                        pe.wait_ge(s_w2_in, 48 * (layer + 1))
                        pe.wait_ge(s_ot_ready, start_of(C, layer + 1) - GROUPS)
                    if has(it * 2 + j - 4):
                        pe.wait_ge(s_y_done, m + NQ)
                    for b in range(QUAD):
                        for k, (a, n) in enumerate(HB):
                            last = nc.tensor.matmul(value_ps[:, b * P:(b + 1) * P], hidden[3 * ((j + 1) % 2) + k][0:n, b * P:(b + 1) * P],
                                                    w2_sb[0:n, k * P:(k + 1) * P], start=(k == 0), stop=(k == 2))
                    last.then_inc(s_f_w2, 1)

            for phase in (A, B):
                pe.wait_ge(s_added, start_of(phase, 0))
                turn_input(phase, 0, 0, 0)
                attention(pe, step, phase)
            with pe.Fori(0, DEPTH) as layer:
                pe.wait_ge(s_added, start_of(C, layer))
                pe.wait_ge(s_y_done, (layer + 1) * NQ)
                turn_input(C, layer, 0, 0)
                attention(pe, step, C, layer)
                mlp(pe, mlp_step, layer)

        @block.scalar
        def _(act):
            def copy_input(phase, layer, b, slot):
                nb = (phase + layer) * NB + b
                act.wait_ge(s_xturn, nb + 1)
                if phase == B:
                    act.wait_ge(s_cturn, b + 1)
                if phase == C:
                    act.wait_ge(s_v_proj, start_of(C, layer) + b * NG - NG)
                    act.wait_ge(s_xt_zero, 2)
                    nc.scalar.activation(xt[slot][0:DH, :], misc_ps[0:DH, 0:P], ACT.Copy)
                    nc.scalar.activation(xt[slot][DH:P, 1:P], misc_ps[DH:P, 0:P - 1], ACT.Copy).then_inc(s_xt_ready, 1)
                else:
                    if has(b - 2):
                        act.wait_ge(s_heads, start_of(phase, 0) + b * NG - NG)
                    nc.scalar.activation(xt[slot][:, :], misc_ps[:, 0:P], ACT.Copy).then_inc(s_xt_ready, 1)
                    if phase == B:
                        nc.scalar.activation(ct[slot][:, :], misc_ps[:, P:2 * P], ACT.Copy).then_inc(s_ct_ready, 1)

            def step(phase, layer, it, j):
                base = start_of(phase, layer)
                now = base + it * STEPS + j
                if here(it, j, LAG.exp):
                    g = now - LAG.exp
                    act.wait_ge(s_top_turn, g + 1)
                    nc.scalar.activation(top_t[j % 2][:, :], misc_bf[0:2 * HG, 0:P], ACT.Copy).then_inc(s_top_ready, 1)
                if phase == C and here(it, j, 0):
                    g = now - 2 * GROUPS
                    act.wait_ge(s_proj, g + 1)
                    if has(it * STEPS + j - 1):
                        act.wait_ge(s_nrm2, g)
                    nc.scalar.activation(squares[:, :, :].rearrange("t h d -> t (h d)"), proj_ps[j % 2][:, :], ACT.Square).then_inc(s_sq_done, 1)
                if phase == C and here(it, j, LAG.heads):
                    g = now - LAG.heads
                    jl = (j - LAG.heads) % STEPS
                    act.wait_ge(s_heads, g + 1)
                    act.wait_ge(s_kz_zero, 2)
                    if has(it * STEPS + j - LAG.heads - 2):
                        act.wait_ge(s_scores, g - 1)
                    nc.scalar.activation(qt[jl % 2][:, :], heads_ps[:, 0:2 * P], ACT.Copy).then_inc(s_q_ready, 1)
                    pairs = kz[jl % 2][:, :, :].rearrange("d (a b) k -> d b a k", b=2)
                    turned_k = heads_ps[:, 2 * P:4 * P].rearrange("d (a k) -> d a k", a=2)
                    nc.scalar.activation(pairs[0:DH, 0], turned_k[0:DH], ACT.Copy).then_inc(s_k_half, 1)
                    nc.scalar.activation(pairs[DH:P, 1], turned_k[DH:P], ACT.Copy).then_inc(s_k_ready, 1)
                if phase != B and here(it, j, 0):
                    g = now
                    act.wait_ge(s_v_proj, g + 1)
                    width = DH if phase == C else DS
                    act.wait_ge(s_vone_set, 2 * NG * (2 if phase == C else 1))
                    if has(it * STEPS + j - 2 * NG):
                        act.wait_ge(s_pv, g + 1 - 2 * NG)
                    nc.scalar.activation(val[j][:, :, 0:width], misc_ps[:, 0:HG * width].rearrange("t (h d) -> t h d", h=HG), ACT.Copy).then_inc(s_v_ready, 1)
                if here(it, j, LAG.exp):
                    g = now - LAG.exp
                    act.wait_ge(s_shifted_scores, g + 1)
                    if has(it * STEPS + j - LAG.exp - 2):
                        act.wait_ge(s_pturn, g - 1)
                    nc.scalar.activation(prob[j % 2][:, :, :].rearrange("q h k -> q (h k)"), score_ps[j % 2][:, :], ACT.Exp).then_inc(s_exp_done, 1)
                if phase != A and here(it, j, LAG.value):
                    g = now - LAG.value - GROUPS
                    act.wait_ge(s_oturn, g + 1)
                    if has(it * STEPS + j - LAG.value - 2):
                        act.wait_ge(s_wo_done, g - 1)
                    if phase == C:
                        nc.scalar.activation(head_t[j % 2][:, :], value_ps[:, 0:2 * P], ACT.Copy).then_inc(s_ot_ready, 1)
                    else:
                        nc.scalar.activation(head_t[j % 2][0:PAD, 0:P], value_ps[0:PAD, 0:P], ACT.Copy).then_inc(s_ot_ready, 1)
                if here(it, j, LAG.turn):
                    g = now - LAG.turn
                    act.wait_ge(s_pturn, g + 1)
                    if has(it * STEPS + j - LAG.turn - 2):
                        act.wait_ge(s_pv, g - 1)
                    nc.scalar.activation(prob_t[(j + 1) % 2][:, :, :].rearrange("k h q -> k (h q)"), turn_ps[:, :], ACT.Copy).then_inc(s_pt_ready, 1)
                if j % NG == 2 and here(it, j, -NG + 2):
                    copy_input(phase, layer, it * 2 + j // NG + 1, (j // NG + 1) % 2)

            def mlp_step(layer, it, j):
                q = layer * NQ + it * 2 + j
                if here_q(it, j, 2):
                    m = q - 2
                    for k in range(3):
                        n = HB[k][1]
                        act.wait_ge(s_f_gate_ps, 3 * m + k + 1)
                        if has(it * 2 + j - 4):
                            act.wait_ge(s_f_hid, 3 * m + k - 5)
                        nc.scalar.activation(gate[3 * (j % 2) + k][0:n, :], hid_ps[((j % 2) * 6 + 2 * k) % 4][0:n, :], ACT.Gelu,
                                             bias=mlp_now[0:n, 5 + k:6 + k]).then_inc(s_f_gate, 1)
                if here_q(it, j, 1):
                    m = q - 1
                    act.wait_ge(s_f_turn, m + 1)
                    if has(it * 2 + j - 3):
                        act.wait_ge(s_f_a_ps, 3 * m - 3)
                    nc.scalar.activation(normed_t[(j + 1) % 2][:, :], heads_ps[:, :], ACT.Identity, bias=mlp_now[:, 1:2],
                                         scale=mlp_now[:, 0:1]).then_inc(s_f_xt, 1)

            for phase in (A, B):
                act.wait_ge(s_added, start_of(phase, 0))
                copy_input(phase, 0, 0, 0)
                attention(act, step, phase)
            act.wait_ge(s_table_in, 16 * 11)
            with act.Fori(0, DEPTH) as layer:
                act.wait_ge(s_layer_set, layer + 1)
                act.wait_ge(s_added, start_of(C, layer))
                act.wait_ge(s_y_done, (layer + 1) * NQ)
                copy_input(C, layer, 0, 0)
                attention(act, step, C, layer)
                mlp(act, mlp_step, layer)

        @block.gpsimd
        def _(pool):
            pool.memset(m_at[:, :], 0.0).then_inc(s_zeros_set, 1)
            pool.memset(per_layer[:, :, :], 0.0).then_inc(s_zeros_set, 1)
            pool.memset(b_qk[:, :, :], 0.0).then_inc(s_zeros_set, 1)
            pool.memset(wpad[:, :, :, :, :, :], 0.0).then_inc(s_wpad_set, 1)
            pool.memset(neg_half[:, :], -0.5).then_inc(s_half_set, 1)
            for v in val:
                pool.memset(v[:, :, DS:DS + 1], 1.0).then_inc(s_vone_set, 1)
            pool.wait_ge(s_small_in, 16 * 17)
            pool.wait_ge(s_wpad_set, 1)
            for ph, w, cols in ((A, aw, (P, 0)), (B, bw, (0, P))):
                for i, c in enumerate(cols):
                    nc.gpsimd.tensor_copy(wpad[:, ph, i, :, :, 0:DS], w[:, c:c + P].rearrange("c (g h d) -> c g h d", g=NG, h=HG)).then_inc(s_wpad_set, 1)
            pool.wait_ge(s_half_set, 1)

            def rstd_of(phase, b, slot):
                pool.wait_ge(s_ln_var, phase * NB + b + 1)
                nc.gpsimd.tensor_tensor(rstd[slot][:, 0:1], var[slot][:, 0:1], neg_half[:, 0:1], ALU.pow).then_inc(s_ln_rstd, 1)

            def prepare(phase, layer, b, slot):
                if phase != C:
                    rstd_of(phase, b, slot)

            def step(phase, layer, it, j):
                if j % NG == 1 and here(it, j, -NG + 1):
                    prepare(phase, layer, it * 2 + j // NG + 1, (j // NG + 1) % 2)
                if phase == C and here(it, j, 0):
                    g = layer * GROUPS + it * STEPS + j
                    pool.wait_ge(s_nrm2g, g + 1)
                    nc.gpsimd.tensor_tensor(rnorm[j % 2][:, :], norm2g[j % 2][:, :], neg_half[:, :], ALU.pow).then_inc(s_rn_done, 1)
                    pool.wait_ge(s_cos_done, g + 1)
                    pool.wait_ge(s_sin_done, g + 1)
                    nc.gpsimd.tensor_tensor(rotated[j % 2][:, :, :, :], by_cos[j % 2][:, :, :, :], by_sin[j % 2][:, :, :, :], ALU.add).then_inc(s_rot_done, 1)
                    pool.wait_ge(s_rot_done, g + 1)
                    pool.wait_ge(s_rn_done, g + 1)
                    if has(it * STEPS + j - 2):
                        pool.wait_ge(s_heads, 2 * GROUPS + g - 1)
                    nc.gpsimd.tensor_tensor(unit[j % 2][:, :, :, :].rearrange("t a h d -> t (a h) d"),
                                            rotated[j % 2][:, :, :, :].rearrange("t a h d -> t (a h) d"),
                                            rnorm[j % 2][:, :].unsqueeze(2).to_broadcast([P, 2 * HG, DH]), ALU.mult).then_inc(s_unit_done, 1)

            def mlp_step(layer, it, j):
                q = layer * NQ + it * 2 + j
                if here_q(it, j, 0):
                    pool.wait_ge(s_f_var, q + 1)
                    nc.gpsimd.tensor_tensor(rstd[j % 2][:, :], var[j % 2][:, :], neg_half[:, 0:QUAD], ALU.pow).then_inc(s_f_rstd, 1)

            for phase in (A, B):
                prepare(phase, 0, 0, 0)
                attention(pool, step, phase)
            with pool.Fori(0, NQ // 2) as q2:
                for j in range(2):
                    pool.wait_ge(s_y_var, q2 * 2 + j + 1)
                    nc.gpsimd.tensor_tensor(rstd[j][:, :], var[j][:, :], neg_half[:, 0:QUAD], ALU.pow).then_inc(s_y_rstd, 1)
            pool.wait_ge(s_pv, 2 * GROUPS)
            for v in val:
                pool.memset(v[:, :, DH:DH + 1], 1.0).then_inc(s_vone_set, 1)
            pool.wait_ge(s_scores, 2 * GROUPS)
            for k in kz:
                pool.memset(k[:, :, :], 0.0).then_inc(s_kz_zero, 1)
            pool.wait_ge(s_kz_zero, 2)
            for t in xt:
                pool.memset(t[DH:P, 0:1], 0.0).then_inc(s_xt_zero, 1)
            pool.wait_ge(s_xt_zero, 2)
            pool.wait_ge(s_table_in, 16 * 11)
            with pool.Fori(0, DEPTH) as layer:
                pool.wait_ge(s_added, start_of(C, layer))
                pool.wait_ge(s_y_done, (layer + 1) * NQ)
                attention(pool, step, C, layer)
                mlp(pool, mlp_step, layer)

        @block.vector
        def _(dve):
            dve.wait_ge(s_const_in, 16)
            nc.vector.tensor_copy(ident_b[:, :], ident)
            nc.vector.tensor_copy(masks_b[:, 0, :], const("causal"))
            nc.vector.tensor_copy(masks_b[:, 1, :], const("band"))
            nc.vector.tensor_copy(sel_b[:, :], const("sel", 2 * HG)).then_inc(s_cast_done, 1)
            dve.wait_ge(s_small_in, 16 * 17)
            nc.vector.tensor_scalar(m_at[:, NG:2 * NG], m_at[:, NG:2 * NG], -1.0, None, ALU.mult).then_inc(s_krow_neg, 1)
            dve.wait_ge(s_krow_neg, 1)
            for g in range(NG):
                nc.vector.tensor_scalar(krow[:, g, :], const("iota"), m_at[:, g:g + 1], m_at[:, NG + g:NG + g + 1], ALU.mult, ALU.add).then_inc(s_krow_set, 1)
            dve.wait_ge(s_krow_set, NG)
            dve.wait_ge(s_x_in, 16)

            def ln_stats(phase, b, slot):
                nb = phase * NB + b
                nc.vector.bn_stats(stats[slot][:, 0, :], seq(x, b)).then_inc(s_ln_stat, 1)
                dve.wait_ge(s_ln_stat, nb + 1)
                nc.vector.memset(scratch[:, :], 0.0)
                nc.vector.bn_aggr(mv[slot][:, 0, :], stats[slot][:, 0, :]).then_inc(s_ln_mv, 1)
                dve.wait_ge(s_ln_mv, nb + 1)
                if has(nb - 2):
                    dve.wait_ge(s_ln_rstd, nb - 1)
                nc.vector.tensor_scalar(var[slot][:, 0:1], mv[slot][:, 0, 1:2], EPS, None, ALU.add).then_inc(s_ln_var, 1)

            def prepare(layer, b, slot):
                nb = (C + layer) * NB + b
                dve.wait_ge(s_xturn, nb - 1)
                nc.vector.tensor_scalar(tok[slot][:, :], seq(y, b), 1.0, None, ALU.mult).then_inc(s_tok_ready, 1)

            def ln_apply(phase, b, slot):
                nb = phase * NB + b
                dve.wait_ge(s_ln_rstd, nb + 1)
                if has(nb - 2):
                    dve.wait_ge(s_xturn, nb - 1)
                nc.vector.tensor_scalar(tok[slot][:, :], seq(x, b), mv[slot][:, 0, 0:1], rstd[slot][:, 0:1], ALU.subtract, ALU.mult).then_inc(s_tok_ready, 1)
                if phase == B:
                    if has(b - 2):
                        dve.wait_ge(s_cturn, b - 1)
                    nc.vector.tensor_scalar(ctok[slot][:, :], seq(ctx_all, b), 1.0, None, ALU.mult).then_inc(s_ctok_ready, 1)
                    dve.wait_ge(s_tok_ready, nb + 1)
                    nc.vector.tensor_tensor(seq(x, b), seq(x, b), b_o[:, :], ALU.add).then_inc(s_bias_added, 1)

            def step(phase, layer, it, j):
                base = start_of(phase, layer)
                now = base + it * STEPS + j
                if phase == C and here(it, j, 0):
                    g = now - 2 * GROUPS
                    dve.wait_ge(s_sq_done, g + 1)
                    nc.vector.tensor_reduce(norm2[j % 2][:, :], squares[:, :, :], AX_X, ALU.add).then_inc(s_nrm2, 1)
                    dve.wait_ge(s_nrm2, g + 1)
                    if has(it * STEPS + j - 2):
                        dve.wait_ge(s_rn_done, g - 1)
                    nc.vector.tensor_scalar(norm2g[j % 2][:, :], norm2[j % 2][:, :], 1e-24, None, ALU.max).then_inc(s_nrm2g, 1)
                if here(it, j, LAG.value):
                    g = now - LAG.value
                    jl = (j - LAG.value) % STEPS
                    width = DH if phase == C else DS
                    got = value_ps[:, 0:HG * (DH + 1)].rearrange("t (h d) -> t h d", h=HG)
                    dve.wait_ge(s_pv, g + 1)
                    nc.vector.reciprocal(rsum[j % 2][:, :].unsqueeze(2), got[:, :, width:width + 1]).then_inc(s_rsum_done, 1)
                    dve.wait_ge(s_rsum_done, g + 1)
                    if phase == C:
                        dst = head_out[j % 2][:, :, :]
                    else:
                        dst = head_out[j % 2][:, 0, 0:PAD].rearrange("t (h d) -> t h d", h=HG)
                    if has(it * STEPS + j - LAG.value - 2):
                        if phase == A:
                            dve.wait_ge(s_added, g - 1)
                        else:
                            dve.wait_ge(s_oturn, g - GROUPS - 1)
                    nc.vector.tensor_tensor(dst, got[:, :, 0:width], rsum[j % 2][:, :].unsqueeze(2).to_broadcast([P, HG, width]), ALU.mult).then_inc(s_out_ready, 1)
                if phase == C and here(it, j, 0):
                    g = now - 2 * GROUPS
                    tab = lambda t: t[:, bass.ds(layer * 2 * DH, 2 * DH)].rearrange("t (a d) -> t a d", a=2)
                    got = proj_ps[j % 2][:, :].rearrange("t (a h d) -> t a h d", a=2, h=HG)
                    if has(it * STEPS + j - 2):
                        dve.wait_ge(s_rot_done, g - 1)
                    nc.vector.tensor_tensor(by_cos[j % 2][:, :, :, :], got, tab(rot_cos).unsqueeze(2).to_broadcast([P, 2, HG, DH]), ALU.mult).then_inc(s_cos_done, 1)
                    nc.vector.tensor_tensor(by_sin[j % 2][:, :, :, 0:HALF], got[:, :, :, HALF:DH],
                                            tab(rot_sin)[:, :, 0:HALF].unsqueeze(2).to_broadcast([P, 2, HG, HALF]), ALU.mult)
                    nc.vector.tensor_tensor(by_sin[j % 2][:, :, :, HALF:DH], got[:, :, :, 0:HALF],
                                            tab(rot_sin)[:, :, HALF:DH].unsqueeze(2).to_broadcast([P, 2, HG, HALF]), ALU.mult).then_inc(s_sin_done, 1)
                if phase != C and here(it, j, LAG.heads):
                    g = now - LAG.heads
                    jl = (j - LAG.heads) % STEPS
                    dve.wait_ge(s_heads, g + 1)
                    if has(it * STEPS + j - LAG.heads - 2):
                        dve.wait_ge(s_scores, g - 1)
                    if phase == A:
                        nc.vector.scalar_tensor_tensor(out=qt[j % 2][:, 0:P], in0=heads_ps[:, 0:P], scalar=float(P) ** -0.5, in1=const("qrow"), op0=ALU.mult, op1=ALU.add).then_inc(s_q_ready, 1)
                        nc.vector.tensor_tensor(kt[j % 2][:, :], heads_ps[:, P:2 * P], krow[:, jl % NG, :], ALU.add).then_inc(s_k_ready, 1)
                    else:
                        nc.vector.tensor_scalar(qt[j % 2][:, 0:P], heads_ps[:, 0:P], b_qk[:, 0, jl % NG:jl % NG + 1], float(DS) ** -0.5, ALU.add, ALU.mult).then_inc(s_q_ready, 1)
                        nc.vector.tensor_scalar(kt[j % 2][:, :], heads_ps[:, P:2 * P], b_qk[:, 1, jl % NG:jl % NG + 1], None, ALU.add).then_inc(s_k_ready, 1)
                    dve.wait_ge(s_k_ready, g + 1)
                    nc.vector.tensor_tensor(kz[j % 2][:, :, :], kt[j % 2][:, :].unsqueeze(1).to_broadcast([P, HG, P]),
                                            const("block").unsqueeze(2).to_broadcast([P, HG, P]), ALU.mult).then_inc(s_kz_ready, 1)
                if phase == B and here(it, j, 0):
                    g = now
                    dve.wait_ge(s_v_proj, g + 1)
                    dve.wait_ge(s_vone_set, 2 * NG)
                    if has(it * STEPS + j - 2 * NG):
                        dve.wait_ge(s_pv, g + 1 - 2 * NG)
                    at = slice((j % NG) * PAD, (j % NG + 1) * PAD)
                    nc.vector.tensor_tensor(val[j][:, :, 0:DS], misc_ps[:, 0:PAD].rearrange("t (h d) -> t h d", h=HG),
                                            b_v[:, at].rearrange("t (h d) -> t h d", h=HG), ALU.add).then_inc(s_v_ready, 1)
                if phase != C and j % NG == 0 and here(it, j, -NG):
                    ln_stats(phase, it * 2 + j // NG + 1, (j // NG + 1) % 2)
                if phase != C and j % NG == 1 and here(it, j, -NG + 1):
                    ln_apply(phase, it * 2 + j // NG + 1, (j // NG + 1) % 2)
                if phase == C and j % NG == 1 and here(it, j, -NG + 1):
                    prepare(layer, it * 2 + j // NG + 1, (j // NG + 1) % 2)
                if here(it, j, LAG.scores):
                    g = now - LAG.scores
                    jl = (j - LAG.scores) % STEPS
                    dve.wait_ge(s_scores, g + 1)
                    nc.vector.tensor_reduce(top[jl % 2][:, :], score_ps[jl % 2][:, :].rearrange("q (h k) -> q h k", h=HG), AX_X, ALU.max, negate=True).then_inc(s_top_done, 1)
                    dve.wait_ge(s_top_done, g + 1)
                    if has(it * STEPS + j - LAG.scores - 2):
                        dve.wait_ge(s_top_turn, g - 1)
                    nc.vector.tensor_copy(top_b[jl % 2][:, 0:HG], top[jl % 2][:, :]).then_inc(s_top_hi, 1)
                    dve.wait_ge(s_top_hi, g + 1)
                    nc.vector.tensor_tensor(top_b[jl % 2][:, HG:2 * HG], top[jl % 2][:, :], top_b[jl % 2][:, 0:HG], ALU.subtract).then_inc(s_top_lo, 1)
                if phase == A and here(it, j, LAG.value):
                    g = now - LAG.value
                    jl = (j - LAG.value) % STEPS
                    b = it * 2 + (j - LAG.value) // NG
                    dve.wait_ge(s_out_ready, g + 1)
                    at = bass.ds(b * P + (jl % NG) * PAD, PAD)
                    nc.vector.tensor_tensor(x[:, at], x[:, at], head_out[j % 2][:, 0, 0:PAD], ALU.add).then_inc(s_added, 1)
                if phase != A and here(it, j, LAG.out):
                    g = now - LAG.out
                    jl = (j - LAG.out) % STEPS
                    b = it * 2 + (j - LAG.out) // NG
                    dve.wait_ge(s_wo_done, g - GROUPS + 1)
                    dst = seq(x if phase == B else y, b)
                    if phase == B:
                        dve.wait_ge(s_bias_added, b + 1)
                    dve.wait_ge(s_added, g)
                    nc.vector.tensor_tensor(dst, dst, misc_ps[:, 0:P], ALU.add).then_inc(s_added, 1)

            def mlp_step(layer, it, j):
                q = layer * NQ + it * 2 + j
                if here_q(it, j, 2):
                    m = q - 2
                    for k in range(3):
                        n = HB[k][1]
                        dve.wait_ge(s_f_a_ps, 3 * m + k + 1)
                        dve.wait_ge(s_f_gate, 3 * m + k + 1)
                        if has(it * 2 + j - 4):
                            dve.wait_ge(s_f_w2, m - 1)
                        nc.vector.scalar_tensor_tensor(out=hidden[3 * (j % 2) + k][0:n, :], in0=hid_ps[((j % 2) * 6 + 2 * k + 1) % 4][0:n, :],
                                                       scalar=mlp_now[0:n, 2 + k:3 + k], in1=gate[3 * (j % 2) + k][0:n, :],
                                                       op0=ALU.add, op1=ALU.mult).then_inc(s_f_hid, 1)
                if here_q(it, j, 0):
                    dve.wait_ge(s_f_shift, q + 1)
                    if has(it * 2 + j - 2):
                        dve.wait_ge(s_f_norm, 4 * q - 4)
                    ys = seq(y, (it * 2 + j) * QUAD, QUAD).rearrange("t (b c) -> t b c", b=QUAD)
                    nc.vector.tensor_scalar(shifted[j % 2][:, :, 0:DH], ys[:, :, 0:DH], 1.0, None, ALU.mult).then_inc(s_f_left, 1)
                    nc.vector.tensor_copy(shifted[j % 2][:, :, DH:P], turn_ps[:, 0:QUAD * DH].rearrange("t (b c) -> t b c", b=QUAD)).then_inc(s_f_right, 1)
                    dve.wait_ge(s_f_right, q + 1)
                    dve.wait_ge(s_f_left, q + 1)
                    for b in range(QUAD):
                        nc.vector.bn_stats(stats[j % 2][:, b, :], shifted[j % 2][:, b, :]).then_inc(s_f_stat, 1)
                    dve.wait_ge(s_f_stat, QUAD * (q + 1))
                    nc.vector.memset(scratch[:, :], 0.0)
                    for b in range(QUAD):
                        nc.vector.bn_aggr(mv[j % 2][:, b, :], stats[j % 2][:, b, :]).then_inc(s_f_mv, 1)
                    dve.wait_ge(s_f_mv, QUAD * (q + 1))
                    nc.vector.tensor_scalar(var[j % 2][:, :].unsqueeze(2), mv[j % 2][:, :, 1:2], EPS, None, ALU.add).then_inc(s_f_var, 1)
                    dve.wait_ge(s_f_rstd, q + 1)
                    if has(it * 2 + j - 2):
                        dve.wait_ge(s_f_turn, q - 1)
                    for b in range(QUAD):
                        nc.vector.tensor_scalar(normed[j % 2][:, b, :], shifted[j % 2][:, b, :], mv[j % 2][:, b, 0:1], rstd[j % 2][:, b:b + 1], ALU.subtract, ALU.mult).then_inc(s_f_norm, 1)
                if here_q(it, j, 3):
                    m = q - 3
                    dve.wait_ge(s_f_w2, m + 1)
                    at = (it * 2 + j - 3) * QUAD
                    dst = seq(y, at, QUAD)
                    nc.vector.tensor_tensor(dst, dst, value_ps[:, :], ALU.add).then_inc(s_f_b2, 1)
                    dve.wait_ge(s_f_b2, m + 1)
                    dst = dst.rearrange("t (b c) -> t b c", b=QUAD)
                    nc.vector.tensor_tensor(dst, dst, b2_sb[:, bass.ds(layer * P, P)].unsqueeze(1).to_broadcast([P, QUAD, P]), ALU.add).then_inc(s_y_done, 1)

            for phase in (A, B):
                if phase == B:
                    dve.wait_ge(s_ctx_in, 16)
                dve.wait_ge(s_added, start_of(phase, 0))
                ln_stats(phase, 0, 0)
                ln_apply(phase, 0, 0)
                attention(dve, step, phase)
            dve.wait_ge(s_added, 2 * GROUPS)
            with dve.Fori(0, NQ // 2) as q2:
                for j in range(2):
                    q = q2 * 2 + j
                    for b in range(QUAD):
                        nc.vector.bn_stats(stats[j][:, b, :], seq(x, q * QUAD + b)).then_inc(s_y_stat, 1)
                    dve.wait_ge(s_y_stat, QUAD * (q + 1))
                    nc.vector.memset(scratch[:, :], 0.0)
                    for b in range(QUAD):
                        nc.vector.bn_aggr(mv[j][:, b, :], stats[j][:, b, :]).then_inc(s_y_mv, 1)
                    dve.wait_ge(s_y_mv, QUAD * (q + 1))
                    nc.vector.tensor_scalar(var[j][:, :].unsqueeze(2), mv[j][:, :, 1:2], EPS, None, ALU.add).then_inc(s_y_var, 1)
                    dve.wait_ge(s_y_rstd, q + 1)
                    for b in range(QUAD):
                        last = nc.vector.tensor_scalar(seq(y, q * QUAD + b), seq(x, q * QUAD + b), mv[j][:, b, 0:1], rstd[j][:, b:b + 1], ALU.subtract, ALU.mult)
                    last.then_inc(s_y_done, 1)
            dve.wait_ge(s_table_in, 16 * 11)
            scales = qk_scale[:, :, :, :]
            for dst, src, at, frm in ((rot_cos, "cos", slice(0, DH), slice(0, DH)), (rot_sin, "sin", slice(0, HALF), slice(HALF, DH)),
                                      (rot_sin, "sin", slice(HALF, DH), slice(0, HALF))):
                for l in range(DEPTH):
                    nc.vector.tensor_tensor(dst[:, l * 2 * DH:(l + 1) * 2 * DH].rearrange("t (a d) -> t a d", a=2)[:, :, at],
                                            const(src).rearrange("t (a d) -> t a d", a=2)[:, :, at],
                                            scales[:, l, :, frm], ALU.mult).then_inc(s_tables_set, 1)
            dve.wait_ge(s_tables_set, 3 * DEPTH)
            with dve.Fori(0, DEPTH) as layer:
                dve.wait_ge(s_added, start_of(C, layer))
                dve.wait_ge(s_y_done, (layer + 1) * NQ)
                nc.vector.tensor_scalar(mlp_now[:, :], per_layer[:, :, :].rearrange("p l n -> p (l n)")[:, bass.ds(layer * 8, 8)],
                                        1.0, None, ALU.mult).then_inc(s_layer_set, 1)
                prepare(layer, 0, 0)
                attention(dve, step, C, layer)
                mlp(dve, mlp_step, layer)
            dve.wait_ge(s_y_done, (DEPTH + 1) * NQ)
            for q in range(NQ):
                dst = y[:, q * QUAD * P:(q + 1) * QUAD * P]
                nc.vector.tensor_tensor(dst, dst, x[:, q * QUAD * P:(q + 1) * QUAD * P], ALU.add).then_inc(s_sum_done, 1)


_INS = ["x", "ctx_1024", "L0_attn_W_kqv", "L0_attn_m", "L0_xattn_w_q", "L0_xattn_b_q", "L0_xattn_w_k", "L0_xattn_b_k",
        "L0_xattn_w_v", "L0_xattn_b_v", "L0_xattn_w_o", "L0_xattn_b_o", "L0_ffn_Wqkv", "L0_ffn_q_scale", "L0_ffn_k_scale",
        "L0_ffn_Wo", "L0_ffn_ln_g", "L0_ffn_ln_b", "L0_ffn_W1", "L0_ffn_b1", "L0_ffn_W2", "L0_ffn_b2"]


def kernel(**inputs):
    import numpy as _np
    import concourse.bacc as _bacc
    from concourse import mybir as _mybir
    from concourse.bass_utils import run_bass_kernel_spmd as _run

    nc = _bacc.Bacc("TRN2", target_bir_lowering=False, num_devices=1)
    arrays, args = {}, []
    for name in _INS + ["constants"]:
        a = constants() if name == "constants" else _np.asarray(inputs[name])
        if name.startswith("L0_xattn_w_"):
            a = a.T
        a = _np.ascontiguousarray(a)
        arrays[f"in_{name}_dram"] = a
        args.append(nc.dram_tensor(f"in_{name}_dram", a.shape, _mybir.dt.from_np(a.dtype), kind="ExternalInput").ap())
    args.append(nc.dram_tensor("out_0_dram", (NB, P, P), F32, kind="ExternalOutput").ap())
    build(nc, *args)
    r = _run(nc, [arrays], core_ids=[0])
    return r.results[0]["out_0_dram"]
```

```python
from contextlib import ExitStack

import numpy as np

import concourse.bass as bass
from concourse import mybir

F32 = mybir.dt.float32
BF16 = mybir.dt.bfloat16
ALU = mybir.AluOpType
ACT = mybir.ActivationFunctionType
AX_X = mybir.AxisListType.X

P = 128
NB = 32
NH = 16
HG = 4
NG = NH // HG
GROUPS = NB * NG
DEPTH = 6
DH = 64
HALF = DH // 2
INNER = NH * DH
DS = P // NH
PAD = 32
WINDOW = 32
HID = 341
HB = [(0, 128), (128, 128), (256, 85)]
QUAD = 4
NQ = NB // QUAD
EPS = 1e-5
MASKED = -1e30
A, B, C = 0, 1, 2

STEPS = 2 * NG


class LAG:
    heads = 2
    scores = 3
    exp = 4
    turn = 5
    value = 6
    out = 7


DRAIN = 7

COLS = {}
_at = 0
for _name, _n in (("ident", P), ("shift", P), ("iota", P), ("qrow", P), ("block", HG), ("cos", 2 * DH),
                  ("sin", 2 * DH), ("causal", P), ("band", P), ("sel", HG * P)):
    COLS[_name] = (_at, _n)
    _at += _n
NCONST = _at


def constants():
    t = np.zeros((P, NCONST), np.float32)

    def put(name, v):
        a, n = COLS[name]
        t[:v.shape[0], a:a + n] = v.reshape(v.shape[0], n)

    i = np.arange(P)
    put("ident", np.eye(P, dtype=np.float32))
    put("shift", np.eye(P, k=1, dtype=np.float32))
    put("iota", np.tile(i.astype(np.float32), (P, 1)))
    qrow = np.zeros((P, P), np.float32)
    qrow[DS::PAD] = 1.0
    qrow[DS + 1::PAD] = i
    put("qrow", qrow)
    put("block", (i[:, None] // PAD == np.arange(HG)[None]).astype(np.float32))
    half = np.arange(0, DH, 2, dtype=np.float32)
    inv_freq = (np.float32(1.0) / np.float32(10000.0) ** (half / np.float32(DH))).astype(np.float32)
    pos = i.astype(np.float32)
    freqs = pos[:, None] * inv_freq[None]
    base = (half + np.float32(0.4 * DH)) / np.float32(1.4 * DH)
    power = (pos - P // 2) / np.float32(WINDOW // 2)
    scale = (base[None] ** power[:, None]).astype(np.float32)
    cos, sin = np.cos(freqs), np.sin(freqs)
    both = lambda q, k: np.stack([8.0 * q, k], 1)
    inv = np.float32(1.0) / scale
    put("cos", both(np.concatenate([cos * scale] * 2, -1), np.concatenate([cos * inv] * 2, -1)))
    put("sin", both(np.concatenate([-sin * scale, sin * scale], -1), np.concatenate([-sin * inv, sin * inv], -1)))
    ahead = i[:, None] - i[None]
    put("causal", np.where(ahead >= 0, 0.0, MASKED))
    put("band", np.where((ahead >= 0) & (ahead <= WINDOW), 0.0, MASKED))
    sel = np.zeros((2 * HG, HG, P), np.float32)
    for h in range(HG):
        sel[h, h] = sel[HG + h, h] = 1.0
    put("sel", sel)
    return t


def has(index):
    return not isinstance(index, int) or index >= 0


def in_range(it, j, lag, n):
    return not isinstance(it, int) or 0 <= it * n[1] + j - lag < n[0]


def build(nc, x_in, ctx_in, a_w, a_m, b_wq, b_bq, b_wk, b_bk, b_wv, b_bv, b_wo, b_bo, wqkv, q_scale, k_scale,
          wo, ln_g, ln_b, w1, b1, w2, b2, const_d, out):
    with ExitStack() as stack:
        def sb(name, shape, dt=F32):
            return stack.enter_context(nc.sbuf_tensor(name, shape, dt))

        def ring(name, n, shape, dt=F32):
            return [sb(f"{name}{i}", shape, dt) for i in range(n)]

        x = sb("x", [P, NB * P])
        y = sb("y", [P, NB * P])
        ctx_all = sb("ctx_all", [P, NB * P])
        cst = sb("cst", [P, NCONST])
        ident = cst[:, 0:P]
        ident_b = sb("ident_b", [P, P], BF16)
        masks_b = sb("masks_b", [P, 2, P], BF16)
        sel_b = sb("sel_b", [2 * HG, HG * P], BF16)
        neg_half = sb("neg_half", [P, 2 * HG])
        stage = sb("stage", [P, 4 * P])
        aw = sb("aw", [P, 3 * P])
        bw = sb("bw", [P, 3 * P])
        wpad = sb("wpad", [P, 2, 2, NG, HG, PAD])
        bwo = sb("bwo", [PAD, NG, P])
        m_at = sb("m_at", [P, 2 * NG])
        krow = sb("krow", [P, NG, P])
        b_qk = sb("b_qk", [P, 2, NG])
        b_v = sb("b_v", [P, P])
        b_o = sb("b_o", [P, P])
        wqkv_sb = sb("wqkv_sb", [P, 3 * INNER])
        wo_sb = sb("wo_sb", [P, INNER])
        w1_sb = sb("w1_sb", [P, 2 * HID])
        w2_sb = sb("w2_sb", [P, 3 * P])
        qk_scale = sb("qk_scale", [P, DEPTH, 2, DH])
        rot_cos = sb("rot_cos", [P, DEPTH * 2 * DH])
        rot_sin = sb("rot_sin", [P, DEPTH * 2 * DH])
        per_layer = sb("per_layer", [P, DEPTH, 8])
        mlp_now = sb("mlp_now", [P, 8])
        b2_sb = sb("b2_sb", [P, DEPTH * P])
        tok = ring("tok", 2, [P, P])
        xt = ring("xt", 2, [P, P])
        ct = ring("ct", 2, [P, P])
        ctok = ring("ctok", 2, [P, P])
        squares = sb("squares", [P, 2 * HG, DH])
        norm2 = ring("norm2", 2, [P, 2 * HG])
        norm2g = ring("norm2g", 2, [P, 2 * HG])
        rnorm = ring("rnorm", 2, [P, 2 * HG])
        by_cos = ring("by_cos", 2, [P, 2, HG, DH])
        by_sin = ring("by_sin", 2, [P, 2, HG, DH])
        rotated = ring("rotated", 2, [P, 2, HG, DH])
        unit = ring("unit", 2, [P, 2, HG, DH])
        qt = ring("qt", 2, [P, 2 * P])
        kt = ring("kt", 2, [P, P])
        kz = ring("kz", 2, [P, HG, P])
        val = ring("val", 2 * NG, [P, HG, DH + 1])
        top = ring("top", 2, [P, HG])
        top_b = ring("top_b", 2, [P, 2 * HG], BF16)
        top_t = ring("top_t", 2, [2 * HG, P], BF16)
        prob = ring("prob", 2, [P, HG, P])
        prob_t = ring("prob_t", 2, [P, HG, P])
        rsum = ring("rsum", 2, [P, HG])
        head_out = ring("head_out", 2, [P, HG, DH])
        head_t = ring("head_t", 2, [P, 2 * P])
        stats = ring("stats", 2, [P, QUAD, 6])
        mv = ring("mv", 2, [P, QUAD, 2])
        scratch = sb("scratch", [P, 1])
        var = ring("var", 2, [P, QUAD])
        rstd = ring("rstd", 2, [P, QUAD])
        shifted = ring("shifted", 2, [P, QUAD, P])
        normed = ring("normed", 2, [P, QUAD, P])
        normed_t = ring("normed_t", 2, [P, QUAD * P])
        gate = ring("gate", 6, [P, QUAD * P])
        hidden = ring("hidden", 6, [P, QUAD * P])

        bank = [stack.enter_context(nc.psum_tensor(f"bank{i}", [P, 512], F32)) for i in range(8)]
        proj_ps = bank[0:2]
        misc_ps = bank[2]
        misc_bf = misc_ps[:, :].bitcast(BF16)
        heads_ps = bank[3]
        score_ps = bank[4:6]
        turn_ps = bank[6]
        value_ps = bank[7]
        hid_ps = [bank[0], bank[1], bank[4], bank[5]]

        def sem(name):
            return stack.enter_context(nc.semaphore(name))

        s_const_in = sem("const_in")
        s_x_in = sem("x_in")
        s_ctx_in = sem("ctx_in")
        s_small_in = sem("small_in")
        s_table_in = sem("table_in")
        s_wqkv_in = sem("wqkv_in")
        s_wo_in = sem("wo_in")
        s_w1_in = sem("w1_in")
        s_w2_in = sem("w2_in")
        s_out_done = sem("out_done")
        s_zeros_set = sem("zeros_set")
        s_cast_done = sem("cast_done")
        s_wpad_set = sem("wpad_set")
        s_krow_set = sem("krow_set")
        s_krow_neg = sem("krow_neg")
        s_tables_set = sem("tables_set")
        s_vone_set = sem("vone_set")
        s_half_set = sem("half_set")
        s_kz_zero = sem("kz_zero")
        s_xt_zero = sem("xt_zero")
        s_ln_stat = sem("ln_stat")
        s_ln_mv = sem("ln_mv")
        s_ln_var = sem("ln_var")
        s_ln_rstd = sem("ln_rstd")
        s_tok_ready = sem("tok_ready")
        s_xturn = sem("xturn")
        s_xt_ready = sem("xt_ready")
        s_cturn = sem("cturn")
        s_ct_ready = sem("ct_ready")
        s_ctok_ready = sem("ctok_ready")
        s_proj = sem("proj")
        s_sq_done = sem("sq_done")
        s_nrm2 = sem("nrm2")
        s_nrm2g = sem("nrm2g")
        s_rn_done = sem("rn_done")
        s_cos_done = sem("cos_done")
        s_sin_done = sem("sin_done")
        s_rot_done = sem("rot_done")
        s_unit_done = sem("unit_done")
        s_heads = sem("heads")
        s_q_ready = sem("q_ready")
        s_k_half = sem("k_half")
        s_k_ready = sem("k_ready")
        s_kz_ready = sem("kz_ready")
        s_v_proj = sem("v_proj")
        s_v_ready = sem("v_ready")
        s_scores = sem("scores")
        s_top_done = sem("top_done")
        s_top_hi = sem("top_hi")
        s_top_lo = sem("top_lo")
        s_top_turn = sem("top_turn")
        s_top_ready = sem("top_ready")
        s_shifted_scores = sem("shifted_scores")
        s_exp_done = sem("exp_done")
        s_pturn = sem("pturn")
        s_pt_ready = sem("pt_ready")
        s_pv = sem("pv")
        s_rsum_done = sem("rsum_done")
        s_out_ready = sem("out_ready")
        s_oturn = sem("oturn")
        s_ot_ready = sem("ot_ready")
        s_wo_done = sem("wo_done")
        s_added = sem("added")
        s_bias_added = sem("bias_added")
        s_f_shift = sem("f_shift")
        s_f_left = sem("f_left")
        s_f_right = sem("f_right")
        s_f_stat = sem("f_stat")
        s_f_mv = sem("f_mv")
        s_f_var = sem("f_var")
        s_f_rstd = sem("f_rstd")
        s_f_norm = sem("f_norm")
        s_f_b2 = sem("f_b2")
        s_f_turn = sem("f_turn")
        s_f_xt = sem("f_xt")
        s_f_gate_ps = sem("f_gate_ps")
        s_f_a_ps = sem("f_a_ps")
        s_f_gate = sem("f_gate")
        s_f_hid = sem("f_hid")
        s_f_w2 = sem("f_w2")
        s_y_done = sem("y_done")
        s_layer_set = sem("layer_set")
        s_y_stat = sem("y_stat")
        s_y_mv = sem("y_mv")
        s_y_var = sem("y_var")
        s_y_rstd = sem("y_rstd")
        s_sum_done = sem("sum_done")

        def const(name, rows=P):
            a, n = COLS[name]
            return cst[0:rows, a:a + n]

        def seq(t, b, n=1):
            return t[:, bass.ds(b * P, n * P)]

        def start_of(phase, layer):
            return phase * GROUPS + layer * GROUPS

        def attention(eng, step, phase, layer=0):
            bodies = GROUPS // STEPS
            for j in range(STEPS):
                step(phase, layer, 0, j)
            with eng.Fori(1, bodies - 1) as it:
                for j in range(STEPS):
                    step(phase, layer, it, j)
            for j in range(STEPS):
                step(phase, layer, bodies - 1, j)
            for j in range(DRAIN):
                step(phase, layer, bodies, j)

        def mlp(eng, step, layer):
            for it in (0, 1):
                for j in range(2):
                    step(layer, it, j)
            with eng.Fori(2, NQ // 2) as it:
                for j in range(2):
                    step(layer, it, j)
            for j in range(3):
                step(layer, NQ // 2 + j // 2, j % 2)

        def here(it, j, lag):
            return in_range(it, j, lag, (GROUPS, STEPS))

        def here_q(it, j, lag):
            return in_range(it, j, lag, (NQ, 2))

        def issued(it, j, lag, after):
            if not isinstance(it, int):
                return it * STEPS + j - lag + after
            return max(0, min(GROUPS, it * STEPS + j - lag + after))

        def turned(it, j, after):
            done = 1 + j // NG + (1 if j % NG > 2 or (j % NG == 2 and after) else 0)
            if not isinstance(it, int):
                return it * 2 + done
            return min(NB, it * 2 + done)

        block = stack.enter_context(nc.Block())

        @block.sync
        def _(sp):
            sp.dma_start(cst[:, :], const_d).then_inc(s_const_in, 16)
            sp.dma_start(x[:, :].rearrange("t (b c) -> t b c", c=P), x_in.rearrange("b t c -> t b c")).then_inc(s_x_in, 16)
            sp.dma_start(aw[:, :], a_w).then_inc(s_small_in, 16)
            sp.dma_start(bw[:, 0:P], b_wq).then_inc(s_small_in, 16)
            sp.dma_start(bw[:, P:2 * P], b_wk).then_inc(s_small_in, 16)
            sp.dma_start(bw[:, 2 * P:3 * P], b_wv).then_inc(s_small_in, 16)
            sp.dma_start(bwo[:, :, :], b_wo.rearrange("(g r) c -> r g c", r=PAD)).then_inc(s_small_in, 16)
            sp.dma_start(b_v[:, :], b_bv.partition_broadcast(P)).then_inc(s_small_in, 16)
            sp.dma_start(b_o[:, :], b_bo.partition_broadcast(P)).then_inc(s_small_in, 16)
            sp.wait_ge(s_zeros_set, 3)
            with nc.allow_non_contiguous_dma("small loads"):
                for r in range(2):
                    sp.dma_start(m_at[DS + r::PAD, r * NG:(r + 1) * NG],
                                 a_m.rearrange("(g h) a b -> h (g a b)", h=HG)).then_inc(s_small_in, 16)
                for i, v in enumerate((b_bq, b_bk)):
                    for h in range(HG):
                        sp.dma_start(b_qk[PAD * h:PAD * h + DS, i, :],
                                     v.rearrange("(g h d) -> h d g", h=HG, d=DS)[h]).then_inc(s_small_in, 16)
                sp.dma_start(ctx_all[:, :].rearrange("t (b c) -> t b c", c=P), ctx_in.rearrange("b t c -> t b c")).then_inc(s_ctx_in, 16)
                for i, v in enumerate((q_scale, k_scale)):
                    sp.dma_start(qk_scale[:, :, i, :], v.partition_broadcast(P)).then_inc(s_table_in, 16)
                sp.dma_start(per_layer[:, :, 0], ln_g.rearrange("l c -> c l")).then_inc(s_table_in, 16)
                sp.dma_start(per_layer[:, :, 1], ln_b.rearrange("l c -> c l")).then_inc(s_table_in, 16)
                sp.dma_start(b2_sb[:, :].rearrange("p (l c) -> p l c", c=P), b2.partition_broadcast(P)).then_inc(s_table_in, 16)
                for i in range(2):
                    for k, (a, n) in enumerate(HB):
                        sp.dma_start(per_layer[0:n, :, 2 + 3 * i + k],
                                     b1[:, i * HID + a:i * HID + a + n].rearrange("l p -> p l")).then_inc(s_table_in, 16)
            for l in range(DEPTH):
                if l:
                    sp.wait_ge(s_v_proj, start_of(C, l))
                sp.dma_start(wqkv_sb[:, :], wqkv[l]).then_inc(s_wqkv_in, 16)
                if l:
                    sp.wait_ge(s_wo_done, start_of(C, l) - GROUPS)
                sp.dma_start(wo_sb[:, :].rearrange("p (k c) -> p k c", c=P), wo[l].rearrange("(k p) c -> p k c", p=P)).then_inc(s_wo_in, 16)
                if l:
                    sp.wait_ge(s_f_a_ps, 3 * NQ * l)
                    sp.wait_ge(s_f_w2, NQ * l)
                sp.dma_start(w1_sb[:, :], w1[l]).then_inc(s_w1_in, 16)
                for k, (a, n) in enumerate(HB):
                    sp.dma_start(w2_sb[0:n, k * P:(k + 1) * P], w2[l, a:a + n]).then_inc(s_w2_in, 16)
            for q in range(NQ):
                sp.wait_ge(s_sum_done, q + 1)
                sp.dma_start(out[q * QUAD:(q + 1) * QUAD].rearrange("b t c -> t b c"),
                             y[:, q * QUAD * P:(q + 1) * QUAD * P].rearrange("t (b c) -> t b c", c=P)).then_inc(s_out_done, 16)
            sp.wait_ge(s_out_done, 16 * NQ)

        @block.tensor
        def _(pe):
            pe.wait_ge(s_const_in, 16)
            pe.wait_ge(s_cast_done, 1)

            def turn_input(phase, layer, b, slot):
                nb = (phase + layer) * NB + b
                pe.wait_ge(s_tok_ready, nb + 1)
                nc.tensor.transpose(misc_ps[:, 0:P], tok[slot][:, :], ident).then_inc(s_xturn, 1)
                if phase == B:
                    pe.wait_ge(s_ctok_ready, b + 1)
                    nc.tensor.transpose(misc_ps[:, P:2 * P], ctok[slot][:, :], ident).then_inc(s_cturn, 1)

            def turn_heads(phase, layer, it, j):
                base = start_of(phase, layer)
                now = base + it * STEPS + j
                nseq = (phase + layer) * NB
                if here(it, j, LAG.heads):
                    g = now - LAG.heads
                    jl = (j - LAG.heads) % STEPS
                    if phase == C:
                        pe.wait_ge(s_unit_done, g - 2 * GROUPS + 1)
                        if has(it * STEPS + j - LAG.heads - 1):
                            pe.wait_ge(s_k_ready, g)
                        flat = unit[jl % 2][:, :, :, :].rearrange("t a h d -> t (a h d)")
                        for k in range(4):
                            last = nc.tensor.transpose(heads_ps[:, k * P:(k + 1) * P], flat[:, k * P:(k + 1) * P], ident)
                    else:
                        if j % NG == LAG.heads:
                            nth = it * 2 + j // NG + 1
                            pe.wait_ge(s_xt_ready, nseq + nth)
                            if phase == B:
                                pe.wait_ge(s_ct_ready, nth)
                        if isinstance(it, int) and it == 0 and j == LAG.heads:
                            pe.wait_ge(s_wpad_set, 5)
                        if has(it * STEPS + j - LAG.heads - 1):
                            pe.wait_ge(s_k_ready, g)
                        src = xt if phase == A else ct
                        for i, t in enumerate((xt, src)):
                            w = wpad[:, phase, i, jl % NG, :, :].rearrange("c h d -> c (h d)")
                            last = nc.tensor.matmul(heads_ps[:, i * P:(i + 1) * P], w, t[jl // NG % 2][:, :], start=True, stop=True)
                    last.then_inc(s_heads, 1)

            def project(phase, layer, it, j):
                base = start_of(phase, layer)
                now = base + it * STEPS + j
                nseq = (phase + layer) * NB
                if phase == C and here(it, j, 0):
                    g = now - 2 * GROUPS
                    if j % NG == 0:
                        pe.wait_ge(s_xt_ready, nseq + it * 2 + j // NG + 1)
                    if isinstance(it, int) and it == 0 and j == 0:
                        pe.wait_ge(s_wqkv_in, 16 * (layer + 1))
                    gc = (j % NG) * HG * DH
                    for i in range(2):
                        last = nc.tensor.matmul(proj_ps[j % 2][:, i * HG * DH:(i + 1) * HG * DH], xt[j // NG % 2][:, :],
                                                wqkv_sb[:, i * INNER + gc:i * INNER + gc + HG * DH], start=True, stop=True)
                    last.then_inc(s_proj, 1)

            def project_out(phase, layer, it, j):
                base = start_of(phase, layer)
                now = base + it * STEPS + j
                if phase != A and here(it, j, LAG.out):
                    g = now - LAG.out
                    jl = (j - LAG.out) % STEPS
                    pe.wait_ge(s_ot_ready, g - GROUPS + 1)
                    if phase == C:
                        if isinstance(it, int) and it == 0 and j == LAG.out:
                            pe.wait_ge(s_wo_in, 16 * (layer + 1))
                        for k in range(2):
                            c = ((jl % NG) * 2 + k) * P
                            last = nc.tensor.matmul(turn_ps[:, 0:P], head_t[jl % 2][:, k * P:(k + 1) * P], wo_sb[:, c:c + P],
                                                    start=(k == 0), stop=(k == 1))
                    else:
                        last = nc.tensor.matmul(turn_ps[:, 0:P], head_t[jl % 2][0:PAD, 0:P], bwo[:, jl % NG, :], start=True, stop=True)
                    last.then_inc(s_wo_done, 1)

            def turn_maxima(phase, layer, it, j):
                base = start_of(phase, layer)
                now = base + it * STEPS + j
                nseq = (phase + layer) * NB
                if here(it, j, LAG.exp):
                    g = now - LAG.exp
                    pe.wait_ge(s_v_ready, base + issued(it, j, 0, 0))
                    if j % NG == 3:
                        pe.wait_ge(s_xt_ready, nseq + turned(it, j, 0))
                        if phase == B:
                            pe.wait_ge(s_ct_ready, turned(it, j, 0))
                    pe.wait_ge(s_top_lo, g + 1)
                    nc.tensor.transpose(misc_bf[0:2 * HG, 0:P], top_b[j % 2][:, :], ident_b[:, :]).then_inc(s_top_turn, 1)

            def sum_values(phase, layer, it, j):
                base = start_of(phase, layer)
                now = base + it * STEPS + j
                if here(it, j, LAG.value):
                    g = now - LAG.value
                    jl = (j - LAG.value) % STEPS
                    pe.wait_ge(s_pt_ready, g + 1)
                    if phase == A and has(it * STEPS + j - LAG.value - 1):
                        pe.wait_ge(s_out_ready, g)
                    width = DH if phase == C else DS
                    for h in range(HG):
                        last = nc.tensor.matmul(value_ps[:, h * (DH + 1):h * (DH + 1) + width + 1], prob_t[jl % 2][:, h, :],
                                                val[jl][:, h, 0:width + 1], start=True, stop=True)
                    last.then_inc(s_pv, 1)

            def shift_scores(phase, layer, it, j):
                base = start_of(phase, layer)
                now = base + it * STEPS + j
                if here(it, j, LAG.exp):
                    g = now - LAG.exp
                    jl = (j - LAG.exp) % STEPS
                    pe.wait_ge(s_top_ready, g + 1)
                    nc.tensor.matmul(score_ps[jl % 2][:, :], top_t[jl % 2][:, :], sel_b[:, :], start=False, stop=True,
                                     skip_group_check=True).then_inc(s_shifted_scores, 1)

            def project_values(phase, layer, it, j):
                base = start_of(phase, layer)
                nseq = (phase + layer) * NB
                if here(it, j, 0):
                    if not here(it, j, LAG.exp):
                        pe.wait_ge(s_v_ready, base + issued(it, j, 0, 0))
                        pe.wait_ge(s_xt_ready, nseq + turned(it, j, 0))
                        if phase == B:
                            pe.wait_ge(s_ct_ready, turned(it, j, 0))
                        if phase != C:
                            pe.wait_ge(s_small_in, 16 * 17)
                    t = (ct if phase == B else xt)[j // NG % 2]
                    if phase == C:
                        w = wqkv_sb[:, 2 * INNER + (j % NG) * HG * DH:2 * INNER + (j % NG + 1) * HG * DH]
                    else:
                        w = (aw if phase == A else bw)[:, 2 * P + (j % NG) * PAD:2 * P + (j % NG + 1) * PAD]
                    n = HG * (DH if phase == C else DS)
                    nc.tensor.matmul(misc_ps[:, 0:n], t[:, :], w, start=True, stop=True).then_inc(s_v_proj, 1)

            def turn_probs(phase, layer, it, j):
                base = start_of(phase, layer)
                now = base + it * STEPS + j
                if here(it, j, LAG.turn):
                    g = now - LAG.turn
                    jl = (j - LAG.turn) % STEPS
                    pe.wait_ge(s_exp_done, g + 1)
                    if phase != A and here(it, j, LAG.out):
                        pe.wait_ge(s_added, base + issued(it, j, LAG.out, 1))
                    for h in range(HG):
                        last = nc.tensor.transpose(turn_ps[:, h * P:(h + 1) * P], prob[jl % 2][:, h, :], ident)
                    last.then_inc(s_pturn, 1)

            def scores(phase, layer, it, j):
                base = start_of(phase, layer)
                now = base + it * STEPS + j
                if here(it, j, LAG.scores):
                    g = now - LAG.scores
                    jl = (j - LAG.scores) % STEPS
                    if phase != C:
                        pe.wait_ge(s_kz_ready, g + 1)
                    elif not here(it, j, LAG.heads):
                        pe.wait_ge(s_k_ready, g + 1)
                    if phase != B:
                        nc.tensor.matmul(score_ps[jl % 2][:, :].rearrange("q (h k) -> q h k", h=HG), ident_b[:, :],
                                         masks_b[:, phase // 2, :].unsqueeze(1).to_broadcast([P, HG, P]), start=True, stop=False,
                                         skip_group_check=True)
                    keys = kz[jl % 2][:, :, :].rearrange("d h k -> d (h k)")
                    per = 2 if phase == C else 4
                    for k in range(HG // per):
                        last = nc.tensor.matmul(score_ps[jl % 2][:, k * per * P:(k + 1) * per * P], qt[jl % 2][:, k * P:(k + 1) * P],
                                                keys[:, k * per * P:(k + 1) * per * P], start=(phase == B), stop=False,
                                                skip_group_check=True)
                    last.then_inc(s_scores, 1)

            def turn_out(phase, layer, it, j):
                base = start_of(phase, layer)
                now = base + it * STEPS + j
                if phase != A and here(it, j, LAG.value):
                    g = now - LAG.value
                    jl = (j - LAG.value) % STEPS
                    pe.wait_ge(s_out_ready, g + 1)
                    if phase == C:
                        flat = head_out[jl % 2][:, :, :].rearrange("t h d -> t (h d)")
                        for k in range(2):
                            last = nc.tensor.transpose(value_ps[:, k * P:(k + 1) * P], flat[:, k * P:(k + 1) * P], ident)
                    else:
                        last = nc.tensor.transpose(value_ps[0:PAD, 0:P], head_out[jl % 2][:, 0, 0:PAD], ident)
                    last.then_inc(s_oturn, 1)

            def turn_next(phase, layer, it, j):
                base = start_of(phase, layer)
                if j % NG == 2 and here(it, j, -NG + 2):
                    pe.wait_ge(s_v_ready, base + issued(it, j, 0, 1))
                    turn_input(phase, layer, it * 2 + j // NG + 1, (j // NG + 1) % 2)

            def step(phase, layer, it, j):
                if phase == C:
                    turn_heads(phase, layer, it, j)
                    project(phase, layer, it, j)
                    project_out(phase, layer, it, j)
                    turn_maxima(phase, layer, it, j)
                    sum_values(phase, layer, it, j)
                    shift_scores(phase, layer, it, j)
                    project_values(phase, layer, it, j)
                    turn_probs(phase, layer, it, j)
                    scores(phase, layer, it, j)
                    turn_out(phase, layer, it, j)
                    turn_next(phase, layer, it, j)
                else:
                    turn_heads(phase, layer, it, j)
                    project_out(phase, layer, it, j)
                    sum_values(phase, layer, it, j)
                    turn_maxima(phase, layer, it, j)
                    turn_probs(phase, layer, it, j)
                    shift_scores(phase, layer, it, j)
                    project_values(phase, layer, it, j)
                    scores(phase, layer, it, j)
                    turn_out(phase, layer, it, j)
                    turn_next(phase, layer, it, j)

            def mlp_step(layer, it, j):
                q = layer * NQ + it * 2 + j
                if here_q(it, j, 0):
                    pe.wait_ge(s_added, start_of(C, layer + 1))
                    if has(it * 2 + j - 1):
                        pe.wait_ge(s_f_right, q)
                    nc.tensor.matmul(turn_ps[:, 0:QUAD * DH].rearrange("t (b c) -> t b c", b=QUAD), const("shift"),
                                     seq(y, (it * 2 + j) * QUAD, QUAD).rearrange("t (b c) -> t b c", b=QUAD)[:, :, DH:P],
                                     start=True, stop=True).then_inc(s_f_shift, 1)
                if here_q(it, j, 2):
                    k0 = (j % 2) * 6
                    m = q - 2
                    pe.wait_ge(s_f_xt, m + 1)
                    if isinstance(it, int) and it == 1 and j == 0:
                        pe.wait_ge(s_w1_in, 16 * (layer + 1))
                        pe.wait_ge(s_exp_done, start_of(C, layer + 1))
                    for k in range(3):
                        a, n = HB[k]
                        for i, ready in ((1, s_f_gate_ps), (0, s_f_a_ps)):
                            use = 2 * k + 1 - i
                            free = s_f_gate if i else s_f_hid
                            if has(3 * (it * 2 + j - 2) + k - 2):
                                pe.wait_ge(free, 3 * m + k - 1)
                            nc.tensor.matmul(hid_ps[(k0 + use) % 4][0:n, :], w1_sb[:, i * HID + a:i * HID + a + n],
                                             normed_t[j % 2][:, :], start=True, stop=True).then_inc(ready, 1)
                if here_q(it, j, 1):
                    m = q - 1
                    pe.wait_ge(s_f_norm, 4 * m + 4)
                    if has(it * 2 + j - 2):
                        pe.wait_ge(s_f_xt, m)
                    for b in range(QUAD):
                        last = nc.tensor.transpose(heads_ps[:, b * P:(b + 1) * P], normed[(j + 1) % 2][:, b, :], ident)
                    last.then_inc(s_f_turn, 1)
                if here_q(it, j, 3):
                    m = q - 3
                    pe.wait_ge(s_f_hid, 3 * m + 3)
                    if isinstance(it, int) and it == 1 and j == 1:
                        pe.wait_ge(s_w2_in, 48 * (layer + 1))
                        pe.wait_ge(s_ot_ready, start_of(C, layer + 1) - GROUPS)
                    if has(it * 2 + j - 4):
                        pe.wait_ge(s_y_done, m + NQ)
                    for b in range(QUAD):
                        for k, (a, n) in enumerate(HB):
                            last = nc.tensor.matmul(value_ps[:, b * P:(b + 1) * P], hidden[3 * ((j + 1) % 2) + k][0:n, b * P:(b + 1) * P],
                                                    w2_sb[0:n, k * P:(k + 1) * P], start=(k == 0), stop=(k == 2))
                    last.then_inc(s_f_w2, 1)

            for phase in (A, B):
                pe.wait_ge(s_added, start_of(phase, 0))
                turn_input(phase, 0, 0, 0)
                attention(pe, step, phase)
            with pe.Fori(0, DEPTH) as layer:
                pe.wait_ge(s_added, start_of(C, layer))
                pe.wait_ge(s_y_done, (layer + 1) * NQ)
                turn_input(C, layer, 0, 0)
                attention(pe, step, C, layer)
                mlp(pe, mlp_step, layer)

        @block.scalar
        def _(act):
            def copy_input(phase, layer, b, slot):
                nb = (phase + layer) * NB + b
                act.wait_ge(s_xturn, nb + 1)
                if phase == B:
                    act.wait_ge(s_cturn, b + 1)
                if phase == C:
                    if isinstance(b, int) and b < 2:
                        act.wait_ge(s_xt_zero, 2)
                    nc.scalar.activation(xt[slot][0:DH, :], misc_ps[0:DH, 0:P], ACT.Copy)
                    nc.scalar.activation(xt[slot][DH:P, 1:P], misc_ps[DH:P, 0:P - 1], ACT.Copy).then_inc(s_xt_ready, 1)
                else:
                    nc.scalar.activation(xt[slot][:, :], misc_ps[:, 0:P], ACT.Copy).then_inc(s_xt_ready, 1)
                    if phase == B:
                        nc.scalar.activation(ct[slot][:, :], misc_ps[:, P:2 * P], ACT.Copy).then_inc(s_ct_ready, 1)

            def copy_heads(phase, layer, it, j):
                base = start_of(phase, layer)
                now = base + it * STEPS + j
                if phase == C and here(it, j, LAG.heads):
                    g = now - LAG.heads
                    jl = (j - LAG.heads) % STEPS
                    act.wait_ge(s_heads, g + 1)
                    if isinstance(it, int) and it == 0 and j == LAG.heads:
                        act.wait_ge(s_kz_zero, 2)
                    nc.scalar.activation(qt[jl % 2][:, :], heads_ps[:, 0:2 * P], ACT.Copy).then_inc(s_q_ready, 1)
                    pairs = kz[jl % 2][:, :, :].rearrange("d (a b) k -> d b a k", b=2)
                    turned_k = heads_ps[:, 2 * P:4 * P].rearrange("d (a k) -> d a k", a=2)
                    nc.scalar.activation(pairs[0:DH, 0], turned_k[0:DH], ACT.Copy).then_inc(s_k_half, 1)
                    nc.scalar.activation(pairs[DH:P, 1], turned_k[DH:P], ACT.Copy).then_inc(s_k_ready, 1)

            def square(phase, layer, it, j):
                base = start_of(phase, layer)
                now = base + it * STEPS + j
                if phase == C and here(it, j, 0):
                    g = now - 2 * GROUPS
                    act.wait_ge(s_proj, g + 1)
                    if has(it * STEPS + j - 1):
                        act.wait_ge(s_nrm2, g)
                    nc.scalar.activation(squares[:, :, :].rearrange("t h d -> t (h d)"), proj_ps[j % 2][:, :], ACT.Square).then_inc(s_sq_done, 1)

            def copy_maxima(phase, layer, it, j):
                base = start_of(phase, layer)
                now = base + it * STEPS + j
                if here(it, j, LAG.exp):
                    g = now - LAG.exp
                    act.wait_ge(s_top_turn, g + 1)
                    nc.scalar.activation(top_t[j % 2][:, :], misc_bf[0:2 * HG, 0:P], ACT.Copy).then_inc(s_top_ready, 1)

            def exponentials(phase, layer, it, j):
                base = start_of(phase, layer)
                now = base + it * STEPS + j
                if here(it, j, LAG.exp):
                    g = now - LAG.exp
                    act.wait_ge(s_shifted_scores, g + 1)
                    nc.scalar.activation(prob[j % 2][:, :, :].rearrange("q h k -> q (h k)"), score_ps[j % 2][:, :], ACT.Exp).then_inc(s_exp_done, 1)

            def copy_values(phase, layer, it, j):
                base = start_of(phase, layer)
                now = base + it * STEPS + j
                if phase != B and here(it, j, 0):
                    g = now
                    act.wait_ge(s_v_proj, g + 1)
                    width = DH if phase == C else DS
                    if isinstance(it, int) and it == 0:
                        act.wait_ge(s_vone_set, 2 * NG * (2 if phase == C else 1))
                    nc.scalar.activation(val[j][:, :, 0:width], misc_ps[:, 0:HG * width].rearrange("t (h d) -> t h d", h=HG), ACT.Copy).then_inc(s_v_ready, 1)

            def copy_probs(phase, layer, it, j):
                base = start_of(phase, layer)
                now = base + it * STEPS + j
                if here(it, j, LAG.turn):
                    g = now - LAG.turn
                    act.wait_ge(s_pturn, g + 1)
                    nc.scalar.activation(prob_t[(j + 1) % 2][:, :, :].rearrange("k h q -> k (h q)"), turn_ps[:, :], ACT.Copy).then_inc(s_pt_ready, 1)

            def copy_out(phase, layer, it, j):
                base = start_of(phase, layer)
                now = base + it * STEPS + j
                if phase != A and here(it, j, LAG.value):
                    g = now - LAG.value - GROUPS
                    act.wait_ge(s_oturn, g + 1)
                    if phase == C:
                        nc.scalar.activation(head_t[j % 2][:, :], value_ps[:, 0:2 * P], ACT.Copy).then_inc(s_ot_ready, 1)
                    else:
                        nc.scalar.activation(head_t[j % 2][0:PAD, 0:P], value_ps[0:PAD, 0:P], ACT.Copy).then_inc(s_ot_ready, 1)

            def copy_next(phase, layer, it, j):
                if j % NG == 2 and here(it, j, -NG + 2):
                    copy_input(phase, layer, it * 2 + j // NG + 1, (j // NG + 1) % 2)

            def step(phase, layer, it, j):
                if phase == C:
                    copy_heads(phase, layer, it, j)
                    square(phase, layer, it, j)
                    copy_maxima(phase, layer, it, j)
                    exponentials(phase, layer, it, j)
                    copy_values(phase, layer, it, j)
                    copy_probs(phase, layer, it, j)
                    copy_out(phase, layer, it, j)
                    copy_next(phase, layer, it, j)
                else:
                    copy_maxima(phase, layer, it, j)
                    copy_probs(phase, layer, it, j)
                    exponentials(phase, layer, it, j)
                    copy_values(phase, layer, it, j)
                    copy_out(phase, layer, it, j)
                    copy_next(phase, layer, it, j)

            def mlp_step(layer, it, j):
                q = layer * NQ + it * 2 + j
                if here_q(it, j, 2):
                    m = q - 2
                    for k in range(3):
                        n = HB[k][1]
                        act.wait_ge(s_f_gate_ps, 3 * m + k + 1)
                        if has(it * 2 + j - 4):
                            act.wait_ge(s_f_hid, 3 * m + k - 5)
                        nc.scalar.activation(gate[3 * (j % 2) + k][0:n, :], hid_ps[((j % 2) * 6 + 2 * k) % 4][0:n, :], ACT.Gelu,
                                             bias=mlp_now[0:n, 5 + k:6 + k]).then_inc(s_f_gate, 1)
                if here_q(it, j, 1):
                    m = q - 1
                    act.wait_ge(s_f_turn, m + 1)
                    if has(it * 2 + j - 3):
                        act.wait_ge(s_f_a_ps, 3 * m - 3)
                    nc.scalar.activation(normed_t[(j + 1) % 2][:, :], heads_ps[:, :], ACT.Identity, bias=mlp_now[:, 1:2],
                                         scale=mlp_now[:, 0:1]).then_inc(s_f_xt, 1)

            for phase in (A, B):
                act.wait_ge(s_added, start_of(phase, 0))
                copy_input(phase, 0, 0, 0)
                attention(act, step, phase)
            act.wait_ge(s_table_in, 16 * 11)
            with act.Fori(0, DEPTH) as layer:
                act.wait_ge(s_layer_set, layer + 1)
                act.wait_ge(s_added, start_of(C, layer))
                act.wait_ge(s_y_done, (layer + 1) * NQ)
                copy_input(C, layer, 0, 0)
                attention(act, step, C, layer)
                mlp(act, mlp_step, layer)

        @block.gpsimd
        def _(pool):
            pool.memset(m_at[:, :], 0.0).then_inc(s_zeros_set, 1)
            pool.memset(per_layer[:, :, :], 0.0).then_inc(s_zeros_set, 1)
            pool.memset(b_qk[:, :, :], 0.0).then_inc(s_zeros_set, 1)
            pool.memset(wpad[:, :, :, :, :, :], 0.0).then_inc(s_wpad_set, 1)
            pool.memset(neg_half[:, :], -0.5).then_inc(s_half_set, 1)
            for v in val:
                pool.memset(v[:, :, DS:DS + 1], 1.0).then_inc(s_vone_set, 1)
            pool.wait_ge(s_small_in, 16 * 17)
            pool.wait_ge(s_wpad_set, 1)
            for ph, w, cols in ((A, aw, (P, 0)), (B, bw, (0, P))):
                for i, c in enumerate(cols):
                    nc.gpsimd.tensor_copy(wpad[:, ph, i, :, :, 0:DS], w[:, c:c + P].rearrange("c (g h d) -> c g h d", g=NG, h=HG)).then_inc(s_wpad_set, 1)
            pool.wait_ge(s_half_set, 1)

            def rstd_of(phase, b, slot):
                pool.wait_ge(s_ln_var, phase * NB + b + 1)
                nc.gpsimd.tensor_tensor(rstd[slot][:, 0:1], var[slot][:, 0:1], neg_half[:, 0:1], ALU.pow).then_inc(s_ln_rstd, 1)

            def prepare(phase, layer, b, slot):
                if phase != C:
                    rstd_of(phase, b, slot)

            def step(phase, layer, it, j):
                if j % NG == 1 and here(it, j, -NG + 1):
                    prepare(phase, layer, it * 2 + j // NG + 1, (j // NG + 1) % 2)
                if phase != C and here(it, j, LAG.heads):
                    g = start_of(phase, 0) + it * STEPS + j - LAG.heads
                    pool.wait_ge(s_k_ready, g + 1)
                    nc.gpsimd.tensor_tensor(kz[j % 2][:, :, :], kt[j % 2][:, :].unsqueeze(1).to_broadcast([P, HG, P]),
                                            const("block").unsqueeze(2).to_broadcast([P, HG, P]), ALU.mult).then_inc(s_kz_ready, 1)
                if phase == C and here(it, j, 0):
                    g = layer * GROUPS + it * STEPS + j
                    pool.wait_ge(s_nrm2g, g + 1)
                    nc.gpsimd.tensor_tensor(rnorm[j % 2][:, :], norm2g[j % 2][:, :], neg_half[:, :], ALU.pow).then_inc(s_rn_done, 1)
                    pool.wait_ge(s_sin_done, g + 1)
                    nc.gpsimd.tensor_tensor(rotated[j % 2][:, :, :, :], by_cos[j % 2][:, :, :, :], by_sin[j % 2][:, :, :, :], ALU.add).then_inc(s_rot_done, 1)
                    pool.wait_ge(s_rot_done, g + 1)
                    pool.wait_ge(s_rn_done, g + 1)
                    if has(it * STEPS + j - 2):
                        pool.wait_ge(s_heads, 2 * GROUPS + g - 1)
                    nc.gpsimd.tensor_tensor(unit[j % 2][:, :, :, :].rearrange("t a h d -> t (a h) d"),
                                            rotated[j % 2][:, :, :, :].rearrange("t a h d -> t (a h) d"),
                                            rnorm[j % 2][:, :].unsqueeze(2).to_broadcast([P, 2 * HG, DH]), ALU.mult).then_inc(s_unit_done, 1)

            def mlp_step(layer, it, j):
                q = layer * NQ + it * 2 + j
                if here_q(it, j, 0):
                    pool.wait_ge(s_f_var, q + 1)
                    nc.gpsimd.tensor_tensor(rstd[j % 2][:, :], var[j % 2][:, :], neg_half[:, 0:QUAD], ALU.pow).then_inc(s_f_rstd, 1)

            for phase in (A, B):
                prepare(phase, 0, 0, 0)
                attention(pool, step, phase)
            with pool.Fori(0, NQ // 2) as q2:
                for j in range(2):
                    pool.wait_ge(s_y_var, q2 * 2 + j + 1)
                    nc.gpsimd.tensor_tensor(rstd[j][:, :], var[j][:, :], neg_half[:, 0:QUAD], ALU.pow).then_inc(s_y_rstd, 1)
            pool.wait_ge(s_pv, 2 * GROUPS)
            for v in val:
                pool.memset(v[:, :, DH:DH + 1], 1.0).then_inc(s_vone_set, 1)
            pool.wait_ge(s_scores, 2 * GROUPS)
            for k in kz:
                pool.memset(k[:, :, :], 0.0).then_inc(s_kz_zero, 1)
            pool.wait_ge(s_kz_zero, 2)
            for t in xt:
                pool.memset(t[DH:P, 0:1], 0.0).then_inc(s_xt_zero, 1)
            pool.wait_ge(s_xt_zero, 2)
            pool.wait_ge(s_table_in, 16 * 11)
            with pool.Fori(0, DEPTH) as layer:
                pool.wait_ge(s_added, start_of(C, layer))
                pool.wait_ge(s_y_done, (layer + 1) * NQ)
                attention(pool, step, C, layer)
                mlp(pool, mlp_step, layer)

        @block.vector
        def _(dve):
            dve.wait_ge(s_const_in, 16)
            nc.vector.tensor_copy(ident_b[:, :], ident)
            nc.vector.tensor_copy(masks_b[:, 0, :], const("causal"))
            nc.vector.tensor_copy(masks_b[:, 1, :], const("band"))
            nc.vector.tensor_copy(sel_b[:, :], const("sel", 2 * HG)).then_inc(s_cast_done, 1)
            dve.wait_ge(s_small_in, 16 * 17)
            nc.vector.tensor_scalar(m_at[:, NG:2 * NG], m_at[:, NG:2 * NG], -1.0, None, ALU.mult).then_inc(s_krow_neg, 1)
            dve.wait_ge(s_krow_neg, 1)
            for g in range(NG):
                nc.vector.tensor_scalar(krow[:, g, :], const("iota"), m_at[:, g:g + 1], m_at[:, NG + g:NG + g + 1], ALU.mult, ALU.add).then_inc(s_krow_set, 1)
            dve.wait_ge(s_krow_set, NG)
            dve.wait_ge(s_x_in, 16)

            def ln_stats(phase, b, slot):
                nb = phase * NB + b
                nc.vector.bn_stats(stats[slot][:, 0, :], seq(x, b)).then_inc(s_ln_stat, 1)
                dve.wait_ge(s_ln_stat, nb + 1)
                nc.vector.memset(scratch[:, :], 0.0)
                nc.vector.bn_aggr(mv[slot][:, 0, :], stats[slot][:, 0, :]).then_inc(s_ln_mv, 1)
                dve.wait_ge(s_ln_mv, nb + 1)
                if has(nb - 2):
                    dve.wait_ge(s_ln_rstd, nb - 1)
                nc.vector.tensor_scalar(var[slot][:, 0:1], mv[slot][:, 0, 1:2], EPS, None, ALU.add).then_inc(s_ln_var, 1)

            def prepare(layer, b, slot):
                nb = (C + layer) * NB + b
                dve.wait_ge(s_xturn, nb - 1)
                nc.vector.tensor_scalar(tok[slot][:, :], seq(y, b), 1.0, None, ALU.mult).then_inc(s_tok_ready, 1)

            def ln_apply(phase, b, slot):
                nb = phase * NB + b
                dve.wait_ge(s_ln_rstd, nb + 1)
                if has(nb - 2):
                    dve.wait_ge(s_xturn, nb - 1)
                nc.vector.tensor_scalar(tok[slot][:, :], seq(x, b), mv[slot][:, 0, 0:1], rstd[slot][:, 0:1], ALU.subtract, ALU.mult).then_inc(s_tok_ready, 1)
                if phase == B:
                    if has(b - 2):
                        dve.wait_ge(s_cturn, b - 1)
                    nc.vector.tensor_scalar(ctok[slot][:, :], seq(ctx_all, b), 1.0, None, ALU.mult).then_inc(s_ctok_ready, 1)
                    dve.wait_ge(s_tok_ready, nb + 1)
                    nc.vector.tensor_tensor(seq(x, b), seq(x, b), b_o[:, :], ALU.add).then_inc(s_bias_added, 1)

            def norms(phase, layer, it, j):
                base = start_of(phase, layer)
                now = base + it * STEPS + j
                if phase == C and here(it, j, 0):
                    g = now - 2 * GROUPS
                    dve.wait_ge(s_sq_done, g + 1)
                    nc.vector.tensor_reduce(norm2[j % 2][:, :], squares[:, :, :], AX_X, ALU.add).then_inc(s_nrm2, 1)
                    dve.wait_ge(s_nrm2, g + 1)
                    if has(it * STEPS + j - 2):
                        dve.wait_ge(s_rot_done, g - 1)
                    nc.vector.tensor_scalar(norm2g[j % 2][:, :], norm2[j % 2][:, :], 1e-24, None, ALU.max).then_inc(s_nrm2g, 1)

            def add_projected(phase, layer, it, j):
                base = start_of(phase, layer)
                now = base + it * STEPS + j
                if phase != A and here(it, j, LAG.out):
                    g = now - LAG.out
                    jl = (j - LAG.out) % STEPS
                    b = it * 2 + (j - LAG.out) // NG
                    dve.wait_ge(s_wo_done, g - GROUPS + 1)
                    dst = seq(x if phase == B else y, b)
                    if phase == B:
                        dve.wait_ge(s_bias_added, b + 1)
                    dve.wait_ge(s_added, g)
                    nc.vector.tensor_tensor(dst, dst, turn_ps[:, 0:P], ALU.add).then_inc(s_added, 1)

            def rotary_products(phase, layer, it, j):
                base = start_of(phase, layer)
                now = base + it * STEPS + j
                if phase == C and here(it, j, 0):
                    g = now - 2 * GROUPS
                    tab = lambda t: t[:, bass.ds(layer * 2 * DH, 2 * DH)].rearrange("t (a d) -> t a d", a=2)
                    got = proj_ps[j % 2][:, :].rearrange("t (a h d) -> t a h d", a=2, h=HG)
                    nc.vector.tensor_tensor(by_cos[j % 2][:, :, :, :], got, tab(rot_cos).unsqueeze(2).to_broadcast([P, 2, HG, DH]), ALU.mult).then_inc(s_cos_done, 1)
                    nc.vector.tensor_tensor(by_sin[j % 2][:, :, :, 0:HALF], got[:, :, :, HALF:DH],
                                            tab(rot_sin)[:, :, 0:HALF].unsqueeze(2).to_broadcast([P, 2, HG, HALF]), ALU.mult)
                    nc.vector.tensor_tensor(by_sin[j % 2][:, :, :, HALF:DH], got[:, :, :, 0:HALF],
                                            tab(rot_sin)[:, :, HALF:DH].unsqueeze(2).to_broadcast([P, 2, HG, HALF]), ALU.mult).then_inc(s_sin_done, 1)

            def divide(phase, layer, it, j):
                base = start_of(phase, layer)
                now = base + it * STEPS + j
                if here(it, j, LAG.value):
                    g = now - LAG.value
                    jl = (j - LAG.value) % STEPS
                    width = DH if phase == C else DS
                    got = value_ps[:, 0:HG * (DH + 1)].rearrange("t (h d) -> t h d", h=HG)
                    dve.wait_ge(s_pv, g + 1)
                    nc.vector.reciprocal(rsum[j % 2][:, :].unsqueeze(2), got[:, :, width:width + 1]).then_inc(s_rsum_done, 1)
                    dve.wait_ge(s_rsum_done, g + 1)
                    if phase == C:
                        dst = head_out[j % 2][:, :, :]
                    else:
                        dst = head_out[j % 2][:, 0, 0:PAD].rearrange("t (h d) -> t h d", h=HG)
                    if phase == A and has(it * STEPS + j - LAG.value - 2):
                        dve.wait_ge(s_added, g - 1)
                    nc.vector.tensor_tensor(dst, got[:, :, 0:width], rsum[j % 2][:, :].unsqueeze(2).to_broadcast([P, HG, width]), ALU.mult).then_inc(s_out_ready, 1)

            def copy_heads(phase, layer, it, j):
                base = start_of(phase, layer)
                now = base + it * STEPS + j
                if phase != C and here(it, j, LAG.heads):
                    g = now - LAG.heads
                    jl = (j - LAG.heads) % STEPS
                    dve.wait_ge(s_heads, g + 1)
                    if phase == A:
                        nc.vector.scalar_tensor_tensor(out=qt[j % 2][:, 0:P], in0=heads_ps[:, 0:P], scalar=float(P) ** -0.5, in1=const("qrow"), op0=ALU.mult, op1=ALU.add).then_inc(s_q_ready, 1)
                        nc.vector.tensor_tensor(kt[j % 2][:, :], heads_ps[:, P:2 * P], krow[:, jl % NG, :], ALU.add).then_inc(s_k_ready, 1)
                    else:
                        nc.vector.tensor_scalar(qt[j % 2][:, 0:P], heads_ps[:, 0:P], b_qk[:, 0, jl % NG:jl % NG + 1], float(DS) ** -0.5, ALU.add, ALU.mult).then_inc(s_q_ready, 1)
                        nc.vector.tensor_scalar(kt[j % 2][:, :], heads_ps[:, P:2 * P], b_qk[:, 1, jl % NG:jl % NG + 1], None, ALU.add).then_inc(s_k_ready, 1)

            def copy_values(phase, layer, it, j):
                base = start_of(phase, layer)
                now = base + it * STEPS + j
                if phase == B and here(it, j, 0):
                    g = now
                    dve.wait_ge(s_v_proj, g + 1)
                    dve.wait_ge(s_vone_set, 2 * NG)
                    if has(it * STEPS + j - 2 * NG):
                        dve.wait_ge(s_pv, g + 1 - 2 * NG)
                    at = slice((j % NG) * PAD, (j % NG + 1) * PAD)
                    nc.vector.tensor_tensor(val[j][:, :, 0:DS], misc_ps[:, 0:PAD].rearrange("t (h d) -> t h d", h=HG),
                                            b_v[:, at].rearrange("t (h d) -> t h d", h=HG), ALU.add).then_inc(s_v_ready, 1)

            def next_sequence(phase, layer, it, j):
                if phase != C and j % NG == 0 and here(it, j, -NG):
                    ln_stats(phase, it * 2 + j // NG + 1, (j // NG + 1) % 2)
                if phase != C and j % NG == 1 and here(it, j, -NG + 1):
                    ln_apply(phase, it * 2 + j // NG + 1, (j // NG + 1) % 2)
                if phase == C and j % NG == 1 and here(it, j, -NG + 1):
                    prepare(layer, it * 2 + j // NG + 1, (j // NG + 1) % 2)

            def maxima(phase, layer, it, j):
                base = start_of(phase, layer)
                now = base + it * STEPS + j
                if here(it, j, LAG.scores):
                    g = now - LAG.scores
                    jl = (j - LAG.scores) % STEPS
                    dve.wait_ge(s_scores, g + 1)
                    nc.vector.tensor_reduce(top[jl % 2][:, :], score_ps[jl % 2][:, :].rearrange("q (h k) -> q h k", h=HG), AX_X, ALU.max, negate=True).then_inc(s_top_done, 1)
                    dve.wait_ge(s_top_done, g + 1)
                    nc.vector.tensor_copy(top_b[jl % 2][:, 0:HG], top[jl % 2][:, :]).then_inc(s_top_hi, 1)
                    dve.wait_ge(s_top_hi, g + 1)
                    nc.vector.tensor_tensor(top_b[jl % 2][:, HG:2 * HG], top[jl % 2][:, :], top_b[jl % 2][:, 0:HG], ALU.subtract).then_inc(s_top_lo, 1)

            def add_direct(phase, layer, it, j):
                base = start_of(phase, layer)
                now = base + it * STEPS + j
                if phase == A and here(it, j, LAG.value):
                    g = now - LAG.value
                    jl = (j - LAG.value) % STEPS
                    b = it * 2 + (j - LAG.value) // NG
                    dve.wait_ge(s_out_ready, g + 1)
                    at = bass.ds(b * P + (jl % NG) * PAD, PAD)
                    nc.vector.tensor_tensor(x[:, at], x[:, at], head_out[j % 2][:, 0, 0:PAD], ALU.add).then_inc(s_added, 1)

            def step(phase, layer, it, j):
                if phase == C:
                    add_projected(phase, layer, it, j)
                    norms(phase, layer, it, j)
                    divide(phase, layer, it, j)
                    rotary_products(phase, layer, it, j)
                    next_sequence(phase, layer, it, j)
                    maxima(phase, layer, it, j)
                else:
                    add_projected(phase, layer, it, j)
                    copy_heads(phase, layer, it, j)
                    divide(phase, layer, it, j)
                    copy_values(phase, layer, it, j)
                    next_sequence(phase, layer, it, j)
                    maxima(phase, layer, it, j)
                    add_direct(phase, layer, it, j)

            def mlp_step(layer, it, j):
                q = layer * NQ + it * 2 + j
                if here_q(it, j, 2):
                    m = q - 2
                    for k in range(3):
                        n = HB[k][1]
                        dve.wait_ge(s_f_a_ps, 3 * m + k + 1)
                        dve.wait_ge(s_f_gate, 3 * m + k + 1)
                        if has(it * 2 + j - 4):
                            dve.wait_ge(s_f_w2, m - 1)
                        nc.vector.scalar_tensor_tensor(out=hidden[3 * (j % 2) + k][0:n, :], in0=hid_ps[((j % 2) * 6 + 2 * k + 1) % 4][0:n, :],
                                                       scalar=mlp_now[0:n, 2 + k:3 + k], in1=gate[3 * (j % 2) + k][0:n, :],
                                                       op0=ALU.add, op1=ALU.mult).then_inc(s_f_hid, 1)
                if here_q(it, j, 0):
                    dve.wait_ge(s_f_shift, q + 1)
                    if has(it * 2 + j - 2):
                        dve.wait_ge(s_f_norm, 4 * q - 4)
                    ys = seq(y, (it * 2 + j) * QUAD, QUAD).rearrange("t (b c) -> t b c", b=QUAD)
                    nc.vector.tensor_scalar(shifted[j % 2][:, :, 0:DH], ys[:, :, 0:DH], 1.0, None, ALU.mult).then_inc(s_f_left, 1)
                    nc.vector.tensor_copy(shifted[j % 2][:, :, DH:P], turn_ps[:, 0:QUAD * DH].rearrange("t (b c) -> t b c", b=QUAD)).then_inc(s_f_right, 1)
                    dve.wait_ge(s_f_right, q + 1)
                    dve.wait_ge(s_f_left, q + 1)
                    for b in range(QUAD):
                        nc.vector.bn_stats(stats[j % 2][:, b, :], shifted[j % 2][:, b, :]).then_inc(s_f_stat, 1)
                    dve.wait_ge(s_f_stat, QUAD * (q + 1))
                    nc.vector.memset(scratch[:, :], 0.0)
                    for b in range(QUAD):
                        nc.vector.bn_aggr(mv[j % 2][:, b, :], stats[j % 2][:, b, :]).then_inc(s_f_mv, 1)
                    dve.wait_ge(s_f_mv, QUAD * (q + 1))
                    nc.vector.tensor_scalar(var[j % 2][:, :].unsqueeze(2), mv[j % 2][:, :, 1:2], EPS, None, ALU.add).then_inc(s_f_var, 1)
                    dve.wait_ge(s_f_rstd, q + 1)
                    if has(it * 2 + j - 2):
                        dve.wait_ge(s_f_turn, q - 1)
                    for b in range(QUAD):
                        nc.vector.tensor_scalar(normed[j % 2][:, b, :], shifted[j % 2][:, b, :], mv[j % 2][:, b, 0:1], rstd[j % 2][:, b:b + 1], ALU.subtract, ALU.mult).then_inc(s_f_norm, 1)
                if here_q(it, j, 3):
                    m = q - 3
                    dve.wait_ge(s_f_w2, m + 1)
                    at = (it * 2 + j - 3) * QUAD
                    dst = seq(y, at, QUAD)
                    nc.vector.tensor_tensor(dst, dst, value_ps[:, :], ALU.add).then_inc(s_f_b2, 1)
                    dve.wait_ge(s_f_b2, m + 1)
                    dst = dst.rearrange("t (b c) -> t b c", b=QUAD)
                    nc.vector.tensor_tensor(dst, dst, b2_sb[:, bass.ds(layer * P, P)].unsqueeze(1).to_broadcast([P, QUAD, P]), ALU.add).then_inc(s_y_done, 1)

            for phase in (A, B):
                if phase == B:
                    dve.wait_ge(s_ctx_in, 16)
                dve.wait_ge(s_added, start_of(phase, 0))
                ln_stats(phase, 0, 0)
                ln_apply(phase, 0, 0)
                attention(dve, step, phase)
            dve.wait_ge(s_added, 2 * GROUPS)
            with dve.Fori(0, NQ // 2) as q2:
                for j in range(2):
                    q = q2 * 2 + j
                    for b in range(QUAD):
                        nc.vector.bn_stats(stats[j][:, b, :], seq(x, q * QUAD + b)).then_inc(s_y_stat, 1)
                    dve.wait_ge(s_y_stat, QUAD * (q + 1))
                    nc.vector.memset(scratch[:, :], 0.0)
                    for b in range(QUAD):
                        nc.vector.bn_aggr(mv[j][:, b, :], stats[j][:, b, :]).then_inc(s_y_mv, 1)
                    dve.wait_ge(s_y_mv, QUAD * (q + 1))
                    nc.vector.tensor_scalar(var[j][:, :].unsqueeze(2), mv[j][:, :, 1:2], EPS, None, ALU.add).then_inc(s_y_var, 1)
                    dve.wait_ge(s_y_rstd, q + 1)
                    for b in range(QUAD):
                        last = nc.vector.tensor_scalar(seq(y, q * QUAD + b), seq(x, q * QUAD + b), mv[j][:, b, 0:1], rstd[j][:, b:b + 1], ALU.subtract, ALU.mult)
                    last.then_inc(s_y_done, 1)
            dve.wait_ge(s_table_in, 16 * 11)
            scales = qk_scale[:, :, :, :]
            for dst, src, at, frm in ((rot_cos, "cos", slice(0, DH), slice(0, DH)), (rot_sin, "sin", slice(0, HALF), slice(HALF, DH)),
                                      (rot_sin, "sin", slice(HALF, DH), slice(0, HALF))):
                for l in range(DEPTH):
                    nc.vector.tensor_tensor(dst[:, l * 2 * DH:(l + 1) * 2 * DH].rearrange("t (a d) -> t a d", a=2)[:, :, at],
                                            const(src).rearrange("t (a d) -> t a d", a=2)[:, :, at],
                                            scales[:, l, :, frm], ALU.mult).then_inc(s_tables_set, 1)
            dve.wait_ge(s_tables_set, 3 * DEPTH)
            with dve.Fori(0, DEPTH) as layer:
                dve.wait_ge(s_added, start_of(C, layer))
                dve.wait_ge(s_y_done, (layer + 1) * NQ)
                nc.vector.tensor_scalar(mlp_now[:, :], per_layer[:, :, :].rearrange("p l n -> p (l n)")[:, bass.ds(layer * 8, 8)],
                                        1.0, None, ALU.mult).then_inc(s_layer_set, 1)
                prepare(layer, 0, 0)
                attention(dve, step, C, layer)
                mlp(dve, mlp_step, layer)
            dve.wait_ge(s_y_done, (DEPTH + 1) * NQ)
            for q in range(NQ):
                dst = y[:, q * QUAD * P:(q + 1) * QUAD * P]
                nc.vector.tensor_tensor(dst, dst, x[:, q * QUAD * P:(q + 1) * QUAD * P], ALU.add).then_inc(s_sum_done, 1)


_INS = ["x", "ctx_1024", "L0_attn_W_kqv", "L0_attn_m", "L0_xattn_w_q", "L0_xattn_b_q", "L0_xattn_w_k", "L0_xattn_b_k",
        "L0_xattn_w_v", "L0_xattn_b_v", "L0_xattn_w_o", "L0_xattn_b_o", "L0_ffn_Wqkv", "L0_ffn_q_scale", "L0_ffn_k_scale",
        "L0_ffn_Wo", "L0_ffn_ln_g", "L0_ffn_ln_b", "L0_ffn_W1", "L0_ffn_b1", "L0_ffn_W2", "L0_ffn_b2"]


def kernel(**inputs):
    import numpy as _np
    import concourse.bacc as _bacc
    from concourse import mybir as _mybir
    from concourse.bass_utils import run_bass_kernel_spmd as _run

    nc = _bacc.Bacc("TRN2", target_bir_lowering=False, num_devices=1)
    arrays, args = {}, []
    for name in _INS + ["constants"]:
        a = constants() if name == "constants" else _np.asarray(inputs[name])
        if name.startswith("L0_xattn_w_"):
            a = a.T
        a = _np.ascontiguousarray(a)
        arrays[f"in_{name}_dram"] = a
        args.append(nc.dram_tensor(f"in_{name}_dram", a.shape, _mybir.dt.from_np(a.dtype), kind="ExternalInput").ap())
    args.append(nc.dram_tensor("out_0_dram", (NB, P, P), F32, kind="ExternalOutput").ap())
    build(nc, *args)
    r = _run(nc, [arrays], core_ids=[0])
    return r.results[0]["out_0_dram"]
```

```python
from contextlib import ExitStack

import numpy as np

import concourse.bass as bass
from concourse import mybir

F32 = mybir.dt.float32
BF16 = mybir.dt.bfloat16
F32R = mybir.dt.float32r
ALU = mybir.AluOpType
ACT = mybir.ActivationFunctionType
AX_X = mybir.AxisListType.X

P = 128
NB = 32
NH = 16
HG = 4
NG = NH // HG
GROUPS = NB * NG
DEPTH = 6
DH = 64
HALF = DH // 2
INNER = NH * DH
DS = P // NH
PAD = 32
PARTS = 3
POS = PARTS * DS
WINDOW = 32
HID = 341
HB = [(0, 128), (128, 128), (256, 85)]
QUAD = 4
NQ = NB // QUAD
EPS = 1e-5
MASKED = -1e30
A, B, C = 0, 1, 2

STEPS = 2 * NG


class LAG:
    heads = 2
    scores = 3
    exp = 4
    turn = 5
    value = 6
    out = 7


DRAIN = 7
MLP_EARLY = (4, 5)

COLS = {}
_at = 0
for _name, _n in (("ident", P), ("shift", P), ("iota", P), ("qrow", P), ("split", 8), ("block", HG), ("cos", 2 * DH),
                  ("sin", 2 * DH), ("causal", P), ("band", P)):
    COLS[_name] = (_at, _n)
    _at += _n
NCONST = _at


def constants():
    t = np.zeros((P, NCONST), np.float32)

    def put(name, v):
        a, n = COLS[name]
        t[:v.shape[0], a:a + n] = v.reshape(v.shape[0], n)

    i = np.arange(P)
    put("ident", np.eye(P, dtype=np.float32))
    put("shift", np.eye(P, k=1, dtype=np.float32))
    put("iota", np.tile(i.astype(np.float32), (P, 1)))
    qrow = np.zeros((P, P), np.float32)
    for r in range(2):
        qrow[POS + r::PAD] = 1.0
        qrow[POS + 2 + r::PAD] = i
    put("qrow", qrow)
    put("block", (i[:, None] // PAD == np.arange(HG)[None]).astype(np.float32))
    upper, rest, none = (1.0, 0.0), (-1.0, 1.0), (0.0, 0.0)
    for_q = [upper] * (2 * DS) + [rest] * DS + [none] * (PAD - POS)
    for_k = [upper] * DS + [rest] * DS + [upper] * DS + [upper, rest] * 2 + [none] * (PAD - POS - 4)
    columns = [np.tile(np.array(rows), (HG, 1)) * s for s in (float(P) ** -0.5, 1.0, float(DS) ** -0.5, 1.0)
               for rows in ((for_q if s != 1.0 else for_k),)]
    put("split", np.concatenate(columns, 1))
    half = np.arange(0, DH, 2, dtype=np.float32)
    inv_freq = (np.float32(1.0) / np.float32(10000.0) ** (half / np.float32(DH))).astype(np.float32)
    pos = i.astype(np.float32)
    freqs = pos[:, None] * inv_freq[None]
    base = (half + np.float32(0.4 * DH)) / np.float32(1.4 * DH)
    power = (pos - P // 2) / np.float32(WINDOW // 2)
    scale = (base[None] ** power[:, None]).astype(np.float32)
    cos, sin = np.cos(freqs), np.sin(freqs)
    both = lambda q, k: np.stack([8.0 * q, k], 1)
    inv = np.float32(1.0) / scale
    put("cos", both(np.concatenate([cos * scale] * 2, -1), np.concatenate([cos * inv] * 2, -1)))
    put("sin", both(np.concatenate([-sin * scale, sin * scale], -1), np.concatenate([-sin * inv, sin * inv], -1)))
    ahead = i[:, None] - i[None]
    put("causal", np.where(ahead >= 0, 0.0, MASKED))
    put("band", np.where((ahead >= 0) & (ahead <= WINDOW), 0.0, MASKED))
    return t


def has(index):
    return not isinstance(index, int) or index >= 0


def in_range(it, j, lag, n):
    return not isinstance(it, int) or 0 <= it * n[1] + j - lag < n[0]


def build(nc, x_in, ctx_in, a_w, a_m, b_wq, b_bq, b_wk, b_bk, b_wv, b_bv, b_wo, b_bo, wqkv, q_scale, k_scale,
          wo, ln_g, ln_b, w1, b1, w2, b2, const_d, out):
    with ExitStack() as stack:
        def sb(name, shape, dt=F32):
            return stack.enter_context(nc.sbuf_tensor(name, shape, dt))

        def ring(name, n, shape, dt=F32):
            return [sb(f"{name}{i}", shape, dt) for i in range(n)]

        x = sb("x", [P, NB * P])
        y = sb("y", [P, NB * P])
        ctx_all = sb("ctx_all", [P, NB * P])
        cst = sb("cst", [P, NCONST])
        ident = cst[:, 0:P]
        ident_b = sb("ident_b", [P, P], BF16)
        masks_b = sb("masks_b", [P, 2, P], BF16)
        neg_half = sb("neg_half", [P, 2 * HG])
        one = sb("one", [P, 1])
        stage = sb("stage", [P, 4 * P])
        aw = sb("aw", [P, 3 * P])
        bw = sb("bw", [P, 3 * P])
        wpad = sb("wpad", [P, 2, 2, NG, HG, PAD])
        bwo = sb("bwo", [PAD, NG, P])
        m_at = sb("m_at", [P, 2 * NG])
        krow_raw, krow_upper = (y[:, i * NG * P:(i + 1) * NG * P].rearrange("d (g k) -> d g k", g=NG) for i in (0, 1))
        krow_upper = krow_upper.bitcast(F32R)
        krow = sb("krow", [P, NG, P], F32R)
        b_qk = sb("b_qk", [P, 2, NG])
        b_v = sb("b_v", [P, P])
        b_o = sb("b_o", [P, P])
        wqkv_sb = sb("wqkv_sb", [P, 3 * INNER])
        wqkv_high = sb("wqkv_high", [P, 3, INNER], F32R)
        wqkv_low = sb("wqkv_low", [P, 3, INNER], F32R)
        wo_sb = sb("wo_sb", [P, INNER])
        w1_sb = sb("w1_sb", [P, 2 * HID])
        w1_high = sb("w1_high", [P, 2 * HID], F32R)
        w1_low = sb("w1_low", [P, 2 * HID], F32R)
        w2_sb = sb("w2_sb", [P, 3 * P])
        qk_scale = sb("qk_scale", [P, DEPTH, 2, DH])
        rot_cos = sb("rot_cos", [P, DEPTH * 2 * DH])
        rot_sin = sb("rot_sin", [P, DEPTH * 2 * DH])
        per_layer = sb("per_layer", [P, DEPTH, 8])
        mlp_now = sb("mlp_now", [P, 8])
        b2_sb = sb("b2_sb", [P, DEPTH * P])
        tok = ring("tok", 2, [P, P])
        xt = ring("xt", 2, [P, P])
        xt_high = ring("xt_high", 2, [P, P], F32R)
        xt_low = ring("xt_low", 2, [P, P], F32R)
        ct = ring("ct", 2, [P, P])
        ctok = ring("ctok", 2, [P, P])
        squares = sb("squares", [P, 2 * HG, DH])
        norm2 = ring("norm2", 2, [P, 2 * HG])
        norm2g = ring("norm2g", 2, [P, 2 * HG])
        rnorm = ring("rnorm", 2, [P, 2 * HG])
        by_cos = ring("by_cos", 2, [P, 2, HG, DH])
        by_sin = ring("by_sin", 2, [P, 2, HG, DH])
        qk_raw = [b[:, :, :, :].rearrange("t a h d -> t a (h d)")[:, :, 0:P] for b in by_cos]
        qk_upper = [b[:, :, :, :].rearrange("t a h d -> t a (h d)")[:, :, 0:P].bitcast(F32R) for b in by_sin]
        rotated = ring("rotated", 2, [P, 2, HG, DH])
        unit = ring("unit", 2, [P, 2, HG, DH])
        qt = ring("qt", 2, [P, 2 * P])
        qk_parts = ring("qk_parts", 2, [P, 2, P], F32R)
        kz_parts = ring("kz_parts", 2, [P, HG, P], F32R)
        kz = ring("kz", 2, [P, HG, P])
        val = ring("val", 2 * NG, [P, HG, DH])
        top = ring("top", 2, [P, HG])
        prob = ring("prob", 2, [P, HG, P])
        prob_t = ring("prob_t", 2, [P, HG, P])
        psum_raw = ring("psum_raw", 2, [P, HG])
        rsum = ring("rsum", 2, [P, HG])
        head_out = ring("head_out", 2, [P, 1, PAD])
        head_t = ring("head_t", 2, [P, 2 * P])
        stats = ring("stats", 2, [P, QUAD, 6])
        mv = ring("mv", 2, [P, QUAD, 2])
        scratch = sb("scratch", [P, 1])
        var = ring("var", 2, [P, QUAD])
        rstd = ring("rstd", 2, [P, QUAD])
        shifted = ring("shifted", 2, [P, QUAD, P])
        normed = ring("normed", 2, [P, QUAD, P])
        flat = lambda b: b[:, :, :, :].rearrange("t a h d -> t (a h d)")
        normed_t = [flat(b) for b in unit]
        normed_high = ring("normed_high", 2, [P, QUAD * P], F32R)
        normed_low = ring("normed_low", 2, [P, QUAD * P], F32R)
        gate = [ctx_all[:, i * QUAD * P:(i + 1) * QUAD * P] for i in range(6)]
        hidden = [flat(b) for b in by_cos + by_sin + rotated]

        bank = [stack.enter_context(nc.psum_tensor(f"bank{i}", [P, 512], F32)) for i in range(8)]
        proj_ps = bank[0:2]
        misc_ps = bank[2]
        heads_ps = bank[3]
        score_ps = bank[4:6]
        turn_ps = bank[6]
        value_ps = bank[7]
        small_value_ps = (bank[7], bank[0])
        small_out_ps = bank[1]
        out_ps = (bank[7], bank[6])
        hid_ps = [bank[0], bank[1], bank[4], bank[5]]

        def sem(name):
            return stack.enter_context(nc.semaphore(name))

        s_const_in = sem("const_in")
        s_x_in = sem("x_in")
        s_ctx_in = sem("ctx_in")
        s_small_in = sem("small_in")
        s_table_in = sem("table_in")
        s_wqkv_in = sem("wqkv_in")
        s_wo_in = sem("wo_in")
        s_w1_in = sem("w1_in")
        s_w2_in = sem("w2_in")
        s_out_done = sem("out_done")
        s_zeros_set = sem("zeros_set")
        s_cast_done = sem("cast_done")
        s_wpad_set = sem("wpad_set")
        s_krow_set = sem("krow_set")
        s_krow_upper = sem("krow_upper_set")
        s_krow_split = sem("krow_split")
        s_kz_ready = sem("kz_ready")
        s_bias_in = sem("bias_in")
        s_qk_raw = sem("qk_raw_ready")
        s_qk_upper = sem("qk_upper_ready")
        s_krow_neg = sem("krow_neg")
        s_tables_set = sem("tables_set")
        s_vone_set = sem("vone_set")
        s_half_set = sem("half_set")
        s_kz_zero = sem("kz_zero")
        s_xt_zero = sem("xt_zero")
        s_ln_stat = sem("ln_stat")
        s_ln_mv = sem("ln_mv")
        s_ln_var = sem("ln_var")
        s_ln_rstd = sem("ln_rstd")
        s_tok_ready = sem("tok_ready")
        s_xturn = sem("xturn")
        s_xt_ready = sem("xt_ready")
        s_xt_high = sem("xt_high_ready")
        s_xt_split = sem("xt_split")
        s_w_high = sem("w_high")
        s_w_split = sem("w_split")
        s_cturn = sem("cturn")
        s_ct_ready = sem("ct_ready")
        s_ctok_ready = sem("ctok_ready")
        s_proj = sem("proj")
        s_sq_done = sem("sq_done")
        s_nrm2 = sem("nrm2")
        s_nrm2g = sem("nrm2g")
        s_rn_done = sem("rn_done")
        s_cos_done = sem("cos_done")
        s_sin_done = sem("sin_done")
        s_rot_done = sem("rot_done")
        s_unit_done = sem("unit_done")
        s_heads = sem("heads")
        s_q_ready = sem("q_ready")
        s_k_half = sem("k_half")
        s_k_ready = sem("k_ready")
        s_v_proj = sem("v_proj")
        s_v_ready = sem("v_ready")
        s_scores = sem("scores")
        s_top_done = sem("top_done")
        s_exp_done = sem("exp_done")
        s_scaled = sem("scaled")
        s_pturn = sem("pturn")
        s_pt_ready = sem("pt_ready")
        s_pv = sem("pv")
        s_rsum_done = sem("rsum_done")
        s_out_ready = sem("out_ready")
        s_oturn = sem("oturn")
        s_ot_ready = sem("ot_ready")
        s_wo_done = sem("wo_done")
        s_added = sem("added")
        s_bias_added = sem("bias_added")
        s_f_shift = sem("f_shift")
        s_f_left = sem("f_left")
        s_f_right = sem("f_right")
        s_f_stat = sem("f_stat")
        s_f_mv = sem("f_mv")
        s_f_var = sem("f_var")
        s_f_rstd = sem("f_rstd")
        s_f_norm = sem("f_norm")
        s_f_b2 = sem("f_b2")
        s_f_turn = sem("f_turn")
        s_f_xt = sem("f_xt")
        s_f_low = sem("f_low")
        s_w1_high = sem("w1_high_set")
        s_w1_split = sem("w1_split")
        s_f_gate_ps = sem("f_gate_ps")
        s_f_a_ps = sem("f_a_ps")
        s_f_gate = sem("f_gate")
        s_f_hid = sem("f_hid")
        s_f_w2 = sem("f_w2")
        s_y_done = sem("y_done")
        s_layer_set = sem("layer_set")
        s_y_stat = sem("y_stat")
        s_y_mv = sem("y_mv")
        s_y_var = sem("y_var")
        s_y_rstd = sem("y_rstd")
        s_sum_done = sem("sum_done")

        def const(name, rows=P):
            a, n = COLS[name]
            return cst[0:rows, a:a + n]

        def seq(t, b, n=1):
            return t[:, bass.ds(b * P, n * P)]

        def start_of(phase, layer):
            return phase * GROUPS + layer * GROUPS

        def attention(eng, step, phase, layer=0, mlp_step=None):
            bodies = GROUPS // STEPS
            for j in range(STEPS):
                step(phase, layer, 0, j)
            with eng.Fori(1, bodies - 1) as it:
                for j in range(STEPS):
                    step(phase, layer, it, j)
            for j in range(STEPS):
                step(phase, layer, bodies - 1, j)
            for j in range(DRAIN):
                step(phase, layer, bodies, j)
                if phase == C and j in MLP_EARLY:
                    mlp_step(layer, 0, MLP_EARLY.index(j))

        def mlp(eng, step, layer):
            for j in range(2):
                step(layer, 1, j)
            with eng.Fori(2, NQ // 2) as it:
                for j in range(2):
                    step(layer, it, j)
            for j in range(4):
                step(layer, NQ // 2 + j // 2, j % 2)

        def here(it, j, lag):
            return in_range(it, j, lag, (GROUPS, STEPS))

        def here_q(it, j, lag):
            return in_range(it, j, lag, (NQ, 2))

        def issued(it, j, lag, after):
            if not isinstance(it, int):
                return it * STEPS + j - lag + after
            return max(0, min(GROUPS, it * STEPS + j - lag + after))

        def next_turn(phase):
            return 3 if phase == C else 2

        def turned(it, j, after):
            done = 1 + j // NG + (1 if j % NG > 2 or (j % NG == 2 and after) else 0)
            if not isinstance(it, int):
                return it * 2 + done
            return min(NB, it * 2 + done)

        block = stack.enter_context(nc.Block())

        @block.sync
        def _(sp):
            sp.dma_start(cst[:, :], const_d).then_inc(s_const_in, 16)
            sp.dma_start(x[:, :].rearrange("t (b c) -> t b c", c=P), x_in.rearrange("b t c -> t b c")).then_inc(s_x_in, 16)
            sp.dma_start(aw[:, :], a_w).then_inc(s_small_in, 16)
            sp.dma_start(bw[:, 0:P], b_wq).then_inc(s_small_in, 16)
            sp.dma_start(bw[:, P:2 * P], b_wk).then_inc(s_small_in, 16)
            sp.dma_start(bw[:, 2 * P:3 * P], b_wv).then_inc(s_small_in, 16)
            sp.dma_start(bwo[:, :, :], b_wo.rearrange("(g r) c -> r g c", r=PAD)).then_inc(s_small_in, 16)
            sp.dma_start(b_v[:, :], b_bv.partition_broadcast(P)).then_inc(s_small_in, 16)
            sp.dma_start(b_o[:, :], b_bo.partition_broadcast(P)).then_inc(s_small_in, 16)
            sp.wait_ge(s_zeros_set, 3)
            with nc.allow_non_contiguous_dma("small loads"):
                for r in range(4):
                    sp.dma_start(m_at[POS + r::PAD, (r // 2) * NG:(r // 2 + 1) * NG],
                                 a_m.rearrange("(g h) a b -> h (g a b)", h=HG)).then_inc(s_small_in, 16)
                sp.dma_start(ctx_all[:, :].rearrange("t (b c) -> t b c", c=P), ctx_in.rearrange("b t c -> t b c")).then_inc(s_ctx_in, 16)
                for i, v in enumerate((b_bq, b_bk)):
                    for h in range(HG):
                        for r in range(PARTS):
                            sp.dma_start(b_qk[PAD * h + r * DS:PAD * h + (r + 1) * DS, i, :],
                                         v.rearrange("(g h d) -> h d g", h=HG, d=DS)[h]).then_inc(s_bias_in, 16)
                for i, v in enumerate((q_scale, k_scale)):
                    sp.dma_start(qk_scale[:, :, i, :], v.partition_broadcast(P)).then_inc(s_table_in, 16)
                sp.dma_start(per_layer[:, :, 0], ln_g.rearrange("l c -> c l")).then_inc(s_table_in, 16)
                sp.dma_start(per_layer[:, :, 1], ln_b.rearrange("l c -> c l")).then_inc(s_table_in, 16)
                sp.dma_start(b2_sb[:, :].rearrange("p (l c) -> p l c", c=P), b2.partition_broadcast(P)).then_inc(s_table_in, 16)
                for i in range(2):
                    for k, (a, n) in enumerate(HB):
                        sp.dma_start(per_layer[0:n, :, 2 + 3 * i + k],
                                     b1[:, i * HID + a:i * HID + a + n].rearrange("l p -> p l")).then_inc(s_table_in, 16)
            for l in range(DEPTH):
                if l:
                    sp.wait_ge(s_v_proj, start_of(C, l))
                sp.dma_start(wqkv_sb[:, :], wqkv[l]).then_inc(s_wqkv_in, 16)
                if l:
                    sp.wait_ge(s_wo_done, start_of(C, l) - GROUPS)
                sp.dma_start(wo_sb[:, :].rearrange("p (k c) -> p k c", c=P), wo[l].rearrange("(k p) c -> p k c", p=P)).then_inc(s_wo_in, 16)
                if l:
                    sp.wait_ge(s_f_a_ps, 3 * NQ * l)
                    sp.wait_ge(s_f_w2, NQ * l)
                sp.dma_start(w1_sb[:, :], w1[l]).then_inc(s_w1_in, 16)
                for k, (a, n) in enumerate(HB):
                    sp.dma_start(w2_sb[0:n, k * P:(k + 1) * P], w2[l, a:a + n]).then_inc(s_w2_in, 16)
            for q in range(NQ):
                sp.wait_ge(s_sum_done, q + 1)
                sp.dma_start(out[q * QUAD:(q + 1) * QUAD].rearrange("b t c -> t b c"),
                             y[:, q * QUAD * P:(q + 1) * QUAD * P].rearrange("t (b c) -> t b c", c=P)).then_inc(s_out_done, 16)
            sp.wait_ge(s_out_done, 16 * NQ)

        @block.tensor
        def _(pe):
            pe.wait_ge(s_const_in, 16)
            pe.wait_ge(s_cast_done, 1)

            def turn_input(phase, layer, b, slot):
                nb = (phase + layer) * NB + b
                pe.wait_ge(s_tok_ready, nb + 1)
                nc.tensor.transpose(misc_ps[:, 0:P], tok[slot][:, :], ident).then_inc(s_xturn, 1)
                if phase == B:
                    pe.wait_ge(s_ctok_ready, b + 1)
                    nc.tensor.transpose(misc_ps[:, P:2 * P], ctok[slot][:, :], ident).then_inc(s_cturn, 1)

            def turn_heads(phase, layer, it, j):
                base = start_of(phase, layer)
                now = base + it * STEPS + j
                nseq = (phase + layer) * NB
                if here(it, j, LAG.heads):
                    g = now - LAG.heads
                    jl = (j - LAG.heads) % STEPS
                    if phase == C:
                        pe.wait_ge(s_unit_done, g - 2 * GROUPS + 1)
                        if has(it * STEPS + j - LAG.heads - 1):
                            pe.wait_ge(s_k_ready, g)
                        flat = unit[jl % 2][:, :, :, :].rearrange("t a h d -> t (a h d)")
                        for k in range(4):
                            last = nc.tensor.transpose(heads_ps[:, k * P:(k + 1) * P], flat[:, k * P:(k + 1) * P], ident)
                    else:
                        if j % NG == LAG.heads:
                            nth = it * 2 + j // NG + 1
                            pe.wait_ge(s_xt_ready, nseq + nth)
                            if phase == B:
                                pe.wait_ge(s_ct_ready, nth)
                        if isinstance(it, int) and it == 0 and j == LAG.heads:
                            pe.wait_ge(s_wpad_set, 5)
                        if has(it * STEPS + j - LAG.heads - 1):
                            pe.wait_ge(s_qk_raw, g)
                        src = xt if phase == A else ct
                        for i, t in enumerate((xt, src)):
                            w = wpad[:, phase, i, jl % NG, :, :].rearrange("c h d -> c (h d)")
                            last = nc.tensor.matmul(heads_ps[:, i * P:(i + 1) * P], w, t[jl // NG % 2][:, :], start=True, stop=True)
                    last.then_inc(s_heads, 1)

            def split_product(dst, slot, which, cols):
                parts = ((xt_high, wqkv_high), (xt_high, wqkv_low), (xt_low, wqkv_high))
                for n, (a, w) in enumerate(parts):
                    last = nc.tensor.matmul(dst, a[slot][:, :], w[:, which, cols], start=(n == 0), stop=(n == 2))
                return last

            def project(phase, layer, it, j):
                base = start_of(phase, layer)
                now = base + it * STEPS + j
                nseq = (phase + layer) * NB
                if phase == C and here(it, j, 0):
                    g = now - 2 * GROUPS
                    if j % NG == 0:
                        pe.wait_ge(s_xt_split, layer * NB + it * 2 + j // NG + 1)
                    if isinstance(it, int) and it == 0 and j == 0:
                        pe.wait_ge(s_w_split, layer + 1)
                    gc = (j % NG) * HG * DH
                    dst = proj_ps[j % 2][:, :].rearrange("t (a n) -> t a n", a=2)
                    last = split_product(dst, j // NG % 2, slice(0, 2), slice(gc, gc + HG * DH))
                    last.then_inc(s_proj, 1)

            def project_out(phase, layer, it, j):
                base = start_of(phase, layer)
                now = base + it * STEPS + j
                if phase != A and here(it, j, LAG.out):
                    g = now - LAG.out
                    jl = (j - LAG.out) % STEPS
                    if phase == C:
                        pe.wait_ge(s_ot_ready, g - GROUPS + 1)
                        pe.wait_ge(s_pt_ready, base + issued(it, j, LAG.turn, 0))
                    else:
                        pe.wait_ge(s_ot_ready, g - GROUPS + 1)
                    if not here(it, j, LAG.turn):
                        pe.wait_ge(s_added, g)
                    if phase == C:
                        if isinstance(it, int) and it == 0 and j == LAG.out:
                            pe.wait_ge(s_wo_in, 16 * (layer + 1))
                        for k in range(2):
                            c = ((jl % NG) * 2 + k) * P
                            last = nc.tensor.matmul(turn_ps[:, 0:P], head_t[jl % 2][:, k * P:(k + 1) * P], wo_sb[:, c:c + P],
                                                    start=(k == 0), stop=(k == 1))
                    else:
                        last = nc.tensor.matmul(small_out_ps[:, 0:P], head_t[jl % 2][0:PAD, 0:P], bwo[:, jl % NG, :], start=True, stop=True)
                    last.then_inc(s_wo_done, 1)

            def sum_values(phase, layer, it, j):
                base = start_of(phase, layer)
                now = base + it * STEPS + j
                if here(it, j, LAG.value):
                    g = now - LAG.value
                    jl = (j - LAG.value) % STEPS
                    pe.wait_ge(s_pt_ready, g + 1)
                    if phase == A and has(it * STEPS + j - LAG.value - 2):
                        pe.wait_ge(s_out_ready, g - 1)
                    if phase == C:
                        for k in range(2):
                            last = nc.tensor.matmul(value_ps[:, k * 2 * P:(k + 1) * 2 * P],
                                                    val[jl][:, :, :].rearrange("t h d -> t (h d)")[:, k * P:(k + 1) * P],
                                                    prob_t[jl % 2][:, 2 * k:2 * k + 2, :].rearrange("k h q -> k (h q)"), start=True, stop=True)
                    else:
                        for h in range(HG):
                            last = nc.tensor.matmul(small_value_ps[jl % 2][:, h * (DH + 1):h * (DH + 1) + DS + 1], prob_t[jl % 2][:, h, :],
                                                    val[jl][:, h, 0:DS + 1], start=True, stop=True)
                    last.then_inc(s_pv, 1)

            def project_values(phase, layer, it, j):
                base = start_of(phase, layer)
                nseq = (phase + layer) * NB
                if here(it, j, 0):
                    pe.wait_ge(s_v_ready, base + issued(it, j, 0, 0))
                    first = isinstance(it, int) and it == 0 and j == 0
                    if j % NG == 3 or first:
                        pe.wait_ge(s_xt_ready, nseq + turned(it, j, 0))
                        if phase == B:
                            pe.wait_ge(s_ct_ready, turned(it, j, 0))
                    if phase != C and first:
                        pe.wait_ge(s_small_in, 16 * 11)
                    slot = j // NG % 2
                    if phase == C:
                        gc = (j % NG) * HG * DH
                        split_product(misc_ps[:, 0:HG * DH], slot, 2, slice(gc, gc + HG * DH)).then_inc(s_v_proj, 1)
                    else:
                        w = (aw if phase == A else bw)[:, 2 * P + (j % NG) * PAD:2 * P + (j % NG + 1) * PAD]
                        nc.tensor.matmul(misc_ps[:, 0:PAD], (ct if phase == B else xt)[slot][:, :], w, start=True, stop=True).then_inc(s_v_proj, 1)

            def turn_probs(phase, layer, it, j):
                base = start_of(phase, layer)
                now = base + it * STEPS + j
                if here(it, j, LAG.turn):
                    g = now - LAG.turn
                    jl = (j - LAG.turn) % STEPS
                    if phase == C:
                        pe.wait_ge(s_scaled, g - 2 * GROUPS + 1)
                    else:
                        pe.wait_ge(s_exp_done, g + 1)
                    if phase == C and here(it, j, LAG.out):
                        pe.wait_ge(s_added, base + issued(it, j, LAG.out, 1))
                    for h in range(HG):
                        last = nc.tensor.transpose(turn_ps[:, h * P:(h + 1) * P], prob[jl % 2][:, h, :], ident)
                    last.then_inc(s_pturn, 1)

            def scores(phase, layer, it, j):
                base = start_of(phase, layer)
                now = base + it * STEPS + j
                if here(it, j, LAG.scores):
                    g = now - LAG.scores
                    jl = (j - LAG.scores) % STEPS
                    if phase != C:
                        pe.wait_ge(s_kz_ready, g + 1)
                    elif not here(it, j, LAG.heads):
                        pe.wait_ge(s_k_ready, g + 1)
                    if phase != B:
                        nc.tensor.matmul(score_ps[jl % 2][:, :].rearrange("q (h k) -> q h k", h=HG), ident_b[:, :],
                                         masks_b[:, phase // 2, :].unsqueeze(1).to_broadcast([P, HG, P]), start=True, stop=False,
                                         skip_group_check=True)
                    if phase == C:
                        keys = kz[jl % 2][:, :, :].rearrange("d h k -> d (h k)")
                        for k in range(2):
                            last = nc.tensor.matmul(score_ps[jl % 2][:, k * 2 * P:(k + 1) * 2 * P], qt[jl % 2][:, k * P:(k + 1) * P],
                                                    keys[:, k * 2 * P:(k + 1) * 2 * P], start=False, stop=False,
                                                    skip_group_check=True)
                    else:
                        last = nc.tensor.matmul(score_ps[jl % 2][:, :], qk_parts[jl % 2][:, 0, :],
                                                kz_parts[jl % 2][:, :, :].rearrange("d h k -> d (h k)"),
                                                start=(phase == B), stop=False, skip_group_check=True)
                    last.then_inc(s_scores, 1)

            def turn_out(phase, layer, it, j):
                base = start_of(phase, layer)
                now = base + it * STEPS + j
                if phase == B and here(it, j, LAG.out):
                    g = now - LAG.out
                    jl = (j - LAG.out) % STEPS
                    pe.wait_ge(s_out_ready, g + 1)
                    pe.wait_ge(s_added, g)
                    last = nc.tensor.transpose(small_out_ps[0:PAD, 0:P], head_out[jl % 2][:, 0, 0:PAD], ident)
                    last.then_inc(s_oturn, 1)

            def turn_next(phase, layer, it, j):
                base = start_of(phase, layer)
                at = next_turn(phase)
                if j % NG == at and here(it, j, -NG + at):
                    pe.wait_ge(s_v_ready, base + issued(it, j, 0, phase != C))
                    turn_input(phase, layer, it * 2 + j // NG + 1, (j // NG + 1) % 2)

            def step(phase, layer, it, j):
                if phase == C:
                    turn_heads(phase, layer, it, j)
                    project(phase, layer, it, j)
                    turn_next(phase, layer, it, j)
                    project_out(phase, layer, it, j)
                    sum_values(phase, layer, it, j)
                    project_values(phase, layer, it, j)
                    turn_probs(phase, layer, it, j)
                    scores(phase, layer, it, j)
                else:
                    turn_heads(phase, layer, it, j)
                    project_values(phase, layer, it, j)
                    turn_out(phase, layer, it, j)
                    sum_values(phase, layer, it, j)
                    project_out(phase, layer, it, j)
                    turn_probs(phase, layer, it, j)
                    scores(phase, layer, it, j)
                    turn_next(phase, layer, it, j)

            def mlp_step(layer, it, j):
                q = layer * NQ + it * 2 + j
                if here_q(it, j, 0):
                    if isinstance(it, int) and it == 0:
                        pe.wait_ge(s_added, start_of(C, layer) + (j + 1) * QUAD * NG)
                        pe.wait_ge(s_v_ready, start_of(C, layer + 1))
                    else:
                        pe.wait_ge(s_added, start_of(C, layer + 1))
                    if has(it * 2 + j - 1):
                        pe.wait_ge(s_f_right, q)
                    nc.tensor.matmul(misc_ps[:, 0:QUAD * DH].rearrange("t (b c) -> t b c", b=QUAD), const("shift"),
                                     seq(y, (it * 2 + j) * QUAD, QUAD).rearrange("t (b c) -> t b c", b=QUAD)[:, :, DH:P],
                                     start=True, stop=True).then_inc(s_f_shift, 1)
                if here_q(it, j, 1):
                    m = q - 1
                    pe.wait_ge(s_f_norm, 4 * m + 4)
                    if has(it * 2 + j - 2):
                        pe.wait_ge(s_f_xt, m)
                    for b in range(QUAD):
                        last = nc.tensor.transpose(heads_ps[:, b * P:(b + 1) * P], normed[(j + 1) % 2][:, b, :], ident)
                    last.then_inc(s_f_turn, 1)
                if here_q(it, j, 2):
                    k0 = (j % 2) * 6
                    m = q - 2
                    pe.wait_ge(s_f_low, m + 1)
                    if isinstance(it, int) and it == 1 and j == 0:
                        pe.wait_ge(s_w1_split, layer + 1)
                        pe.wait_ge(s_exp_done, start_of(C, layer + 1))
                    for k in range(3):
                        a, n = HB[k]
                        for i, ready in ((1, s_f_gate_ps), (0, s_f_a_ps)):
                            use = 2 * k + 1 - i
                            free = s_f_gate if i else s_f_hid
                            if has(3 * (it * 2 + j - 2) + k - 2):
                                pe.wait_ge(free, 3 * m + k - 1)
                            parts = ((w1_high, normed_high), (w1_high, normed_low), (w1_low, normed_high))
                            for p, (w, v) in enumerate(parts):
                                last = nc.tensor.matmul(hid_ps[(k0 + use) % 4][0:n, :], w[:, i * HID + a:i * HID + a + n],
                                                        v[j % 2][:, :], start=(p == 0), stop=(p == 2))
                            last.then_inc(ready, 1)
                if here_q(it, j, 3):
                    m = q - 3
                    pe.wait_ge(s_f_hid, 3 * m + 3)
                    if isinstance(it, int) and it == 1 and j == 1:
                        pe.wait_ge(s_w2_in, 48 * (layer + 1))
                        pe.wait_ge(s_ot_ready, start_of(C, layer + 1) - GROUPS)
                    if has(it * 2 + j - 5):
                        pe.wait_ge(s_y_done, m - 1 + NQ)
                    for b in range(QUAD):
                        for k, (a, n) in enumerate(HB):
                            last = nc.tensor.matmul(out_ps[(j + 1) % 2][:, b * P:(b + 1) * P], hidden[3 * ((j + 1) % 2) + k][0:n, b * P:(b + 1) * P],
                                                    w2_sb[0:n, k * P:(k + 1) * P], start=(k == 0), stop=(k == 2))
                    last.then_inc(s_f_w2, 1)

            for phase in (A, B):
                pe.wait_ge(s_added, start_of(phase, 0))
                turn_input(phase, 0, 0, 0)
                attention(pe, step, phase)
            with pe.Fori(0, DEPTH) as layer:
                pe.wait_ge(s_added, start_of(C, layer))
                pe.wait_ge(s_y_done, (layer + 1) * NQ)
                turn_input(C, layer, 0, 0)
                attention(pe, step, C, layer, mlp_step)
                mlp(pe, mlp_step, layer)

        @block.scalar
        def _(act):
            def copy_input(phase, layer, b, slot):
                nb = (phase + layer) * NB + b
                act.wait_ge(s_xturn, nb + 1)
                if phase == B:
                    act.wait_ge(s_cturn, b + 1)
                if phase == C:
                    if isinstance(b, int) and b < 2:
                        act.wait_ge(s_xt_zero, 2)
                    nc.scalar.activation(xt[slot][0:DH, :], misc_ps[0:DH, 0:P], ACT.Copy)
                    nc.scalar.activation(xt[slot][DH:P, 1:P], misc_ps[DH:P, 0:P - 1], ACT.Copy).then_inc(s_xt_ready, 1)
                else:
                    nc.scalar.activation(xt[slot][:, :], misc_ps[:, 0:P], ACT.Copy).then_inc(s_xt_ready, 1)
                    if phase == B:
                        nc.scalar.activation(ct[slot][:, :], misc_ps[:, P:2 * P], ACT.Copy).then_inc(s_ct_ready, 1)

            def copy_heads(phase, layer, it, j):
                base = start_of(phase, layer)
                now = base + it * STEPS + j
                if phase == C and here(it, j, LAG.heads):
                    g = now - LAG.heads
                    jl = (j - LAG.heads) % STEPS
                    act.wait_ge(s_heads, g + 1)
                    if isinstance(it, int) and it == 0 and j == LAG.heads:
                        act.wait_ge(s_kz_zero, 2)
                    nc.scalar.activation(qt[jl % 2][:, :], heads_ps[:, 0:2 * P], ACT.Copy).then_inc(s_q_ready, 1)
                    pairs = kz[jl % 2][:, :, :].rearrange("d (a b) k -> d b a k", b=2)
                    turned_k = heads_ps[:, 2 * P:4 * P].rearrange("d (a k) -> d a k", a=2)
                    nc.scalar.activation(pairs[0:DH, 0], turned_k[0:DH], ACT.Copy).then_inc(s_k_half, 1)
                    nc.scalar.activation(pairs[DH:P, 1], turned_k[DH:P], ACT.Copy).then_inc(s_k_ready, 1)

                if phase != C and here(it, j, LAG.heads):
                    g = now - LAG.heads
                    jl = (j - LAG.heads) % STEPS
                    act.wait_ge(s_heads, g + 1)
                    dst = qk_raw[jl % 2]
                    if phase == A:
                        nc.scalar.activation(dst, heads_ps[:, 0:2 * P].rearrange("d (a t) -> d a t", a=2), ACT.Copy).then_inc(s_qk_raw, 1)
                    else:
                        if isinstance(it, int) and it == 0 and j == LAG.heads:
                            act.wait_ge(s_bias_in, 16 * 2 * HG * PARTS)
                        for i in range(2):
                            last = nc.scalar.activation(dst[:, i, :], heads_ps[:, i * P:(i + 1) * P], ACT.Identity,
                                                        bias=b_qk[:, i, jl % NG:jl % NG + 1])
                        last.then_inc(s_qk_raw, 1)

            def square(phase, layer, it, j):
                base = start_of(phase, layer)
                now = base + it * STEPS + j
                if phase == C and here(it, j, 0):
                    g = now - 2 * GROUPS
                    act.wait_ge(s_sin_done, g + 1)
                    if has(it * STEPS + j - 1):
                        act.wait_ge(s_nrm2, g)
                    nc.scalar.activation(squares[:, :, :].rearrange("t h d -> t (h d)"), proj_ps[j % 2][:, :], ACT.Square).then_inc(s_sq_done, 1)

            def exponentials(phase, layer, it, j):
                base = start_of(phase, layer)
                now = base + it * STEPS + j
                if here(it, j, LAG.exp):
                    g = now - LAG.exp
                    jl = (j - LAG.exp) % STEPS
                    act.wait_ge(s_top_done, g + 1)
                    for h in range(HG):
                        sums = psum_raw[jl % 2][:, h:h + 1] if phase == C else None
                        last = nc.scalar.activation(prob[jl % 2][:, h, :], score_ps[jl % 2][:, h * P:(h + 1) * P], ACT.Exp,
                                                    bias=top[jl % 2][:, h:h + 1], accum_out=sums)
                    last.then_inc(s_exp_done, 1)

            def copy_values(phase, layer, it, j):
                base = start_of(phase, layer)
                now = base + it * STEPS + j
                if phase != B and here(it, j, 0):
                    g = now
                    act.wait_ge(s_v_proj, g + 1)
                    width = DH if phase == C else DS
                    if phase == A and isinstance(it, int) and it == 0 and j == 0:
                        act.wait_ge(s_vone_set, 2 * NG)
                    nc.scalar.activation(val[j][:, :, 0:width], misc_ps[:, 0:HG * width].rearrange("t (h d) -> t h d", h=HG), ACT.Copy).then_inc(s_v_ready, 1)

            def copy_probs(phase, layer, it, j):
                base = start_of(phase, layer)
                now = base + it * STEPS + j
                if here(it, j, LAG.turn):
                    g = now - LAG.turn
                    act.wait_ge(s_pturn, g + 1)
                    nc.scalar.activation(prob_t[(j - LAG.turn) % 2][:, :, :].rearrange("k h q -> k (h q)"), turn_ps[:, :], ACT.Copy).then_inc(s_pt_ready, 1)

            def copy_out(phase, layer, it, j):
                base = start_of(phase, layer)
                now = base + it * STEPS + j
                lag = LAG.value if phase == C else LAG.out
                if phase != A and here(it, j, lag):
                    g = now - lag
                    jl = (j - lag) % STEPS
                    if phase == C:
                        act.wait_ge(s_pv, g + 1)
                        got = value_ps[:, :].rearrange("d (k h q) -> d h k q", k=2, h=2)
                        dst = head_t[jl % 2][:, :].rearrange("d (k q) -> d k q", k=2)
                        nc.scalar.activation(dst[0:DH], got[0:DH, 0], ACT.Copy)
                        nc.scalar.activation(dst[DH:P], got[DH:P, 1], ACT.Copy).then_inc(s_ot_ready, 1)
                    else:
                        act.wait_ge(s_oturn, g - GROUPS + 1)
                        nc.scalar.activation(head_t[jl % 2][0:PAD, 0:P], small_out_ps[0:PAD, 0:P], ACT.Copy).then_inc(s_ot_ready, 1)

            def copy_next(phase, layer, it, j):
                at = next_turn(phase)
                if j % NG == at and here(it, j, -NG + at):
                    copy_input(phase, layer, it * 2 + j // NG + 1, (j // NG + 1) % 2)

            def step(phase, layer, it, j):
                if phase == C:
                    copy_heads(phase, layer, it, j)
                    copy_next(phase, layer, it, j)
                    exponentials(phase, layer, it, j)
                    square(phase, layer, it, j)
                    copy_out(phase, layer, it, j)
                    copy_values(phase, layer, it, j)
                    copy_probs(phase, layer, it, j)
                else:
                    copy_heads(phase, layer, it, j)
                    copy_values(phase, layer, it, j)
                    copy_out(phase, layer, it, j)
                    exponentials(phase, layer, it, j)
                    copy_probs(phase, layer, it, j)
                    copy_next(phase, layer, it, j)

            def mlp_step(layer, it, j):
                q = layer * NQ + it * 2 + j
                if here_q(it, j, 1):
                    m = q - 1
                    act.wait_ge(s_f_turn, m + 1)
                    if has(it * 2 + j - 3):
                        act.wait_ge(s_f_a_ps, 3 * m - 3)
                    for dst in (normed_t[(j + 1) % 2], normed_high[(j + 1) % 2]):
                        last = nc.scalar.activation(dst[:, :], heads_ps[:, :], ACT.Identity, bias=mlp_now[:, 1:2],
                                                    scale=mlp_now[:, 0:1])
                    last.then_inc(s_f_xt, 1)
                if here_q(it, j, 2):
                    m = q - 2
                    for k in range(3):
                        n = HB[k][1]
                        act.wait_ge(s_f_gate_ps, 3 * m + k + 1)
                        if has(it * 2 + j - 4):
                            act.wait_ge(s_f_hid, 3 * m + k - 5)
                        nc.scalar.activation(gate[3 * (j % 2) + k][0:n, :], hid_ps[((j % 2) * 6 + 2 * k) % 4][0:n, :], ACT.Gelu,
                                             bias=mlp_now[0:n, 5 + k:6 + k]).then_inc(s_f_gate, 1)

            for phase in (A, B):
                act.wait_ge(s_added, start_of(phase, 0))
                copy_input(phase, 0, 0, 0)
                attention(act, step, phase)
            act.wait_ge(s_table_in, 16 * 11)
            with act.Fori(0, DEPTH) as layer:
                act.wait_ge(s_layer_set, layer + 1)
                act.wait_ge(s_added, start_of(C, layer))
                act.wait_ge(s_y_done, (layer + 1) * NQ)
                copy_input(C, layer, 0, 0)
                attention(act, step, C, layer, mlp_step)
                mlp(act, mlp_step, layer)

        @block.gpsimd
        def _(pool):
            pool.memset(m_at[:, :], 0.0).then_inc(s_zeros_set, 1)
            pool.memset(per_layer[:, :, :], 0.0).then_inc(s_zeros_set, 1)
            pool.memset(b_qk[:, :, :], 0.0).then_inc(s_zeros_set, 1)
            pool.memset(wpad[:, :, :, :, :, :], 0.0).then_inc(s_wpad_set, 1)
            pool.memset(neg_half[:, :], -0.5).then_inc(s_half_set, 1)
            pool.memset(one[:, :], 1.0).then_inc(s_half_set, 1)
            for v in val:
                pool.memset(v[:, :, DS:DS + 1], 1.0).then_inc(s_vone_set, 1)
            pool.wait_ge(s_small_in, 16 * 11)
            pool.wait_ge(s_wpad_set, 1)
            for ph, w, cols in ((A, aw, (P, 0)), (B, bw, (0, P))):
                for i, c in enumerate(cols):
                    nc.gpsimd.tensor_copy(wpad[:, ph, i, :, :, 0:POS].rearrange("c g h (r d) -> c (g h) r d", r=PARTS),
                                          w[:, c:c + P].rearrange("c (n d) -> c n d", d=DS).unsqueeze(2).to_broadcast([P, NH, PARTS, DS])).then_inc(s_wpad_set, 1)
            pool.wait_ge(s_half_set, 2)

            def rstd_of(phase, b, slot):
                pool.wait_ge(s_ln_var, phase * NB + b + 1)
                nc.gpsimd.tensor_tensor(rstd[slot][:, 0:1], var[slot][:, 0:1], neg_half[:, 0:1], ALU.pow).then_inc(s_ln_rstd, 1)

            def prepare(phase, layer, b, slot):
                if phase != C:
                    rstd_of(phase, b, slot)

            def step(phase, layer, it, j):
                if j % NG == 1 and here(it, j, -NG + 1):
                    prepare(phase, layer, it * 2 + j // NG + 1, (j // NG + 1) % 2)
                if phase != C and here(it, j, LAG.heads):
                    g = start_of(phase, 0) + it * STEPS + j - LAG.heads
                    pool.wait_ge(s_k_ready, g + 1)
                    keys = qk_parts[j % 2][:, 1, :].bitcast(F32)
                    nc.gpsimd.tensor_tensor(kz_parts[j % 2][:, :, :], keys.unsqueeze(1).to_broadcast([P, HG, P]),
                                            const("block").unsqueeze(2).to_broadcast([P, HG, P]), ALU.mult).then_inc(s_kz_ready, 1)
                if phase == C and here(it, j, 0):
                    g = layer * GROUPS + it * STEPS + j
                    pool.wait_ge(s_sin_done, g + 1)
                    nc.gpsimd.tensor_tensor(rotated[j % 2][:, :, :, :], by_cos[j % 2][:, :, :, :], by_sin[j % 2][:, :, :, :], ALU.add).then_inc(s_rot_done, 1)
                    pool.wait_ge(s_nrm2g, g + 1)
                    nc.gpsimd.tensor_tensor(rnorm[j % 2][:, :], norm2g[j % 2][:, :], neg_half[:, :], ALU.pow).then_inc(s_rn_done, 1)
                    pool.wait_ge(s_rot_done, g + 1)
                    pool.wait_ge(s_rn_done, g + 1)
                    if has(it * STEPS + j - 2):
                        pool.wait_ge(s_heads, 2 * GROUPS + g - 1)
                    nc.gpsimd.tensor_tensor(unit[j % 2][:, :, :, :].rearrange("t a h d -> t (a h) d"),
                                            rotated[j % 2][:, :, :, :].rearrange("t a h d -> t (a h) d"),
                                            rnorm[j % 2][:, :].unsqueeze(2).to_broadcast([P, 2 * HG, DH]), ALU.mult).then_inc(s_unit_done, 1)

            def mlp_step(layer, it, j):
                q = layer * NQ + it * 2 + j
                if here_q(it, j, 0):
                    pool.wait_ge(s_f_var, q + 1)
                    nc.gpsimd.tensor_tensor(rstd[j % 2][:, :], var[j % 2][:, :], neg_half[:, 0:QUAD], ALU.pow).then_inc(s_f_rstd, 1)
                if isinstance(it, int) and it == 0 and j == 0:
                    pool.wait_ge(s_w1_in, 16 * (layer + 1))
                    nc.gpsimd.tensor_tensor(w1_high[:, :], w1_sb[:, :], one[:, :].to_broadcast([P, 2 * HID]), ALU.mult).then_inc(s_w1_high, 1)
                    pool.wait_ge(s_w1_high, layer + 1)
                    nc.gpsimd.tensor_tensor(w1_low[:, :], w1_sb[:, :], w1_high[:, :].bitcast(F32), ALU.subtract).then_inc(s_w1_split, 1)
                if here_q(it, j, 1):
                    m = q - 1
                    slot = (j + 1) % 2
                    pool.wait_ge(s_f_xt, m + 1)
                    nc.gpsimd.tensor_tensor(normed_low[slot][:, :], normed_t[slot][:, :], normed_high[slot][:, :].bitcast(F32),
                                            ALU.subtract).then_inc(s_f_low, 1)

            def split_weights(layer):
                pool.wait_ge(s_wqkv_in, 16 * (layer + 1))
                loaded = wqkv_sb[:, :].rearrange("c (a n) -> c a n", a=3)
                nc.gpsimd.tensor_tensor(wqkv_high[:, :, :], loaded, one[:, :].unsqueeze(2).to_broadcast([P, 3, INNER]), ALU.mult).then_inc(s_w_high, 1)
                pool.wait_ge(s_w_high, layer + 1)
                nc.gpsimd.tensor_tensor(wqkv_low[:, :, :], loaded, wqkv_high[:, :, :].bitcast(F32), ALU.subtract).then_inc(s_w_split, 1)

            def windowed_layer(layer):
                pool.wait_ge(s_added, start_of(C, layer))
                pool.wait_ge(s_y_done, (layer + 1) * NQ)
                attention(pool, step, C, layer, mlp_step)
                mlp(pool, mlp_step, layer)

            for phase in (A, B):
                prepare(phase, 0, 0, 0)
                attention(pool, step, phase)
            split_weights(0)
            with pool.Fori(0, NQ // 2) as q2:
                for j in range(2):
                    pool.wait_ge(s_y_var, q2 * 2 + j + 1)
                    nc.gpsimd.tensor_tensor(rstd[j][:, :], var[j][:, :], neg_half[:, 0:QUAD], ALU.pow).then_inc(s_y_rstd, 1)
            pool.wait_ge(s_scores, 2 * GROUPS)
            for k in kz:
                pool.memset(k[:, :, :], 0.0).then_inc(s_kz_zero, 1)
            pool.wait_ge(s_kz_zero, 2)
            for t in xt:
                pool.memset(t[DH:P, 0:1], 0.0).then_inc(s_xt_zero, 1)
            pool.wait_ge(s_xt_zero, 2)
            pool.wait_ge(s_table_in, 16 * 11)
            windowed_layer(0)
            with pool.Fori(1, DEPTH) as layer:
                split_weights(layer)
                windowed_layer(layer)

        @block.vector
        def _(dve):
            dve.wait_ge(s_const_in, 16)
            nc.vector.tensor_copy(ident_b[:, :], ident)
            nc.vector.tensor_copy(masks_b[:, 0, :], const("causal"))
            nc.vector.tensor_copy(masks_b[:, 1, :], const("band")).then_inc(s_cast_done, 1)
            dve.wait_ge(s_small_in, 16 * 11)
            nc.vector.tensor_scalar(m_at[:, NG:2 * NG], m_at[:, NG:2 * NG], -1.0, None, ALU.mult).then_inc(s_krow_neg, 1)
            dve.wait_ge(s_krow_neg, 1)
            for g in range(NG):
                nc.vector.tensor_scalar(krow_raw[:, g, :], const("iota"), m_at[:, g:g + 1], m_at[:, NG + g:NG + g + 1], ALU.mult, ALU.add).then_inc(s_krow_set, 1)
            dve.wait_ge(s_krow_set, NG)
            split = lambda phase, n: const("split")[:, 4 * phase + n:4 * phase + n + 1]
            nc.vector.tensor_scalar(krow_upper[:, :, :], krow_raw[:, :, :], split(A, 2), None, ALU.mult).then_inc(s_krow_upper, 1)
            dve.wait_ge(s_krow_upper, 1)
            nc.vector.scalar_tensor_tensor(out=krow[:, :, :], in0=krow_raw[:, :, :], scalar=split(A, 3), in1=krow_upper[:, :, :].bitcast(F32),
                                           op0=ALU.mult, op1=ALU.add).then_inc(s_krow_split, 1)
            dve.wait_ge(s_krow_split, 1)
            dve.wait_ge(s_x_in, 16)

            def ln_stats(phase, b, slot):
                nb = phase * NB + b
                nc.vector.bn_stats(stats[slot][:, 0, :], seq(x, b)).then_inc(s_ln_stat, 1)
                dve.wait_ge(s_ln_stat, nb + 1)
                nc.vector.memset(scratch[:, :], 0.0)
                nc.vector.bn_aggr(mv[slot][:, 0, :], stats[slot][:, 0, :]).then_inc(s_ln_mv, 1)
                dve.wait_ge(s_ln_mv, nb + 1)
                if has(nb - 2):
                    dve.wait_ge(s_ln_rstd, nb - 1)
                nc.vector.tensor_scalar(var[slot][:, 0:1], mv[slot][:, 0, 1:2], EPS, None, ALU.add).then_inc(s_ln_var, 1)

            def prepare(layer, b, slot):
                nb = (C + layer) * NB + b
                dve.wait_ge(s_xturn, nb - 1)
                nc.vector.tensor_scalar(tok[slot][:, :], seq(y, b), 1.0, None, ALU.mult).then_inc(s_tok_ready, 1)

            def ln_apply(phase, b, slot):
                nb = phase * NB + b
                dve.wait_ge(s_ln_rstd, nb + 1)
                if has(nb - 2):
                    dve.wait_ge(s_xturn, nb - 1)
                nc.vector.tensor_scalar(tok[slot][:, :], seq(x, b), mv[slot][:, 0, 0:1], rstd[slot][:, 0:1], ALU.subtract, ALU.mult).then_inc(s_tok_ready, 1)
                if phase == B:
                    if has(b - 2):
                        dve.wait_ge(s_cturn, b - 1)
                    nc.vector.tensor_scalar(ctok[slot][:, :], seq(ctx_all, b), 1.0, None, ALU.mult).then_inc(s_ctok_ready, 1)
                    dve.wait_ge(s_tok_ready, nb + 1)
                    nc.vector.tensor_tensor(seq(x, b), seq(x, b), b_o[:, :], ALU.add).then_inc(s_bias_added, 1)

            def norms(phase, layer, it, j):
                base = start_of(phase, layer)
                now = base + it * STEPS + j
                if phase == C and here(it, j, 0):
                    g = now - 2 * GROUPS
                    dve.wait_ge(s_sq_done, g + 1)
                    nc.vector.tensor_reduce(norm2[j % 2][:, :], squares[:, :, :], AX_X, ALU.add).then_inc(s_nrm2, 1)
                    dve.wait_ge(s_nrm2, g + 1)
                    if has(it * STEPS + j - 2):
                        dve.wait_ge(s_rn_done, g - 1)
                    nc.vector.tensor_scalar(norm2g[j % 2][:, :], norm2[j % 2][:, :], 1e-24, None, ALU.max).then_inc(s_nrm2g, 1)

            def add_projected(phase, layer, it, j):
                base = start_of(phase, layer)
                now = base + it * STEPS + j
                if phase != A and here(it, j, LAG.out):
                    g = now - LAG.out
                    jl = (j - LAG.out) % STEPS
                    b = it * 2 + (j - LAG.out) // NG
                    dve.wait_ge(s_wo_done, g - GROUPS + 1)
                    dst = seq(x if phase == B else y, b)
                    if phase == B:
                        dve.wait_ge(s_bias_added, b + 1)
                    dve.wait_ge(s_added, g)
                    nc.vector.tensor_tensor(dst, dst, (small_out_ps if phase == B else turn_ps)[:, 0:P], ALU.add).then_inc(s_added, 1)

            def table(t, layer):
                return t[:, bass.ds(layer * 2 * DH, 2 * DH)].rearrange("t (a d) -> t a d", a=2)

            def split_input(layer, b, slot):
                nb = layer * NB + b
                dve.wait_ge(s_xt_ready, 2 * NB + nb + 1)
                nc.vector.tensor_scalar(xt_high[slot][:, :], xt[slot][:, :], 1.0, None, ALU.mult).then_inc(s_xt_high, 1)
                dve.wait_ge(s_xt_high, nb + 1)
                nc.vector.tensor_tensor(xt_low[slot][:, :], xt[slot][:, :], xt_high[slot][:, :].bitcast(F32), ALU.subtract).then_inc(s_xt_split, 1)

            def split_next(phase, layer, it, j):
                if j % NG == 3 and here(it, j, -NG + 3):
                    split_input(layer, it * 2 + j // NG + 1, (j // NG + 1) % 2)

            def cos_products(phase, layer, it, j):
                if here(it, j, 0):
                    g = layer * GROUPS + it * STEPS + j
                    if has(it * STEPS + j - 2):
                        dve.wait_ge(s_rot_done, g - 1)
                    dve.wait_ge(s_proj, g + 1)
                    got = proj_ps[j % 2][:, :].rearrange("t (a h d) -> t a h d", a=2, h=HG)
                    nc.vector.tensor_tensor(by_cos[j % 2][:, :, :, :], got, table(rot_cos, layer).unsqueeze(2).to_broadcast([P, 2, HG, DH]), ALU.mult).then_inc(s_cos_done, 1)

            def sin_products(phase, layer, it, j):
                if here(it, j, 0):
                    got = proj_ps[j % 2][:, :].rearrange("t (a h d) -> t a h d", a=2, h=HG)
                    sines = table(rot_sin, layer)
                    nc.vector.tensor_tensor(by_sin[j % 2][:, :, :, 0:HALF], got[:, :, :, HALF:DH],
                                            sines[:, :, 0:HALF].unsqueeze(2).to_broadcast([P, 2, HG, HALF]), ALU.mult)
                    nc.vector.tensor_tensor(by_sin[j % 2][:, :, :, HALF:DH], got[:, :, :, 0:HALF],
                                            sines[:, :, HALF:DH].unsqueeze(2).to_broadcast([P, 2, HG, HALF]), ALU.mult).then_inc(s_sin_done, 1)

            def divide(phase, layer, it, j):
                base = start_of(phase, layer)
                now = base + it * STEPS + j
                if phase != C and here(it, j, LAG.value):
                    g = now - LAG.value
                    jl = (j - LAG.value) % STEPS
                    got = small_value_ps[jl % 2][:, 0:HG * (DH + 1)].rearrange("t (h d) -> t h d", h=HG)
                    dve.wait_ge(s_pv, g + 1)
                    nc.vector.reciprocal(rsum[jl % 2][:, :].unsqueeze(2), got[:, :, DS:DS + 1]).then_inc(s_rsum_done, 1)
                    dve.wait_ge(s_rsum_done, g + 1)
                    dst = head_out[jl % 2][:, 0, 0:PAD].rearrange("t (h d) -> t h d", h=HG)
                    if phase == A and has(it * STEPS + j - LAG.value - 2):
                        dve.wait_ge(s_added, g - 1)
                    nc.vector.tensor_tensor(dst, got[:, :, 0:DS], rsum[jl % 2][:, :].unsqueeze(2).to_broadcast([P, HG, DS]), ALU.mult).then_inc(s_out_ready, 1)

            def scale_probs(phase, layer, it, j):
                base = start_of(phase, layer)
                now = base + it * STEPS + j
                if phase == C and here(it, j, LAG.exp):
                    g = now - LAG.exp
                    jl = (j - LAG.exp) % STEPS
                    dve.wait_ge(s_exp_done, g + 1)
                    nc.vector.reciprocal(rsum[jl % 2][:, :], psum_raw[jl % 2][:, :]).then_inc(s_rsum_done, 1)
                    dve.wait_ge(s_rsum_done, g + 1)
                    nc.vector.tensor_tensor(prob[jl % 2][:, :, :], prob[jl % 2][:, :, :], rsum[jl % 2][:, :].unsqueeze(2).to_broadcast([P, HG, P]), ALU.mult).then_inc(s_scaled, 1)

            def copy_heads(phase, layer, it, j):
                base = start_of(phase, layer)
                now = base + it * STEPS + j
                if phase != C and here(it, j, LAG.heads):
                    g = now - LAG.heads
                    jl = (j - LAG.heads) % STEPS
                    dve.wait_ge(s_qk_raw, g + 1)
                    raw, upper, parts = qk_raw[jl % 2], qk_upper[jl % 2], qk_parts[jl % 2]
                    for i, rows in enumerate((const("qrow"), krow[:, jl % NG, :].bitcast(F32))):
                        if phase == A:
                            nc.vector.scalar_tensor_tensor(out=upper[:, i, :], in0=raw[:, i, :], scalar=split(phase, 2 * i), in1=rows,
                                                           op0=ALU.mult, op1=ALU.add).then_inc(s_qk_upper, 1)
                        else:
                            nc.vector.tensor_scalar(upper[:, i, :], raw[:, i, :], split(phase, 2 * i), None, ALU.mult).then_inc(s_qk_upper, 1)
                    dve.wait_ge(s_qk_upper, 2 * g + 2)
                    for i in range(2):
                        last = nc.vector.scalar_tensor_tensor(out=parts[:, i, :], in0=raw[:, i, :], scalar=split(phase, 2 * i + 1),
                                                              in1=upper[:, i, :].bitcast(F32), op0=ALU.mult, op1=ALU.add)
                    last.then_inc(s_k_ready, 1)


            def copy_values(phase, layer, it, j):
                base = start_of(phase, layer)
                now = base + it * STEPS + j
                if phase == B and here(it, j, 0):
                    g = now
                    dve.wait_ge(s_v_proj, g + 1)
                    dve.wait_ge(s_vone_set, 2 * NG)
                    if has(it * STEPS + j - 2 * NG):
                        dve.wait_ge(s_pv, g + 1 - 2 * NG)
                    at = slice((j % NG) * PAD, (j % NG + 1) * PAD)
                    nc.vector.tensor_tensor(val[j][:, :, 0:DS], misc_ps[:, 0:PAD].rearrange("t (h d) -> t h d", h=HG),
                                            b_v[:, at].rearrange("t (h d) -> t h d", h=HG), ALU.add).then_inc(s_v_ready, 1)

            def next_sequence(phase, layer, it, j):
                if phase != C and j % NG == 0 and here(it, j, -NG):
                    ln_stats(phase, it * 2 + j // NG + 1, (j // NG + 1) % 2)
                if phase != C and j % NG == 1 and here(it, j, -NG + 1):
                    ln_apply(phase, it * 2 + j // NG + 1, (j // NG + 1) % 2)
                if phase == C and j % NG == 1 and here(it, j, -NG + 1):
                    prepare(layer, it * 2 + j // NG + 1, (j // NG + 1) % 2)

            def maxima(phase, layer, it, j):
                base = start_of(phase, layer)
                now = base + it * STEPS + j
                if here(it, j, LAG.scores):
                    g = now - LAG.scores
                    jl = (j - LAG.scores) % STEPS
                    dve.wait_ge(s_scores, g + 1)
                    nc.vector.tensor_reduce(top[jl % 2][:, :], score_ps[jl % 2][:, :].rearrange("q (h k) -> q h k", h=HG), AX_X, ALU.max, negate=True).then_inc(s_top_done, 1)

            def add_direct(phase, layer, it, j):
                base = start_of(phase, layer)
                now = base + it * STEPS + j
                if phase == A and here(it, j, LAG.value):
                    g = now - LAG.value
                    jl = (j - LAG.value) % STEPS
                    b = it * 2 + (j - LAG.value) // NG
                    dve.wait_ge(s_out_ready, g + 1)
                    at = bass.ds(b * P + (jl % NG) * PAD, PAD)
                    nc.vector.tensor_tensor(x[:, at], x[:, at], head_out[jl % 2][:, 0, 0:PAD], ALU.add).then_inc(s_added, 1)

            def step(phase, layer, it, j):
                if phase == C:
                    cos_products(phase, layer, it, j)
                    add_projected(phase, layer, it, j)
                    sin_products(phase, layer, it, j)
                    split_next(phase, layer, it, j)
                    scale_probs(phase, layer, it, j)
                    norms(phase, layer, it, j)
                    next_sequence(phase, layer, it, j)
                    maxima(phase, layer, it, j)
                else:
                    copy_values(phase, layer, it, j)
                    copy_heads(phase, layer, it, j)
                    divide(phase, layer, it, j)
                    add_projected(phase, layer, it, j)
                    maxima(phase, layer, it, j)
                    add_direct(phase, layer, it, j)
                    next_sequence(phase, layer, it, j)

            def mlp_step(layer, it, j):
                q = layer * NQ + it * 2 + j
                if here_q(it, j, 0):
                    dve.wait_ge(s_f_shift, q + 1)
                    if has(it * 2 + j - 2):
                        dve.wait_ge(s_f_norm, 4 * q - 4)
                    ys = seq(y, (it * 2 + j) * QUAD, QUAD).rearrange("t (b c) -> t b c", b=QUAD)
                    nc.vector.tensor_scalar(shifted[j % 2][:, :, 0:DH], ys[:, :, 0:DH], 1.0, None, ALU.mult).then_inc(s_f_left, 1)
                    nc.vector.tensor_copy(shifted[j % 2][:, :, DH:P], misc_ps[:, 0:QUAD * DH].rearrange("t (b c) -> t b c", b=QUAD)).then_inc(s_f_right, 1)
                    dve.wait_ge(s_f_right, q + 1)
                    dve.wait_ge(s_f_left, q + 1)
                    for b in range(QUAD):
                        nc.vector.bn_stats(stats[j % 2][:, b, :], shifted[j % 2][:, b, :]).then_inc(s_f_stat, 1)
                    dve.wait_ge(s_f_stat, QUAD * (q + 1))
                    nc.vector.memset(scratch[:, :], 0.0)
                    for b in range(QUAD):
                        nc.vector.bn_aggr(mv[j % 2][:, b, :], stats[j % 2][:, b, :]).then_inc(s_f_mv, 1)
                    dve.wait_ge(s_f_mv, QUAD * (q + 1))
                    nc.vector.tensor_scalar(var[j % 2][:, :].unsqueeze(2), mv[j % 2][:, :, 1:2], EPS, None, ALU.add).then_inc(s_f_var, 1)
                if here_q(it, j, 2):
                    m = q - 2
                    for k in range(3):
                        n = HB[k][1]
                        dve.wait_ge(s_f_a_ps, 3 * m + k + 1)
                        dve.wait_ge(s_f_gate, 3 * m + k + 1)
                        if has(it * 2 + j - 4):
                            dve.wait_ge(s_f_w2, m - 1)
                        nc.vector.scalar_tensor_tensor(out=hidden[3 * (j % 2) + k][0:n, :], in0=hid_ps[((j % 2) * 6 + 2 * k + 1) % 4][0:n, :],
                                                       scalar=mlp_now[0:n, 2 + k:3 + k], in1=gate[3 * (j % 2) + k][0:n, :],
                                                       op0=ALU.add, op1=ALU.mult).then_inc(s_f_hid, 1)
                if here_q(it, j, 0):
                    dve.wait_ge(s_f_rstd, q + 1)
                    if has(it * 2 + j - 2):
                        dve.wait_ge(s_f_turn, q - 1)
                    for b in range(QUAD):
                        nc.vector.tensor_scalar(normed[j % 2][:, b, :], shifted[j % 2][:, b, :], mv[j % 2][:, b, 0:1], rstd[j % 2][:, b:b + 1], ALU.subtract, ALU.mult).then_inc(s_f_norm, 1)
                if here_q(it, j, 4):
                    m = q - 4
                    dve.wait_ge(s_f_w2, m + 1)
                    at = (it * 2 + j - 4) * QUAD
                    dst = seq(y, at, QUAD)
                    nc.vector.tensor_tensor(dst, dst, out_ps[j % 2][:, :], ALU.add).then_inc(s_f_b2, 1)
                    dve.wait_ge(s_f_b2, m + 1)
                    dst = dst.rearrange("t (b c) -> t b c", b=QUAD)
                    nc.vector.tensor_tensor(dst, dst, b2_sb[:, bass.ds(layer * P, P)].unsqueeze(1).to_broadcast([P, QUAD, P]), ALU.add).then_inc(s_y_done, 1)

            for phase in (A, B):
                if phase == B:
                    dve.wait_ge(s_ctx_in, 16)
                dve.wait_ge(s_added, start_of(phase, 0))
                ln_stats(phase, 0, 0)
                ln_apply(phase, 0, 0)
                attention(dve, step, phase)
            dve.wait_ge(s_added, 2 * GROUPS)
            with dve.Fori(0, NQ // 2) as q2:
                for j in range(2):
                    q = q2 * 2 + j
                    for b in range(QUAD):
                        nc.vector.bn_stats(stats[j][:, b, :], seq(x, q * QUAD + b)).then_inc(s_y_stat, 1)
                    dve.wait_ge(s_y_stat, QUAD * (q + 1))
                    nc.vector.memset(scratch[:, :], 0.0)
                    for b in range(QUAD):
                        nc.vector.bn_aggr(mv[j][:, b, :], stats[j][:, b, :]).then_inc(s_y_mv, 1)
                    dve.wait_ge(s_y_mv, QUAD * (q + 1))
                    nc.vector.tensor_scalar(var[j][:, :].unsqueeze(2), mv[j][:, :, 1:2], EPS, None, ALU.add).then_inc(s_y_var, 1)
                for j in range(2):
                    q = q2 * 2 + j
                    dve.wait_ge(s_y_rstd, q + 1)
                    for b in range(QUAD):
                        last = nc.vector.tensor_scalar(seq(y, q * QUAD + b), seq(x, q * QUAD + b), mv[j][:, b, 0:1], rstd[j][:, b:b + 1], ALU.subtract, ALU.mult)
                    last.then_inc(s_y_done, 1)
            dve.wait_ge(s_table_in, 16 * 11)
            scales = qk_scale[:, :, :, :]
            for dst, src, at, frm in ((rot_cos, "cos", slice(0, DH), slice(0, DH)), (rot_sin, "sin", slice(0, HALF), slice(HALF, DH)),
                                      (rot_sin, "sin", slice(HALF, DH), slice(0, HALF))):
                for l in range(DEPTH):
                    nc.vector.tensor_tensor(dst[:, l * 2 * DH:(l + 1) * 2 * DH].rearrange("t (a d) -> t a d", a=2)[:, :, at],
                                            const(src).rearrange("t (a d) -> t a d", a=2)[:, :, at],
                                            scales[:, l, :, frm], ALU.mult).then_inc(s_tables_set, 1)
            dve.wait_ge(s_tables_set, 3 * DEPTH)
            with dve.Fori(0, DEPTH) as layer:
                dve.wait_ge(s_added, start_of(C, layer))
                dve.wait_ge(s_y_done, (layer + 1) * NQ)
                nc.vector.tensor_scalar(mlp_now[:, :], per_layer[:, :, :].rearrange("p l n -> p (l n)")[:, bass.ds(layer * 8, 8)],
                                        1.0, None, ALU.mult).then_inc(s_layer_set, 1)
                prepare(layer, 0, 0)
                split_input(layer, 0, 0)
                attention(dve, step, C, layer, mlp_step)
                mlp(dve, mlp_step, layer)
            dve.wait_ge(s_y_done, (DEPTH + 1) * NQ)
            for q in range(NQ):
                dst = y[:, q * QUAD * P:(q + 1) * QUAD * P]
                nc.vector.tensor_tensor(dst, dst, x[:, q * QUAD * P:(q + 1) * QUAD * P], ALU.add).then_inc(s_sum_done, 1)


_INS = ["x", "ctx_1024", "L0_attn_W_kqv", "L0_attn_m", "L0_xattn_w_q", "L0_xattn_b_q", "L0_xattn_w_k", "L0_xattn_b_k",
        "L0_xattn_w_v", "L0_xattn_b_v", "L0_xattn_w_o", "L0_xattn_b_o", "L0_ffn_Wqkv", "L0_ffn_q_scale", "L0_ffn_k_scale",
        "L0_ffn_Wo", "L0_ffn_ln_g", "L0_ffn_ln_b", "L0_ffn_W1", "L0_ffn_b1", "L0_ffn_W2", "L0_ffn_b2"]


def kernel(**inputs):
    import numpy as _np
    import concourse.bacc as _bacc
    from concourse import mybir as _mybir
    from concourse.bass_utils import run_bass_kernel_spmd as _run

    nc = _bacc.Bacc("TRN2", target_bir_lowering=False, num_devices=1)
    arrays, args = {}, []
    for name in _INS + ["constants"]:
        a = constants() if name == "constants" else _np.asarray(inputs[name])
        if name.startswith("L0_xattn_w_"):
            a = a.T
        a = _np.ascontiguousarray(a)
        arrays[f"in_{name}_dram"] = a
        args.append(nc.dram_tensor(f"in_{name}_dram", a.shape, _mybir.dt.from_np(a.dtype), kind="ExternalInput").ap())
    args.append(nc.dram_tensor("out_0_dram", (NB, P, P), F32, kind="ExternalOutput").ap())
    build(nc, *args)
    r = _run(nc, [arrays], core_ids=[0])
    return r.results[0]["out_0_dram"]
```
